# Optimizing a Trainium2 kernel written in Bass

```python
import numpy as np
import jax
import jax.numpy as jnp

def _softmax(x, axis=-1):
    return jax.nn.softmax(x, axis=axis)

def _gelu(x):
    return jax.nn.gelu(x, approximate=True)

def _silu(x):
    return jax.nn.silu(x)

def _sigmoid(x):
    return jax.nn.sigmoid(x)

def _layernorm(x, axis=-1, eps=1e-05):
    m = jnp.mean(x, axis=axis, keepdims=True)
    v = jnp.var(x, axis=axis, keepdims=True)
    return (x - m) / jnp.sqrt(v + eps)

def _scatter_add(tgt, idx, src, axis=0):
    return tgt.at[idx].add(src)

def _segment_sum(src, seg, n):
    return jax.ops.segment_sum(src, seg, n)
kernel_name = 'mk_perceiver_d4_seqx_r8_550403'

def setup_inputs(seed: int=0):
    np.random.seed(seed)
    _w = jnp.asarray

    def _rec_inputs():
        import jax
        import jax.numpy as jnp
        _rk = jax.random.key(seed)
        x = -0.000125 + 0.9999 * jax.random.normal(jax.random.fold_in(_rk, 1), (128, 32, 128), jnp.float32)
        _lenS = 32 - jax.random.randint(jax.random.fold_in(_rk, 7), (128,), 0, max(1, 32 // 4) + 1, jnp.int32)
        _lenS2 = 257 - jax.random.randint(jax.random.fold_in(_rk, 8), (128,), 0, max(1, 257 // 4) + 1, jnp.int32)
        _ctx_2048P = jax.random.normal(jax.random.fold_in(_rk, 11), (128, 16, 256), jnp.float32)
        _ctx_2048c = jax.random.dirichlet(jax.random.fold_in(_rk, 511), 0.3 * jnp.ones((16,), jnp.float32), (128, 257))
        _ctx_2048t = jnp.einsum('bsk,bkd->bsd', _ctx_2048c, _ctx_2048P)
        _ctx_2048t = _ctx_2048t * jax.lax.rsqrt(jnp.mean(jnp.square(_ctx_2048t)) + 1e-12) * 0.953939
        ctx_2048 = -1.39393e-06 + 0.999914 * (_ctx_2048t + 0.3 * jax.random.normal(jax.random.fold_in(_rk, 611), (128, 257, 256), jnp.float32))
        _validS = jnp.arange(32)[None, :] < _lenS[:, None]
        _validS2 = jnp.arange(257)[None, :] < _lenS2[:, None]
        _causal = jnp.tril(jnp.ones((32, 32), dtype=bool))
        mask_BxS2_if0 = jnp.where(jnp.ones((128, 257), dtype=bool), 4, 0).astype(jnp.int32)
        return (x, ctx_2048, mask_BxS2_if0)
    x, ctx_2048, mask_BxS2_if0 = _rec_inputs()

    def _L0_xattn_setup():
        import jax, jax.numpy as jnp
        import numpy as np
        B, N, DIM = (8, 512, 128)
        M, CTX = (32, 256)
        HEADS, DH = (16, 64)
        INNER = HEADS * DH
        EPS = 1e-06

        def _split_heads(t):
            b, n, _ = t.shape
            return t.reshape(b, n, HEADS, DH).transpose(0, 2, 1, 3)
        key = jax.random.key(seed)
        ks = jax.random.split(key, 6)
        x = jax.random.normal(ks[0], (B, N, DIM), dtype=jnp.float32)
        context = jax.random.normal(ks[1], (B, M, CTX), dtype=jnp.float32)
        Wq = jax.random.normal(ks[2], (DIM, INNER), dtype=jnp.float32) / np.sqrt(DIM)
        Wkv = jax.random.normal(ks[3], (CTX, 2 * INNER), dtype=jnp.float32) / np.sqrt(CTX)
        null_kv = jax.random.normal(ks[4], (2, DH), dtype=jnp.float32) / np.sqrt(2.0)
        Wout = jax.random.normal(ks[5], (INNER, DIM), dtype=jnp.float32) / np.sqrt(INNER)
        ln_scale = jnp.ones((DIM,), dtype=jnp.float32)
        ln_bias = jnp.zeros((DIM,), dtype=jnp.float32)
        return {'x': x, 'context': context, 'Wq': Wq, 'Wkv': Wkv, 'null_kv': null_kv, 'Wout': Wout, 'ln_scale': ln_scale, 'ln_bias': ln_bias}
    _L0_xattn_all = _L0_xattn_setup()
    _L0_xattn_in = {k: v for k, v in _L0_xattn_all.items() if k in ('Wq', 'Wkv', 'null_kv', 'Wout', 'ln_scale', 'ln_bias')}
    del _L0_xattn_all

    def _L0_attn_setup():
        import jax, jax.numpy as jnp
        import numpy as np
        EMBED_DIM = 128
        NUM_HEADS = 16
        HEAD_DIM = EMBED_DIM // NUM_HEADS
        NUM_LANDMARKS = 64
        REG = 1e-06
        BATCH = 2
        SEQ = 1024

        def _sq_dists(X, L):
            Xn = jnp.sum(X * X, axis=-1, keepdims=True)
            Ln = jnp.sum(L * L, axis=-1, keepdims=True)
            XL = jnp.einsum('bhnd,bhkd->bhnk', X, L)
            return jnp.maximum(Xn + jnp.swapaxes(Ln, -2, -1) - 2.0 * XL, 0.0)
        key = jax.random.key(seed)
        ks = jax.random.split(key, 10)
        s = 0.02
        inp = {'query': jax.random.normal(ks[0], (BATCH, SEQ, EMBED_DIM), dtype=jnp.float32), 'Wq': jax.random.normal(ks[1], (EMBED_DIM, EMBED_DIM), dtype=jnp.float32) * s, 'bq': jnp.zeros((EMBED_DIM,), jnp.float32), 'Wk': jax.random.normal(ks[2], (EMBED_DIM, EMBED_DIM), dtype=jnp.float32) * s, 'bk': jnp.zeros((EMBED_DIM,), jnp.float32), 'Wv': jax.random.normal(ks[3], (EMBED_DIM, EMBED_DIM), dtype=jnp.float32) * s, 'bv': jnp.zeros((EMBED_DIM,), jnp.float32), 'Wo': jax.random.normal(ks[4], (EMBED_DIM, EMBED_DIM), dtype=jnp.float32) * s, 'bo': jnp.zeros((EMBED_DIM,), jnp.float32), 'temperature': jnp.asarray(float(HEAD_DIM), jnp.float32), 'landmark_idx': jnp.arange(NUM_LANDMARKS, dtype=jnp.int32) * (SEQ // NUM_LANDMARKS)}
        return inp
    _L0_attn_all = _L0_attn_setup()
    _L0_attn_in = {k: v for k, v in _L0_attn_all.items() if k in ('Wq', 'bq', 'Wk', 'bk', 'Wv', 'bv', 'Wo', 'bo', 'temperature', 'landmark_idx')}
    del _L0_attn_all

    def _L0_ffn_setup():
        import jax, jax.numpy as jnp
        import numpy as np
        K = 2
        key = jax.random.key(seed)
        ks = jax.random.split(key, 6)
        B, S, D, U, E = (2, 256, 128, 512, 8)
        return {'x': jax.random.normal(ks[0], (B, S, D), dtype=jnp.float32), 'w_router': jax.random.normal(ks[1], (E, D), dtype=jnp.float32), 'w_up': jax.random.normal(ks[2], (E, U, D), dtype=jnp.float32), 'b_up': jax.random.normal(ks[3], (E, U), dtype=jnp.float32), 'w_down': jax.random.normal(ks[4], (E, D, U), dtype=jnp.float32), 'b_down': jax.random.normal(ks[5], (E, D), dtype=jnp.float32)}
    _L0_ffn_all = _L0_ffn_setup()
    _L0_ffn_in = {k: v for k, v in _L0_ffn_all.items() if k in ('w_router', 'w_up', 'b_up', 'w_down', 'b_down')}
    del _L0_ffn_all

    def _L1_xattn_setup():
        import jax, jax.numpy as jnp
        import numpy as np
        B, L, P = (4, 512, 128)
        D_MODEL = 128
        D_GLOBAL = 256
        HEADDIM = 32
        EPSILON = 0.001
        RMS_EPS = 1e-05

        def rmsnorm(x, g, eps=RMS_EPS):
            var = jnp.mean(jnp.square(x), axis=-1, keepdims=True)
            return x * jax.lax.rsqrt(var + eps) * g

        def _hnet_depool(h, h_patch_full, patch_lens):
            h_patch = h_patch_full[..., :D_MODEL]
            bsz, plen = (h_patch.shape[0], h_patch.shape[1])
            seqlen = h.shape[1]
            logp = jnp.full((bsz, plen), -EPSILON, dtype=jnp.float32)
            bidx = jnp.cumsum(patch_lens, axis=1) - 1
            boundary_mask = jnp.zeros((bsz, seqlen), dtype=jnp.int32)
            boundary_mask = boundary_mask.at[jnp.arange(bsz)[:, None], bidx].set(1)
            dt = (-jnp.log(-jnp.expm1(logp))).astype(h_patch.dtype)
            x = h_patch / dt[..., None]
            n_heads = D_MODEL // HEADDIM
            A = -jnp.ones((n_heads,), dtype=jnp.float32)
            bcoef = jnp.exp(logp).astype(h_patch.dtype)
            x4 = x.reshape(bsz, plen, n_heads, HEADDIM)
            a = jnp.exp(dt[:, :, None] * A[None, None, :])
            u = (dt * bcoef)[:, :, None, None] * x4
            a_b = jnp.broadcast_to(a[..., None], u.shape)

            def comb(lft, rgt):
                aL, uL = lft
                aR, uR = rgt
                return (aL * aR, uL * aR + uR)
            _, s = jax.lax.associative_scan(comb, (a_b, u), axis=1)
            depool = s.reshape(bsz, plen, D_MODEL)
            plug = jnp.clip(jnp.cumsum(boundary_mask, axis=1) - 1, 0, plen - 1)
            depool_out = depool[jnp.arange(bsz)[:, None], plug]
            return depool_out + h
        key = jax.random.key(seed)
        k1, k2, k3, k4 = jax.random.split(key, 4)
        embeds = jax.random.normal(k1, (B, L, D_MODEL), dtype=jnp.float32)
        patch_embeds = jax.random.normal(k2, (B, P, D_GLOBAL), dtype=jnp.float32)
        patch_lens = jnp.full((B, P), L // P, dtype=jnp.int64)
        W_in = jax.random.normal(k3, (D_MODEL, D_MODEL), dtype=jnp.float32) * 0.02
        b_in = jnp.zeros((D_MODEL,), dtype=jnp.float32)
        g_res = jnp.ones((D_MODEL,), dtype=jnp.float32)
        g_init = jnp.ones((D_GLOBAL,), dtype=jnp.float32)
        return {'embeds': embeds, 'patch_embeds': patch_embeds, 'patch_lens': patch_lens, 'W_in': W_in, 'b_in': b_in, 'g_res': g_res, 'g_init': g_init}
    _L1_xattn_all = _L1_xattn_setup()
    _L1_xattn_in = {k: v for k, v in _L1_xattn_all.items() if k in ('W_in', 'b_in', 'g_res', 'g_init')}
    del _L1_xattn_all

    def _L1_attn_setup():
        import jax, jax.numpy as jnp
        import numpy as np
        B_, L_, DM, DS, DC, EX = (4, 256, 128, 16, 4, 2)
        DI = DM * EX
        key = jax.random.key(seed)
        ks = jax.random.split(key, 8)
        s = lambda i, shape, scale: jax.random.normal(ks[i], shape, jnp.float32) * scale
        return dict(x=s(0, (B_, L_, DM), 1.0), in_proj_w=s(1, (2 * DI, DM), 0.02), conv_weight=s(2, (DI, DC), 0.1), conv_bias=jnp.zeros((DI,), jnp.float32), A_log=jax.random.uniform(ks[3], (DS,), jnp.float32, -4.0, -1.0), D=jnp.ones((DI,), jnp.float32), delta_w=s(4, (DS, DI), 0.02), delta_b=jnp.ones((DS,), jnp.float32), B_w=s(5, (DS, DI), 0.02), C_w=s(6, (DS, DI), 0.02), out_proj_w=s(7, (DM, DI), 0.02))
    _L1_attn_all = _L1_attn_setup()
    _L1_attn_in = {k: v for k, v in _L1_attn_all.items() if k in ('in_proj_w', 'conv_weight', 'conv_bias', 'A_log', 'D', 'delta_w', 'delta_b', 'B_w', 'C_w', 'out_proj_w')}
    del _L1_attn_all

    def _L1_ffn_setup():
        import jax, jax.numpy as jnp
        import numpy as np
        ALPHA = 1.702
        LIMIT = 7.0
        EPS = 1e-05
        E = 16
        K = 4

        def _swiglu(h):
            x_glu = jnp.minimum(h[..., ::2], LIMIT)
            x_lin = jnp.clip(h[..., 1::2], LIMIT, LIMIT)
            return x_glu * jax.nn.sigmoid(ALPHA * x_glu) * (x_lin + 1.0)
        key = jax.random.key(seed)
        ks = jax.random.split(key, 7)
        B, T, H, I = (1, 256, 128, 128)
        x = jax.random.normal(ks[0], (B, T, H), jnp.float32)
        scale = jnp.ones((H,), jnp.float32)
        gate_w = jax.random.normal(ks[1], (E, H), jnp.float32) * 0.02
        gate_b = jnp.zeros((E,), jnp.float32)
        mlp1_w = jax.random.normal(ks[2], (E, 2 * I, H), jnp.float32) * 0.02
        mlp1_b = jax.random.normal(ks[3], (E, 2 * I), jnp.float32) * 0.02
        mlp2_w = jax.random.normal(ks[4], (E, H, I), jnp.float32) * 0.02
        mlp2_b = jax.random.normal(ks[5], (E, H), jnp.float32) * 0.02
        return dict(x=x, scale=scale, gate_w=gate_w, gate_b=gate_b, mlp1_w=mlp1_w, mlp1_b=mlp1_b, mlp2_w=mlp2_w, mlp2_b=mlp2_b)
    _L1_ffn_all = _L1_ffn_setup()
    _L1_ffn_in = {k: v for k, v in _L1_ffn_all.items() if k in ('scale', 'gate_w', 'gate_b', 'mlp1_w', 'mlp1_b', 'mlp2_w', 'mlp2_b')}
    del _L1_ffn_all

    def _L2_xattn_setup():
        import jax, jax.numpy as jnp
        import numpy as np
        NUM_HEADS = 16
        key = jax.random.key(seed)
        ks = jax.random.split(key, 5)
        dim = 128
        B, N, N_c = (4, 128, 32)
        x = jax.random.normal(ks[0], (B, N, dim), dtype=jnp.float32)
        context = jax.random.normal(ks[1], (B, N_c, 2 * dim), dtype=jnp.float32)
        w_qkv = jax.random.normal(ks[2], (3 * dim, dim), dtype=jnp.float32) * 0.02
        w_proj = jax.random.normal(ks[3], (dim, dim), dtype=jnp.float32) * 0.02
        b_proj = jax.random.normal(ks[4], (dim,), dtype=jnp.float32) * 0.02
        return {'x': x, 'context': context, 'w_qkv': w_qkv, 'w_proj': w_proj, 'b_proj': b_proj}
    _L2_xattn_all = _L2_xattn_setup()
    _L2_xattn_in = {k: v for k, v in _L2_xattn_all.items() if k in ('w_qkv', 'w_proj', 'b_proj')}
    del _L2_xattn_all

    def _L2_attn_setup():
        import jax, jax.numpy as jnp
        import numpy as np
        B, T, C = (8, 128, 128)
        EPS = 1e-05
        NEG_INF = -1e+38

        def layernorm(x, w, b):
            mu = jnp.mean(x, axis=-1, keepdims=True)
            var = jnp.var(x, axis=-1, keepdims=True)
            return (x - mu) * jax.lax.rsqrt(var + EPS) * w + b

        def wkv_scan(w, u, k, v):
            kt = jnp.swapaxes(k, 0, 1)
            vt = jnp.swapaxes(v, 0, 1)
            bsz = k.shape[0]
            a0 = jnp.zeros((bsz, C), k.dtype)
            b0 = jnp.zeros((bsz, C), k.dtype)
            p0 = jnp.full((bsz, C), NEG_INF, k.dtype)

            def step(carry, inp):
                a, b, p = carry
                kk, vv = inp
                q = jnp.maximum(p, u + kk)
                e1 = jnp.exp(p - q)
                e2 = jnp.exp(u + kk - q)
                out = (e1 * a + e2 * vv) / (e1 * b + e2)
                q2 = jnp.maximum(p + w, kk)
                f1 = jnp.exp(p + w - q2)
                f2 = jnp.exp(kk - q2)
                return ((f1 * a + f2 * vv, f1 * b + f2, q2), out)
            _, outs = jax.lax.scan(step, (a0, b0, p0), (kt, vt))
            return jnp.swapaxes(outs, 0, 1)
        key = jax.random.key(seed)
        ks = jax.random.split(key, 12)
        s = 0.02
        d = {}
        d['x'] = jax.random.normal(ks[0], (B, T, C), jnp.float32)
        d['ln1_w'] = jnp.ones((C,), jnp.float32)
        d['ln1_b'] = jnp.zeros((C,), jnp.float32)
        d['ln2_w'] = jnp.ones((C,), jnp.float32)
        d['ln2_b'] = jnp.zeros((C,), jnp.float32)
        d['Wr'] = jax.random.normal(ks[1], (C, C), jnp.float32) * s
        d['Wk'] = jax.random.normal(ks[2], (C, C), jnp.float32) * s
        d['Wv'] = jax.random.normal(ks[3], (C, C), jnp.float32) * s
        d['Wo'] = jax.random.normal(ks[4], (C, C), jnp.float32) * s
        d['decay'] = jax.random.normal(ks[5], (C,), jnp.float32) * 0.1
        d['u'] = jax.random.normal(ks[6], (C,), jnp.float32) * 0.1
        d['Wfk'] = jax.random.normal(ks[7], (4 * C, C), jnp.float32) * s
        d['Wfv'] = jax.random.normal(ks[8], (C, 4 * C), jnp.float32) * s
        d['Wfr'] = jax.random.normal(ks[9], (C, C), jnp.float32) * s
        return d
    _L2_attn_all = _L2_attn_setup()
    _L2_attn_in = {k: v for k, v in _L2_attn_all.items() if k in ('ln1_w', 'ln1_b', 'ln2_w', 'ln2_b', 'Wr', 'Wk', 'Wv', 'Wo', 'decay', 'u', 'Wfk', 'Wfv', 'Wfr')}
    del _L2_attn_all

    def _L2_ffn_setup():
        import jax, jax.numpy as jnp
        import numpy as np
        H = 16
        E = 8
        EPS = 1e-05

        def _layernorm(x, g, b):
            mu = jnp.mean(x, axis=-1, keepdims=True)
            var = jnp.mean(jnp.square(x - mu), axis=-1, keepdims=True)
            return (x - mu) * jax.lax.rsqrt(var + EPS) * g + b
        key = jax.random.key(seed)
        T, B, C = (128, 8, 128)
        ks = jax.random.split(key, 12)
        s = 0.02
        return {'x': jax.random.normal(ks[0], (T, B, C), jnp.float32), 'in_proj_w': jax.random.normal(ks[1], (3 * C, C), jnp.float32) * s, 'in_proj_b': jnp.zeros((3 * C,), jnp.float32), 'out_w': jax.random.normal(ks[2], (C, C), jnp.float32) * s, 'out_b': jnp.zeros((C,), jnp.float32), 'ln1_g': jnp.ones((C,), jnp.float32), 'ln1_b': jnp.zeros((C,), jnp.float32), 'router_w': jax.random.normal(ks[3], (E, C), jnp.float32) * s, 'router_b': jnp.zeros((E,), jnp.float32), 'w1': jax.random.normal(ks[4], (E, C, C), jnp.float32) * s, 'b1': jnp.zeros((E, C), jnp.float32), 'w2': jax.random.normal(ks[5], (E, C, C), jnp.float32) * s, 'b2': jnp.zeros((E, C), jnp.float32), 'ln2_g': jnp.ones((C,), jnp.float32), 'ln2_b': jnp.zeros((C,), jnp.float32)}
    _L2_ffn_all = _L2_ffn_setup()
    _L2_ffn_in = {k: v for k, v in _L2_ffn_all.items() if k in ('in_proj_w', 'in_proj_b', 'out_w', 'out_b', 'ln1_g', 'ln1_b', 'router_w', 'router_b', 'w1', 'b1', 'w2', 'b2', 'ln2_g', 'ln2_b')}
    del _L2_ffn_all

    def _L3_xattn_setup():
        import jax, jax.numpy as jnp
        import numpy as np
        B, L, P = (4, 512, 128)
        D_MODEL = 128
        D_GLOBAL = 256
        HEADDIM = 32
        EPSILON = 0.001
        RMS_EPS = 1e-05

        def rmsnorm(x, g, eps=RMS_EPS):
            var = jnp.mean(jnp.square(x), axis=-1, keepdims=True)
            return x * jax.lax.rsqrt(var + eps) * g

        def _hnet_depool(h, h_patch_full, patch_lens):
            h_patch = h_patch_full[..., :D_MODEL]
            bsz, plen = (h_patch.shape[0], h_patch.shape[1])
            seqlen = h.shape[1]
            logp = jnp.full((bsz, plen), -EPSILON, dtype=jnp.float32)
            bidx = jnp.cumsum(patch_lens, axis=1) - 1
            boundary_mask = jnp.zeros((bsz, seqlen), dtype=jnp.int32)
            boundary_mask = boundary_mask.at[jnp.arange(bsz)[:, None], bidx].set(1)
            dt = (-jnp.log(-jnp.expm1(logp))).astype(h_patch.dtype)
            x = h_patch / dt[..., None]
            n_heads = D_MODEL // HEADDIM
            A = -jnp.ones((n_heads,), dtype=jnp.float32)
            bcoef = jnp.exp(logp).astype(h_patch.dtype)
            x4 = x.reshape(bsz, plen, n_heads, HEADDIM)
            a = jnp.exp(dt[:, :, None] * A[None, None, :])
            u = (dt * bcoef)[:, :, None, None] * x4
            a_b = jnp.broadcast_to(a[..., None], u.shape)

            def comb(lft, rgt):
                aL, uL = lft
                aR, uR = rgt
                return (aL * aR, uL * aR + uR)
            _, s = jax.lax.associative_scan(comb, (a_b, u), axis=1)
            depool = s.reshape(bsz, plen, D_MODEL)
            plug = jnp.clip(jnp.cumsum(boundary_mask, axis=1) - 1, 0, plen - 1)
            depool_out = depool[jnp.arange(bsz)[:, None], plug]
            return depool_out + h
        key = jax.random.key(seed)
        k1, k2, k3, k4 = jax.random.split(key, 4)
        embeds = jax.random.normal(k1, (B, L, D_MODEL), dtype=jnp.float32)
        patch_embeds = jax.random.normal(k2, (B, P, D_GLOBAL), dtype=jnp.float32)
        patch_lens = jnp.full((B, P), L // P, dtype=jnp.int64)
        W_in = jax.random.normal(k3, (D_MODEL, D_MODEL), dtype=jnp.float32) * 0.02
        b_in = jnp.zeros((D_MODEL,), dtype=jnp.float32)
        g_res = jnp.ones((D_MODEL,), dtype=jnp.float32)
        g_init = jnp.ones((D_GLOBAL,), dtype=jnp.float32)
        return {'embeds': embeds, 'patch_embeds': patch_embeds, 'patch_lens': patch_lens, 'W_in': W_in, 'b_in': b_in, 'g_res': g_res, 'g_init': g_init}
    _L3_xattn_all = _L3_xattn_setup()
    _L3_xattn_in = {k: v for k, v in _L3_xattn_all.items() if k in ('W_in', 'b_in', 'g_res', 'g_init')}
    del _L3_xattn_all

    def _L3_attn_setup():
        import jax, jax.numpy as jnp
        import numpy as np
        HEADS = 16
        MAX_DIST = 128
        key = jax.random.key(seed)
        k1, k2, k3, k4 = jax.random.split(key, 4)
        b, n, dim = (2, 256, 128)
        x = jax.random.normal(k1, (b, n, dim), dtype=jnp.float32)
        W_qkv = jax.random.normal(k2, (3 * dim, dim), dtype=jnp.float32) * dim ** (-0.5)
        W_out = jax.random.normal(k3, (dim, dim), dtype=jnp.float32) * dim ** (-0.5)
        b_out = jnp.zeros((dim,), dtype=jnp.float32)
        rel_emb = jax.random.normal(k4, (2 * MAX_DIST + 1, HEADS), dtype=jnp.float32) * 0.02
        return {'x': x, 'W_qkv': W_qkv, 'W_out': W_out, 'b_out': b_out, 'rel_emb': rel_emb}
    _L3_attn_all = _L3_attn_setup()
    _L3_attn_in = {k: v for k, v in _L3_attn_all.items() if k in ('W_qkv', 'W_out', 'b_out', 'rel_emb')}
    del _L3_attn_all

    def _L3_ffn_setup():
        import jax, jax.numpy as jnp
        import numpy as np
        EPS = 1e-05

        def _quantize(W):
            gamma = jnp.mean(jnp.abs(W))
            return jnp.clip(jnp.round(W / (gamma + EPS)), -1.0, 1.0)
        key = jax.random.key(seed)
        k_x, k_w1, k_b1, k_w2, k_b2 = jax.random.split(key, 5)
        n_embd = 128
        d_ff = 4 * n_embd
        B, S = (4, 512)
        bound1 = 1.0 / np.sqrt(n_embd)
        bound2 = 1.0 / np.sqrt(d_ff)
        x = jax.random.normal(k_x, (B, S, n_embd), dtype=jnp.float32)
        W1 = jax.random.uniform(k_w1, (d_ff, n_embd), jnp.float32, -bound1, bound1)
        b1 = jax.random.uniform(k_b1, (d_ff,), jnp.float32, -bound1, bound1)
        W2 = jax.random.uniform(k_w2, (n_embd, d_ff), jnp.float32, -bound2, bound2)
        b2 = jax.random.uniform(k_b2, (n_embd,), jnp.float32, -bound2, bound2)
        return {'x': x, 'W1': W1, 'b1': b1, 'W2': W2, 'b2': b2}
    _L3_ffn_all = _L3_ffn_setup()
    _L3_ffn_in = {k: v for k, v in _L3_ffn_all.items() if k in ('W1', 'b1', 'W2', 'b2')}
    del _L3_ffn_all
    return {'x': x, 'ctx_2048': ctx_2048, 'mask_BxS2_if0': mask_BxS2_if0, 'L0_xattn_Wq': _L0_xattn_in['Wq'], 'L0_xattn_Wkv': _L0_xattn_in['Wkv'], 'L0_xattn_null_kv': _L0_xattn_in['null_kv'], 'L0_xattn_Wout': _L0_xattn_in['Wout'], 'L0_xattn_ln_scale': _L0_xattn_in['ln_scale'], 'L0_xattn_ln_bias': _L0_xattn_in['ln_bias'], 'L0_attn_Wq': _L0_attn_in['Wq'], 'L0_attn_bq': _L0_attn_in['bq'], 'L0_attn_Wk': _L0_attn_in['Wk'], 'L0_attn_bk': _L0_attn_in['bk'], 'L0_attn_Wv': _L0_attn_in['Wv'], 'L0_attn_bv': _L0_attn_in['bv'], 'L0_attn_Wo': _L0_attn_in['Wo'], 'L0_attn_bo': _L0_attn_in['bo'], 'L0_attn_temperature': _L0_attn_in['temperature'], 'L0_attn_landmark_idx': _L0_attn_in['landmark_idx'], 'L0_ffn_w_router': _L0_ffn_in['w_router'], 'L0_ffn_w_up': _L0_ffn_in['w_up'], 'L0_ffn_b_up': _L0_ffn_in['b_up'], 'L0_ffn_w_down': _L0_ffn_in['w_down'], 'L0_ffn_b_down': _L0_ffn_in['b_down'], 'L1_xattn_W_in': _L1_xattn_in['W_in'], 'L1_xattn_b_in': _L1_xattn_in['b_in'], 'L1_xattn_g_res': _L1_xattn_in['g_res'], 'L1_xattn_g_init': _L1_xattn_in['g_init'], 'L1_attn_in_proj_w': _L1_attn_in['in_proj_w'], 'L1_attn_conv_weight': _L1_attn_in['conv_weight'], 'L1_attn_conv_bias': _L1_attn_in['conv_bias'], 'L1_attn_A_log': _L1_attn_in['A_log'], 'L1_attn_D': _L1_attn_in['D'], 'L1_attn_delta_w': _L1_attn_in['delta_w'], 'L1_attn_delta_b': _L1_attn_in['delta_b'], 'L1_attn_B_w': _L1_attn_in['B_w'], 'L1_attn_C_w': _L1_attn_in['C_w'], 'L1_attn_out_proj_w': _L1_attn_in['out_proj_w'], 'L1_ffn_scale': _L1_ffn_in['scale'], 'L1_ffn_gate_w': _L1_ffn_in['gate_w'], 'L1_ffn_gate_b': _L1_ffn_in['gate_b'], 'L1_ffn_mlp1_w': _L1_ffn_in['mlp1_w'], 'L1_ffn_mlp1_b': _L1_ffn_in['mlp1_b'], 'L1_ffn_mlp2_w': _L1_ffn_in['mlp2_w'], 'L1_ffn_mlp2_b': _L1_ffn_in['mlp2_b'], 'L2_xattn_w_qkv': _L2_xattn_in['w_qkv'], 'L2_xattn_w_proj': _L2_xattn_in['w_proj'], 'L2_xattn_b_proj': _L2_xattn_in['b_proj'], 'L2_attn_ln1_w': _L2_attn_in['ln1_w'], 'L2_attn_ln1_b': _L2_attn_in['ln1_b'], 'L2_attn_ln2_w': _L2_attn_in['ln2_w'], 'L2_attn_ln2_b': _L2_attn_in['ln2_b'], 'L2_attn_Wr': _L2_attn_in['Wr'], 'L2_attn_Wk': _L2_attn_in['Wk'], 'L2_attn_Wv': _L2_attn_in['Wv'], 'L2_attn_Wo': _L2_attn_in['Wo'], 'L2_attn_decay': _L2_attn_in['decay'], 'L2_attn_u': _L2_attn_in['u'], 'L2_attn_Wfk': _L2_attn_in['Wfk'], 'L2_attn_Wfv': _L2_attn_in['Wfv'], 'L2_attn_Wfr': _L2_attn_in['Wfr'], 'L2_ffn_in_proj_w': _L2_ffn_in['in_proj_w'], 'L2_ffn_in_proj_b': _L2_ffn_in['in_proj_b'], 'L2_ffn_out_w': _L2_ffn_in['out_w'], 'L2_ffn_out_b': _L2_ffn_in['out_b'], 'L2_ffn_ln1_g': _L2_ffn_in['ln1_g'], 'L2_ffn_ln1_b': _L2_ffn_in['ln1_b'], 'L2_ffn_router_w': _L2_ffn_in['router_w'], 'L2_ffn_router_b': _L2_ffn_in['router_b'], 'L2_ffn_w1': _L2_ffn_in['w1'], 'L2_ffn_b1': _L2_ffn_in['b1'], 'L2_ffn_w2': _L2_ffn_in['w2'], 'L2_ffn_b2': _L2_ffn_in['b2'], 'L2_ffn_ln2_g': _L2_ffn_in['ln2_g'], 'L2_ffn_ln2_b': _L2_ffn_in['ln2_b'], 'L3_xattn_W_in': _L3_xattn_in['W_in'], 'L3_xattn_b_in': _L3_xattn_in['b_in'], 'L3_xattn_g_res': _L3_xattn_in['g_res'], 'L3_xattn_g_init': _L3_xattn_in['g_init'], 'L3_attn_W_qkv': _L3_attn_in['W_qkv'], 'L3_attn_W_out': _L3_attn_in['W_out'], 'L3_attn_b_out': _L3_attn_in['b_out'], 'L3_attn_rel_emb': _L3_attn_in['rel_emb'], 'L3_ffn_W1': _L3_ffn_in['W1'], 'L3_ffn_b1': _L3_ffn_in['b1'], 'L3_ffn_W2': _L3_ffn_in['W2'], 'L3_ffn_b2': _L3_ffn_in['b2']}

def reference(x, ctx_2048, mask_BxS2_if0, L0_xattn_Wq, L0_xattn_Wkv, L0_xattn_null_kv, L0_xattn_Wout, L0_xattn_ln_scale, L0_xattn_ln_bias, L0_attn_Wq, L0_attn_bq, L0_attn_Wk, L0_attn_bk, L0_attn_Wv, L0_attn_bv, L0_attn_Wo, L0_attn_bo, L0_attn_temperature, L0_attn_landmark_idx, L0_ffn_w_router, L0_ffn_w_up, L0_ffn_b_up, L0_ffn_w_down, L0_ffn_b_down, L1_xattn_W_in, L1_xattn_b_in, L1_xattn_g_res, L1_xattn_g_init, L1_attn_in_proj_w, L1_attn_conv_weight, L1_attn_conv_bias, L1_attn_A_log, L1_attn_D, L1_attn_delta_w, L1_attn_delta_b, L1_attn_B_w, L1_attn_C_w, L1_attn_out_proj_w, L1_ffn_scale, L1_ffn_gate_w, L1_ffn_gate_b, L1_ffn_mlp1_w, L1_ffn_mlp1_b, L1_ffn_mlp2_w, L1_ffn_mlp2_b, L2_xattn_w_qkv, L2_xattn_w_proj, L2_xattn_b_proj, L2_attn_ln1_w, L2_attn_ln1_b, L2_attn_ln2_w, L2_attn_ln2_b, L2_attn_Wr, L2_attn_Wk, L2_attn_Wv, L2_attn_Wo, L2_attn_decay, L2_attn_u, L2_attn_Wfk, L2_attn_Wfv, L2_attn_Wfr, L2_ffn_in_proj_w, L2_ffn_in_proj_b, L2_ffn_out_w, L2_ffn_out_b, L2_ffn_ln1_g, L2_ffn_ln1_b, L2_ffn_router_w, L2_ffn_router_b, L2_ffn_w1, L2_ffn_b1, L2_ffn_w2, L2_ffn_b2, L2_ffn_ln2_g, L2_ffn_ln2_b, L3_xattn_W_in, L3_xattn_b_in, L3_xattn_g_res, L3_xattn_g_init, L3_attn_W_qkv, L3_attn_W_out, L3_attn_b_out, L3_attn_rel_emb, L3_ffn_W1, L3_ffn_b1, L3_ffn_W2, L3_ffn_b2):
    import jax
    import jax.numpy as jnp

    def _L0_xattn_ref(x, context, Wq, Wkv, null_kv, Wout, ln_scale, ln_bias):
        import jax, jax.numpy as jnp
        import numpy as np
        B, N, DIM = (8, 512, 128)
        M, CTX = (32, 256)
        HEADS, DH = (16, 64)
        INNER = HEADS * DH
        EPS = 1e-06

        def _split_heads(t):
            b, n, _ = t.shape
            return t.reshape(b, n, HEADS, DH).transpose(0, 2, 1, 3)
        scale = DH ** (-0.5)
        b = x.shape[0]
        q = _split_heads(jnp.einsum('bnd,df->bnf', x, Wq))
        kv = jnp.einsum('bmc,cf->bmf', context, Wkv)
        k, v = jnp.split(kv, 2, axis=-1)
        k, v = (_split_heads(k), _split_heads(v))
        nk = jnp.broadcast_to(null_kv[0], (b, HEADS, 1, DH))
        nv = jnp.broadcast_to(null_kv[1], (b, HEADS, 1, DH))
        k = jnp.concatenate((nk, k), axis=-2)
        v = jnp.concatenate((nv, v), axis=-2)
        q = q * scale
        sim = jnp.einsum('bhid,bhjd->bhij', q, k)
        attn = jax.nn.softmax(sim, axis=-1)
        out = jnp.einsum('bhij,bhjd->bhid', attn, v)
        out = out.transpose(0, 2, 1, 3).reshape(b, -1, INNER)
        out = jnp.einsum('bnf,fd->bnd', out, Wout)
        mu = jnp.mean(out, axis=-1, keepdims=True)
        var = jnp.var(out, axis=-1, keepdims=True)
        out = (out - mu) * jax.lax.rsqrt(var + EPS) * ln_scale + ln_bias
        return out

    def _L0_attn_ref(query, Wq, bq, Wk, bk, Wv, bv, Wo, bo, temperature, landmark_idx):
        import jax, jax.numpy as jnp
        import numpy as np
        EMBED_DIM = 128
        NUM_HEADS = 16
        HEAD_DIM = EMBED_DIM // NUM_HEADS
        NUM_LANDMARKS = 64
        REG = 1e-06
        BATCH = 2
        SEQ = 1024

        def _sq_dists(X, L):
            Xn = jnp.sum(X * X, axis=-1, keepdims=True)
            Ln = jnp.sum(L * L, axis=-1, keepdims=True)
            XL = jnp.einsum('bhnd,bhkd->bhnk', X, L)
            return jnp.maximum(Xn + jnp.swapaxes(Ln, -2, -1) - 2.0 * XL, 0.0)
        b, n, _ = query.shape
        Q = (query @ Wq.T + bq).reshape(b, n, NUM_HEADS, HEAD_DIM).transpose(0, 2, 1, 3)
        K = (query @ Wk.T + bk).reshape(b, n, NUM_HEADS, HEAD_DIM).transpose(0, 2, 1, 3)
        V = (query @ Wv.T + bv).reshape(b, n, NUM_HEADS, HEAD_DIM).transpose(0, 2, 1, 3)
        landmarks = K[:, :, landmark_idx, :]
        C_Q = _sq_dists(Q, landmarks)
        C_K = _sq_dists(K, landmarks)
        W_sq = C_K[:, :, landmark_idx, :]
        Phi_Q = jnp.exp(-C_Q / temperature)
        Phi_K = jnp.exp(-C_K / temperature)
        W_kernel = jnp.exp(-W_sq / temperature) + REG * jnp.eye(NUM_LANDMARKS, dtype=query.dtype)
        Z = jnp.einsum('bhnk,bhnd->bhkd', Phi_K, V)
        Y = jnp.linalg.solve(W_kernel, Z)
        out_unnorm = jnp.einsum('bhnk,bhkd->bhnd', Phi_Q, Y)
        Phi_K_sum = jnp.sum(Phi_K, axis=-2)[..., None]
        norm = jnp.einsum('bhnk,bhko->bhno', Phi_Q, jnp.linalg.solve(W_kernel, Phi_K_sum))
        norm = jnp.maximum(norm, 1e-10)
        out = out_unnorm / norm
        out = out.transpose(0, 2, 1, 3).reshape(b, n, EMBED_DIM)
        return out @ Wo.T + bo

    def _L0_ffn_ref(x, w_router, w_up, b_up, w_down, b_down):
        import jax, jax.numpy as jnp
        import numpy as np
        K = 2
        logits = jnp.einsum('bsd,ed->bse', x, w_router)
        top_logits, idx = jax.lax.top_k(logits, K)
        router_weights = jax.nn.softmax(top_logits, axis=-1)
        h = jnp.einsum('eud,bsd->bseu', w_up, x) + b_up[None, None]
        h = jax.nn.gelu(h, approximate=False)
        y = jnp.einsum('edu,bseu->bsed', w_down, h) + b_down[None, None]
        y_k = jnp.take_along_axis(y, idx[..., None], axis=2)
        out = jnp.einsum('bskd,bsk->bsd', y_k, router_weights)
        return out

    def _L1_xattn_ref(embeds, patch_embeds, patch_lens, W_in, b_in, g_res, g_init):
        import jax, jax.numpy as jnp
        import numpy as np
        B, L, P = (4, 512, 128)
        D_MODEL = 128
        D_GLOBAL = 256
        HEADDIM = 32
        EPSILON = 0.001
        RMS_EPS = 1e-05

        def rmsnorm(x, g, eps=RMS_EPS):
            var = jnp.mean(jnp.square(x), axis=-1, keepdims=True)
            return x * jax.lax.rsqrt(var + eps) * g

        def _hnet_depool(h, h_patch_full, patch_lens):
            h_patch = h_patch_full[..., :D_MODEL]
            bsz, plen = (h_patch.shape[0], h_patch.shape[1])
            seqlen = h.shape[1]
            logp = jnp.full((bsz, plen), -EPSILON, dtype=jnp.float32)
            bidx = jnp.cumsum(patch_lens, axis=1) - 1
            boundary_mask = jnp.zeros((bsz, seqlen), dtype=jnp.int32)
            boundary_mask = boundary_mask.at[jnp.arange(bsz)[:, None], bidx].set(1)
            dt = (-jnp.log(-jnp.expm1(logp))).astype(h_patch.dtype)
            x = h_patch / dt[..., None]
            n_heads = D_MODEL // HEADDIM
            A = -jnp.ones((n_heads,), dtype=jnp.float32)
            bcoef = jnp.exp(logp).astype(h_patch.dtype)
            x4 = x.reshape(bsz, plen, n_heads, HEADDIM)
            a = jnp.exp(dt[:, :, None] * A[None, None, :])
            u = (dt * bcoef)[:, :, None, None] * x4
            a_b = jnp.broadcast_to(a[..., None], u.shape)

            def comb(lft, rgt):
                aL, uL = lft
                aR, uR = rgt
                return (aL * aR, uL * aR + uR)
            _, s = jax.lax.associative_scan(comb, (a_b, u), axis=1)
            depool = s.reshape(bsz, plen, D_MODEL)
            plug = jnp.clip(jnp.cumsum(boundary_mask, axis=1) - 1, 0, plen - 1)
            depool_out = depool[jnp.arange(bsz)[:, None], plug]
            return depool_out + h
        h = rmsnorm(embeds, g_res)
        h = jnp.einsum('bld,ed->ble', h, W_in) + b_in
        h_patch = rmsnorm(patch_embeds, g_init)
        return _hnet_depool(h, h_patch, patch_lens)

    def _L1_attn_ref(x, in_proj_w, conv_weight, conv_bias, A_log, D, delta_w, delta_b, B_w, C_w, out_proj_w):
        import jax, jax.numpy as jnp
        import numpy as np
        B_, L_, DM, DS, DC, EX = (4, 256, 128, 16, 4, 2)
        DI = DM * EX
        Bb, L, Dm = x.shape
        di, dc = conv_weight.shape
        x_inner = x @ in_proj_w.T
        x_ssm, x_gate = (x_inner[..., :di], x_inner[..., di:])
        xp = jnp.pad(x_ssm, ((0, 0), (dc - 1, 0), (0, 0)))
        xc = conv_bias + sum((xp[:, k:k + L, :] * conv_weight[:, k] for k in range(dc)))
        x_conv = jax.nn.silu(xc)
        delta = jax.nn.softplus(x_conv @ delta_w.T + delta_b)
        Bs = x_conv @ B_w.T
        Cs = x_conv @ C_w.T
        A = -jnp.exp(A_log)
        xavg = x_conv.mean(axis=-1)

        def step(h, inp):
            dt, bt, ct, xa = inp
            h = jnp.exp(dt * A) * h + dt * bt * xa[:, None]
            return (h, (h * ct).sum(-1))
        h0 = jnp.zeros((Bb, A.shape[0]), x.dtype)
        _, ys = jax.lax.scan(step, h0, (delta.transpose(1, 0, 2), Bs.transpose(1, 0, 2), Cs.transpose(1, 0, 2), xavg.T))
        y_ssm = ys.T[..., None]
        y_gated = y_ssm * jax.nn.silu(x_gate)
        y_skip = y_gated + x_conv * D
        return y_skip @ out_proj_w.T

    def _L1_ffn_ref(x, scale, gate_w, gate_b, mlp1_w, mlp1_b, mlp2_w, mlp2_b):
        import jax, jax.numpy as jnp
        import numpy as np
        ALPHA = 1.702
        LIMIT = 7.0
        EPS = 1e-05
        E = 16
        K = 4

        def _swiglu(h):
            x_glu = jnp.minimum(h[..., ::2], LIMIT)
            x_lin = jnp.clip(h[..., 1::2], LIMIT, LIMIT)
            return x_glu * jax.nn.sigmoid(ALPHA * x_glu) * (x_lin + 1.0)
        t = x * jax.lax.rsqrt(jnp.mean(x * x, axis=-1, keepdims=True) + EPS) * scale
        g = jnp.einsum('bth,eh->bte', t, gate_w) + gate_b
        vals, idx = jax.lax.top_k(g, K)
        w = jax.nn.softmax(vals, axis=-1)
        route = jnp.sum(jax.nn.one_hot(idx, E, dtype=t.dtype) * w[..., None], axis=-2)
        route_e = jnp.moveaxis(route, -1, 0)

        def step(acc, p):
            w1, b1, w2, b2, r = p
            h = jnp.einsum('bth,ih->bti', t, w1) + b1
            s = _swiglu(h)
            y = jnp.einsum('bti,hi->bth', s, w2) + b2
            return (acc + r[..., None] * y, None)
        acc, _ = jax.lax.scan(step, jnp.zeros_like(x), (mlp1_w, mlp1_b, mlp2_w, mlp2_b, route_e))
        return x + acc

    def _L2_xattn_ref(x, context, w_qkv, w_proj, b_proj):
        import jax, jax.numpy as jnp
        import numpy as np
        NUM_HEADS = 16
        B, N, C = x.shape
        H = NUM_HEADS
        D = C // H
        scale = D ** (-0.5)
        qkv = (x @ w_qkv.T).reshape(B, N, 3, H, D).transpose(2, 0, 3, 1, 4)
        q, k, v = (qkv[0], qkv[1], qkv[2])
        N_c = context.shape[1]
        kv = context.reshape(B, N_c, 2, H, D).transpose(2, 0, 3, 1, 4)
        extra_k, extra_v = (kv[0], kv[1])
        k = jnp.concatenate([extra_k, k], axis=2)
        v = jnp.concatenate([extra_v, v], axis=2)
        dtype = q.dtype
        attn = jnp.einsum('bhnd,bhmd->bhnm', q * scale, k).astype(jnp.float32)
        attn = jax.nn.softmax(attn, axis=-1).astype(dtype)
        out = jnp.einsum('bhnm,bhmd->bhnd', attn, v)
        out = out.transpose(0, 2, 1, 3).reshape(B, N, C)
        return out @ w_proj.T + b_proj

    def _L2_attn_ref(x, ln1_w, ln1_b, ln2_w, ln2_b, Wr, Wk, Wv, Wo, decay, u, Wfk, Wfv, Wfr):
        import jax, jax.numpy as jnp
        import numpy as np
        B, T, C = (8, 128, 128)
        EPS = 1e-05
        NEG_INF = -1e+38

        def layernorm(x, w, b):
            mu = jnp.mean(x, axis=-1, keepdims=True)
            var = jnp.var(x, axis=-1, keepdims=True)
            return (x - mu) * jax.lax.rsqrt(var + EPS) * w + b

        def wkv_scan(w, u, k, v):
            kt = jnp.swapaxes(k, 0, 1)
            vt = jnp.swapaxes(v, 0, 1)
            bsz = k.shape[0]
            a0 = jnp.zeros((bsz, C), k.dtype)
            b0 = jnp.zeros((bsz, C), k.dtype)
            p0 = jnp.full((bsz, C), NEG_INF, k.dtype)

            def step(carry, inp):
                a, b, p = carry
                kk, vv = inp
                q = jnp.maximum(p, u + kk)
                e1 = jnp.exp(p - q)
                e2 = jnp.exp(u + kk - q)
                out = (e1 * a + e2 * vv) / (e1 * b + e2)
                q2 = jnp.maximum(p + w, kk)
                f1 = jnp.exp(p + w - q2)
                f2 = jnp.exp(kk - q2)
                return ((f1 * a + f2 * vv, f1 * b + f2, q2), out)
            _, outs = jax.lax.scan(step, (a0, b0, p0), (kt, vt))
            return jnp.swapaxes(outs, 0, 1)
        xn = layernorm(x, ln1_w, ln1_b)
        r = jax.nn.sigmoid(xn @ Wr.T)
        k = xn @ Wk.T
        v = xn @ Wv.T
        w = -jnp.exp(decay)
        wkv_f = wkv_scan(w, u, k, v)
        wkv_b = jnp.flip(wkv_scan(w, u, jnp.flip(k, axis=1), jnp.flip(v, axis=1)), axis=1)
        wkv = 0.5 * (wkv_f + wkv_b)
        x = x + r * wkv @ Wo.T
        xn2 = layernorm(x, ln2_w, ln2_b)
        kk = jnp.square(jax.nn.relu(xn2 @ Wfk.T))
        x = x + jax.nn.sigmoid(xn2 @ Wfr.T) * (kk @ Wfv.T)
        return x

    def _L2_ffn_ref(x, in_proj_w, in_proj_b, out_w, out_b, ln1_g, ln1_b, router_w, router_b, w1, b1, w2, b2, ln2_g, ln2_b):
        import jax, jax.numpy as jnp
        import numpy as np
        H = 16
        E = 8
        EPS = 1e-05

        def _layernorm(x, g, b):
            mu = jnp.mean(x, axis=-1, keepdims=True)
            var = jnp.mean(jnp.square(x - mu), axis=-1, keepdims=True)
            return (x - mu) * jax.lax.rsqrt(var + EPS) * g + b
        T, B, C = x.shape
        D = C // H
        qkv = x @ in_proj_w.T + in_proj_b
        q, k, v = jnp.split(qkv, 3, axis=-1)
        q = q.reshape(T, B, H, D)
        k = k.reshape(T, B, H, D)
        v = v.reshape(T, B, H, D)
        scale = 1.0 / np.sqrt(D).astype(np.float32)
        scores = jnp.einsum('tbhd,sbhd->bhts', q, k) * scale
        attn = jax.nn.softmax(scores, axis=-1)
        ctx = jnp.einsum('bhts,sbhd->tbhd', attn, v).reshape(T, B, C)
        attn_out = ctx @ out_w.T + out_b
        h = _layernorm(x + attn_out, ln1_g, ln1_b)
        flat = h.reshape(-1, C)
        logits = flat @ router_w.T + router_b
        probs = jax.nn.softmax(logits, axis=-1)
        _, top_i = jax.lax.top_k(probs, 2)
        assign = jnp.max(top_i, axis=-1)
        out = jnp.zeros_like(flat)
        for e in range(E):
            he = jax.nn.gelu(flat @ w1[e].T + b1[e], approximate=False)
            oe = he @ w2[e].T + b2[e]
            out = jnp.where((assign == e)[:, None], oe, out)
        moe_out = out.reshape(T, B, C)
        return _layernorm(h + moe_out, ln2_g, ln2_b)

    def _L3_xattn_ref(embeds, patch_embeds, patch_lens, W_in, b_in, g_res, g_init):
        import jax, jax.numpy as jnp
        import numpy as np
        B, L, P = (4, 512, 128)
        D_MODEL = 128
        D_GLOBAL = 256
        HEADDIM = 32
        EPSILON = 0.001
        RMS_EPS = 1e-05

        def rmsnorm(x, g, eps=RMS_EPS):
            var = jnp.mean(jnp.square(x), axis=-1, keepdims=True)
            return x * jax.lax.rsqrt(var + eps) * g

        def _hnet_depool(h, h_patch_full, patch_lens):
            h_patch = h_patch_full[..., :D_MODEL]
            bsz, plen = (h_patch.shape[0], h_patch.shape[1])
            seqlen = h.shape[1]
            logp = jnp.full((bsz, plen), -EPSILON, dtype=jnp.float32)
            bidx = jnp.cumsum(patch_lens, axis=1) - 1
            boundary_mask = jnp.zeros((bsz, seqlen), dtype=jnp.int32)
            boundary_mask = boundary_mask.at[jnp.arange(bsz)[:, None], bidx].set(1)
            dt = (-jnp.log(-jnp.expm1(logp))).astype(h_patch.dtype)
            x = h_patch / dt[..., None]
            n_heads = D_MODEL // HEADDIM
            A = -jnp.ones((n_heads,), dtype=jnp.float32)
            bcoef = jnp.exp(logp).astype(h_patch.dtype)
            x4 = x.reshape(bsz, plen, n_heads, HEADDIM)
            a = jnp.exp(dt[:, :, None] * A[None, None, :])
            u = (dt * bcoef)[:, :, None, None] * x4
            a_b = jnp.broadcast_to(a[..., None], u.shape)

            def comb(lft, rgt):
                aL, uL = lft
                aR, uR = rgt
                return (aL * aR, uL * aR + uR)
            _, s = jax.lax.associative_scan(comb, (a_b, u), axis=1)
            depool = s.reshape(bsz, plen, D_MODEL)
            plug = jnp.clip(jnp.cumsum(boundary_mask, axis=1) - 1, 0, plen - 1)
            depool_out = depool[jnp.arange(bsz)[:, None], plug]
            return depool_out + h
        h = rmsnorm(embeds, g_res)
        h = jnp.einsum('bld,ed->ble', h, W_in) + b_in
        h_patch = rmsnorm(patch_embeds, g_init)
        return _hnet_depool(h, h_patch, patch_lens)

    def _L3_attn_ref(x, W_qkv, W_out, b_out, rel_emb):
        import jax, jax.numpy as jnp
        import numpy as np
        HEADS = 16
        MAX_DIST = 128
        b, n, dim = x.shape
        h = HEADS
        d = dim // h
        scale = d ** (-0.5)
        qkv = jnp.einsum('bnd,ed->bne', x, W_qkv)
        q, k, v = jnp.split(qkv, 3, axis=-1)

        def to_heads(t):
            return t.reshape(b, n, h, d).transpose(0, 2, 1, 3)
        q, k, v = (to_heads(q), to_heads(k), to_heads(v))
        dist = jnp.arange(n)[None, :] - jnp.arange(n)[:, None]
        idx = jnp.clip(dist, -MAX_DIST, MAX_DIST) + MAX_DIST
        rel_bias = rel_emb[idx].transpose(2, 0, 1)[None]
        scores = jnp.einsum('bhqd,bhkd->bhqk', q, k) * scale + rel_bias
        attn = jax.nn.softmax(scores, axis=-1)
        out = jnp.einsum('bhqk,bhkd->bhqd', attn, v)
        out = out.transpose(0, 2, 1, 3).reshape(b, n, dim)
        return jnp.einsum('bnd,ed->bne', out, W_out) + b_out

    def _L3_ffn_ref(x, W1, b1, W2, b2):
        import jax, jax.numpy as jnp
        import numpy as np
        EPS = 1e-05

        def _quantize(W):
            gamma = jnp.mean(jnp.abs(W))
            return jnp.clip(jnp.round(W / (gamma + EPS)), -1.0, 1.0)
        Wq1 = _quantize(W1)
        Wq2 = _quantize(W2)
        h = jax.nn.relu(jnp.einsum('bsd,fd->bsf', x, Wq1) + b1)
        out = jnp.einsum('bsf,df->bsd', h, Wq2) + b2
        return out
    x = x + _L0_xattn_ref(_layernorm(x, axis=-1), ctx_2048, L0_xattn_Wq, L0_xattn_Wkv, L0_xattn_null_kv, L0_xattn_Wout, L0_xattn_ln_scale, L0_xattn_ln_bias)
    x = x + _L0_attn_ref(_layernorm(x, axis=-1), L0_attn_Wq, L0_attn_bq, L0_attn_Wk, L0_attn_bk, L0_attn_Wv, L0_attn_bv, L0_attn_Wo, L0_attn_bo, L0_attn_temperature, L0_attn_landmark_idx)
    x = x + _L0_ffn_ref(_layernorm(x, axis=-1), L0_ffn_w_router, L0_ffn_w_up, L0_ffn_b_up, L0_ffn_w_down, L0_ffn_b_down)
    x = x + _L1_xattn_ref(_layernorm(x, axis=-1), ctx_2048, mask_BxS2_if0, L1_xattn_W_in, L1_xattn_b_in, L1_xattn_g_res, L1_xattn_g_init)
    x = x + _L1_attn_ref(_layernorm(x, axis=-1), L1_attn_in_proj_w, L1_attn_conv_weight, L1_attn_conv_bias, L1_attn_A_log, L1_attn_D, L1_attn_delta_w, L1_attn_delta_b, L1_attn_B_w, L1_attn_C_w, L1_attn_out_proj_w)
    x = x + _L1_ffn_ref(_layernorm(x, axis=-1), L1_ffn_scale, L1_ffn_gate_w, L1_ffn_gate_b, L1_ffn_mlp1_w, L1_ffn_mlp1_b, L1_ffn_mlp2_w, L1_ffn_mlp2_b)
    x = x + _L2_xattn_ref(_layernorm(x, axis=-1), ctx_2048, L2_xattn_w_qkv, L2_xattn_w_proj, L2_xattn_b_proj)
    x = x + _L2_attn_ref(_layernorm(x, axis=-1), L2_attn_ln1_w, L2_attn_ln1_b, L2_attn_ln2_w, L2_attn_ln2_b, L2_attn_Wr, L2_attn_Wk, L2_attn_Wv, L2_attn_Wo, L2_attn_decay, L2_attn_u, L2_attn_Wfk, L2_attn_Wfv, L2_attn_Wfr)
    x = x + _L2_ffn_ref(_layernorm(x, axis=-1), L2_ffn_in_proj_w, L2_ffn_in_proj_b, L2_ffn_out_w, L2_ffn_out_b, L2_ffn_ln1_g, L2_ffn_ln1_b, L2_ffn_router_w, L2_ffn_router_b, L2_ffn_w1, L2_ffn_b1, L2_ffn_w2, L2_ffn_b2, L2_ffn_ln2_g, L2_ffn_ln2_b)
    x = x + _L3_xattn_ref(_layernorm(x, axis=-1), ctx_2048, mask_BxS2_if0, L3_xattn_W_in, L3_xattn_b_in, L3_xattn_g_res, L3_xattn_g_init)
    x = x + _L3_attn_ref(_layernorm(x, axis=-1), L3_attn_W_qkv, L3_attn_W_out, L3_attn_b_out, L3_attn_rel_emb)
    x = x + _L3_ffn_ref(_layernorm(x, axis=-1), L3_ffn_W1, L3_ffn_b1, L3_ffn_W2, L3_ffn_b2)
    return x

_drawn_inputs = setup_inputs


def setup_inputs(seed=0):
    import zlib

    import numpy as np

    out = dict(_drawn_inputs(seed))
    spreads = {'L0_xattn_ln_scale': (1.0, 0.2),
     'L0_xattn_ln_bias': (0.0, 0.1),
     'L0_attn_bq': (0.0, 2.0),
     'L0_attn_bk': (0.0, 2.0),
     'L0_attn_bv': (0.0, 0.1),
     'L0_attn_bo': (0.0, 0.1),
     'L1_xattn_b_in': (0.0, 2.0),
     'L1_xattn_g_res': (1.0, 0.6),
     'L1_xattn_g_init': (1.0, 0.6),
     'L1_attn_conv_bias': (0.0, 0.8),
     'L1_attn_D': (1.0, 0.6),
     'L1_attn_delta_b': (1.0, 0.6),
     'L1_ffn_scale': (1.0, 0.6),
     'L1_ffn_gate_b': (0.0, 2.0),
     'L2_attn_ln1_w': (1.0, 0.6),
     'L2_attn_ln1_b': (0.0, 2.0),
     'L2_attn_ln2_w': (1.0, 0.6),
     'L2_attn_ln2_b': (0.0, 2.0),
     'L2_ffn_in_proj_b': (0.0, 2.0),
     'L2_ffn_out_b': (0.0, 2.0),
     'L2_ffn_ln1_g': (1.0, 0.6),
     'L2_ffn_ln1_b': (0.0, 2.0),
     'L2_ffn_router_b': (0.0, 2.0),
     'L2_ffn_b1': (0.0, 2.0),
     'L2_ffn_b2': (0.0, 2.0),
     'L2_ffn_ln2_g': (1.0, 0.6),
     'L2_ffn_ln2_b': (0.0, 2.0),
     'L3_xattn_b_in': (0.0, 2.0),
     'L3_xattn_g_res': (1.0, 0.6),
     'L3_xattn_g_init': (1.0, 0.6),
     'L3_attn_b_out': (0.0, 2.0)}
    factors = {'L0_attn_Wq': 8.0,
     'L0_attn_Wk': 8.0,
     'L0_ffn_b_down': 8.0,
     'L1_xattn_W_in': 8.0,
     'L1_attn_in_proj_w': 8.0,
     'L1_attn_conv_weight': 8.0,
     'L1_attn_A_log': 64.0,
     'L1_attn_delta_w': 8.0,
     'L1_attn_B_w': 8.0,
     'L1_attn_C_w': 8.0,
     'L1_attn_out_proj_w': 8.0,
     'L1_ffn_gate_w': 64.0,
     'L1_ffn_mlp1_w': 64.0,
     'L1_ffn_mlp1_b': 64.0,
     'L1_ffn_mlp2_w': 64.0,
     'L1_ffn_mlp2_b': 200.0,
     'L2_xattn_w_qkv': 64.0,
     'L2_xattn_w_proj': 64.0,
     'L2_xattn_b_proj': 200.0,
     'L2_attn_Wr': 64.0,
     'L2_attn_Wk': 64.0,
     'L2_attn_Wv': 64.0,
     'L2_attn_Wo': 64.0,
     'L2_attn_decay': 64.0,
     'L2_attn_u': 64.0,
     'L2_attn_Wfk': 64.0,
     'L2_attn_Wfv': 64.0,
     'L2_attn_Wfr': 64.0,
     'L2_ffn_in_proj_w': 200.0,
     'L2_ffn_out_w': 200.0,
     'L2_ffn_router_w': 200.0,
     'L2_ffn_w1': 200.0,
     'L2_ffn_w2': 200.0,
     'L3_xattn_W_in': 200.0,
     'L3_attn_W_qkv': 64.0,
     'L3_attn_W_out': 64.0,
     'L3_attn_rel_emb': 200.0,
     'L3_ffn_b1': 200.0,
     'L3_ffn_b2': 200.0,
     'L3_ffn_W1': 48.584,
     'L3_ffn_W2': 40.432}
    for name, (base, spread) in spreads.items():
        noise = np.random.default_rng([zlib.crc32(name.encode()), seed]).standard_normal(out[name].shape)
        drawn = base * np.exp(spread * noise) if base else spread * noise
        out[name] = jnp.asarray(drawn.astype(out[name].dtype))
    for name, factor in factors.items():
        out[name] = (out[name] * factor).astype(out[name].dtype)
    return out
```

```python
from contextlib import ExitStack

import numpy as np

import concourse.bass as bass
from concourse import mybir

ALU = mybir.AluOpType
ACT = mybir.ActivationFunctionType
F32 = mybir.dt.float32
I32 = mybir.dt.int32
AX = mybir.AxisListType.X
ds = bass.ds

B, S, D = 128, 32, 128
TOK = B * S
P = 128
TILES = TOK // P
BT = P // S
CHUNK = 512
TC = CHUNK // P
CHUNKS = TOK // CHUNK
BC = CHUNK // S
KEYS = 257
C = 256
H16 = 16
DH = 8
EPS = 1e-5
LOG_TINY = -87.33654
LOG_PASS = -1e-3
PATCH_DECAY = float(-np.expm1(LOG_PASS))
PATCH_GAIN = float(np.exp(LOG_PASS))


class Chain:

    def __init__(self, eng, sem, base=0, per=None):
        self.eng, self.sem, self.base, self.per, self.n = eng, sem, base, per, 0

    def __call__(self, ins):
        self.n += 1
        ins.then_inc(self.sem, 1)
        self.eng.wait_ge(self.sem, self.base + self.n)

    def done(self):
        assert self.per is None or self.n == self.per, f"chain {self.sem} has {self.n} links, not {self.per}"


class Core:

    def __init__(self, nc, ctx, args):
        self.nc, self.ctx, self.a = nc, ctx, args

        self.sems = []

    def sem(self, name):
        self.sems.append(self.nc.alloc_semaphore(name=name))
        return self.sems[-1]


class Stage(ExitStack):

    def __init__(self, k):
        super().__init__()
        self.k = k

    def __exit__(self, *exc):
        super().__exit__(*exc)
        self.k.nc.clear_and_free_semaphores(self.k.sems)
        self.k.nc.all_engine_barrier()
        self.k.sems = []


def buffers(nc, ctx):
    def sb(name, shape, dt=F32):
        return ctx.enter_context(nc.sbuf_tensor(name, list(shape), dt))

    def ps(name, shape):
        return ctx.enter_context(nc.psum_tensor(name, list(shape), F32))

    return sb, ps


def bcast(ap, axis, n):
    ap = ap.unsqueeze(axis)
    shape = list(ap.shape)
    shape[axis] = n
    return ap.broadcast_to(shape)



def normalise(k, name, src, gain=None, bias=None, twice=False, keep=None, add_to=None, residual=False, whole=False, eps=EPS):
    nc = k.nc
    ctx = Stage(k)
    with ctx:
        sb, ps = buffers(nc, ctx)
        stats = sb(f"{name}_stats", [P, TILES, 6])
        mean = sb(f"{name}_mean", [P, TILES])
        diff = sb(f"{name}_diff", [P, TILES])
        var = sb(f"{name}_var", [P, TILES])
        var2 = sb(f"{name}_var2", [P, TILES])
        rstd = sb(f"{name}_rstd", [P, TILES])
        rstd2 = sb(f"{name}_rstd2", [P, TILES])
        total = sb(f"{name}_total", [P, TILES])
        expo = sb(f"{name}_expo", [P, TILES])
        cols = sb(f"{name}_cols", [P, 2])
        rows = sb(f"{name}_rows", [P, 2, D])
        xn = sb(f"{name}_xn", [P, 2, TC, D])
        once = sb(f"{name}_once", [P, 2, TC, D])
        psT = ps(f"{name}_psT", [P, 2, CHUNK])

        loaded = k.sem(f"{name}_loaded")
        expo_set = k.sem(f"{name}_expo_set")
        stats_done = k.sem(f"{name}_stats_done")
        link = k.sem(f"{name}_link")
        var_done = k.sem(f"{name}_var_done")
        rstd_done = k.sem(f"{name}_rstd_done")
        applied = k.sem(f"{name}_applied")
        turned = k.sem(f"{name}_turned")
        stored = k.sem(f"{name}_stored")
        kept = k.sem(f"{name}_kept")
        affine_done = k.sem(f"{name}_affine_done")
        res_ready = k.sem(f"{name}_res_ready")
        res_added = k.sem(f"{name}_res_added")
        FREE = 2
        by_rows = add_to is not None or whole
        by_cols = gain is not None and not by_rows
        ADD_LINKS = 2 * (1 if whole else 3)

        with nc.Block() as block:
            @block.sync
            def _(sp):
                if by_rows:
                    sp.dma_start(rows[:, 0, :], k.a[gain].unsqueeze(0).broadcast_to([P, D])).then_inc(loaded, 16)
                    sp.dma_start(rows[:, 1, :], k.a[bias].unsqueeze(0).broadcast_to([P, D])).then_inc(loaded, 16)
                elif gain:
                    sp.dma_start(cols[:, 0:1], k.a[gain].unsqueeze(1)).then_inc(loaded, 16)
                    if bias:
                        sp.dma_start(cols[:, 1:2], k.a[bias].unsqueeze(1)).then_inc(loaded, 16)

            @block.vector
            def _(v):
                with v.Fori(0, CHUNKS) as i:
                    for t in range(TC):
                        v.bn_stats(stats[:, ds(i * TC + t, 1), :],
                                   src[:, ds((i * TC + t) * D, D)]).then_inc(stats_done, 1)
                v.wait_ge(stats_done, TILES)
                ln = Chain(v, link)
                ln(v.tensor_tensor(mean[:], stats[:, :, 1], stats[:, :, 4], ALU.add))
                ln(v.tensor_scalar(mean[:], mean[:], 0.5, None, ALU.mult))
                ln(v.tensor_tensor(diff[:], stats[:, :, 1], stats[:, :, 4], ALU.subtract))
                ln(v.tensor_tensor(diff[:], diff[:], diff[:], ALU.mult))
                ln(v.tensor_tensor(var[:], stats[:, :, 2], stats[:, :, 5], ALU.add))
                ln(v.tensor_scalar(var[:], var[:], 1.0 / D, None, ALU.mult))
                ln(v.scalar_tensor_tensor(out=var[:], in0=diff[:], scalar=0.25, in1=var[:],
                                          op0=ALU.mult, op1=ALU.add))
                v.tensor_scalar(var2[:], var[:], eps, None, ALU.add).then_inc(var_done, 1)
                v.wait_ge(rstd_done, 1)
                if twice:
                    v.wait_ge(var_done, 1)
                    ln(v.tensor_tensor(diff[:], rstd[:], rstd[:], ALU.mult))
                    ln(v.tensor_tensor(diff[:], diff[:], var[:], ALU.mult))
                    v.tensor_scalar(var2[:], diff[:], EPS, None, ALU.add).then_inc(var_done, 1)
                    v.wait_ge(rstd_done, 2)
                    ln(v.tensor_tensor(total[:], rstd[:], rstd2[:], ALU.mult))
                scale = total if twice else rstd
                if by_rows:
                    v.wait_ge(loaded, 32)
                links = ln.n
                with v.Fori(0, CHUNKS // 2) as i:
                    add = Chain(v, link, links + i * ADD_LINKS, ADD_LINKS)
                    for b in range(2):
                        if add_to is None:
                            v.wait_ge(turned, i * 2 + b + 1)
                        if whole:
                            v.wait_ge(kept, i * 2 + b + 1)
                        for t in range(TC):
                            n = (i * 2 + b) * TC + t
                            v.tensor_scalar(xn[:, b, t, :], src[:, ds(n * D, D)], mean[:, ds(n, 1)],
                                            scale[:, ds(n, 1)], ALU.subtract, ALU.mult).then_inc(applied, 1)
                            if residual:
                                if t == 0:
                                    v.wait_ge(res_added, i * 2 + b + 1)
                                v.tensor_scalar(once[:, b, t, :], src[:, ds(n * D, D)], mean[:, ds(n, 1)],
                                                rstd[:, ds(n, 1)], ALU.subtract, ALU.mult).then_inc(res_ready, 1)
                            if keep is not None and not whole:
                                v.tensor_scalar(keep[:, ds(n * D, D)], src[:, ds(n * D, D)], mean[:, ds(n, 1)],
                                                rstd[:, ds(n, 1)], ALU.subtract, ALU.mult).then_inc(kept, 1)
                        if whole:
                            v.wait_ge(applied, ((i * 2 + b) + 1) * TC)
                            add(v.tensor_tensor(xn[:, b], xn[:, b], bcast(rows[:, 0, :], 1, TC), ALU.mult))
                            v.tensor_tensor(xn[:, b], xn[:, b], bcast(rows[:, 1, :], 1, TC),
                                            ALU.add).then_inc(affine_done, 1)
                        if add_to is not None:
                            v.wait_ge(applied, ((i * 2 + b) + 1) * TC)
                            at = add_to[:, ds((i * 2 + b) * CHUNK, CHUNK)].rearrange("p (t d) -> p t d", t=TC)
                            add(v.tensor_tensor(xn[:, b], xn[:, b], bcast(rows[:, 0, :], 1, TC), ALU.mult))
                            add(v.tensor_tensor(xn[:, b], xn[:, b], bcast(rows[:, 1, :], 1, TC), ALU.add))
                            add(v.tensor_tensor(at, at, xn[:, b], ALU.add))
                    if by_rows:
                        add.done()

            @block.gpsimd
            def _(g):
                g.memset(expo[:], -0.5).then_inc(expo_set, 1)
                g.wait_ge(expo_set, 1)
                g.wait_ge(var_done, 1)
                g.tensor_tensor(rstd[:], var2[:], expo[:], ALU.pow).then_inc(rstd_done, 1)
                if twice:
                    g.wait_ge(var_done, 2)
                    g.tensor_tensor(rstd2[:], var2[:], expo[:], ALU.pow).then_inc(rstd_done, 1)
                if whole:
                    g.sem_inc(kept, FREE)
                    with g.Fori(0, CHUNKS // 2) as i:
                        for b in range(2):
                            g.wait_ge(affine_done, i * 2 + b + 1)
                            g.tensor_copy(keep[:, ds((i * 2 + b) * CHUNK, CHUNK)],
                                          xn[:, b].rearrange("p t d -> p (t d)")).then_inc(kept, 1)
                if residual:
                    g.sem_inc(res_added, FREE)
                    with g.Fori(0, CHUNKS // 2) as i:
                        for b in range(2):
                            g.wait_ge(res_ready, (i * 2 + b + 1) * TC)
                            at = src[:, ds((i * 2 + b) * CHUNK, CHUNK)]
                            g.tensor_tensor(at, at, once[:, b].rearrange("p t d -> p (t d)"),
                                            ALU.add).then_inc(res_added, 1)

            if add_to is None:
                @block.tensor
                def _(pe):
                    pe.sem_inc(turned, FREE)
                    with pe.Fori(0, CHUNKS // 2) as i:
                        for b in range(2):
                            pe.wait_ge(affine_done if whole else applied, (i * 2 + b + 1) * (1 if whole else TC))
                            pe.wait_ge(stored, i * 2 + b + 1)
                            for t in range(TC):
                                mm = pe.transpose(psT[:, b, t * P:(t + 1) * P], xn[:, b, t, :], k.ident[:])
                            mm.then_inc(turned, 1)

                @block.scalar
                def _(act):
                    act.sem_inc(stored, FREE)
                    if by_cols:
                        act.wait_ge(loaded, 32 if bias else 16)
                    with act.Fori(0, CHUNKS // 2) as i:
                        for b in range(2):
                            act.wait_ge(turned, i * 2 + b + 1 + FREE)
                            act.activation(k.XT[:, ds((i * 2 + b) * CHUNK, CHUNK)], psT[:, b, :], ACT.Identity,
                                           scale=cols[:, 0:1] if by_cols else 1.0,
                                           bias=cols[:, 1:2] if by_cols and bias else 0.0).then_inc(stored, 1)



def route(v, ln, logits, tri, gt, eq, rank, mask, top, experts):
    other = bcast(logits, 2, experts)
    own = bcast(logits, 3, experts)
    ln(v.tensor_tensor(gt, other, own, ALU.is_gt))
    ln(v.tensor_tensor(eq, other, own, ALU.is_equal))
    ln(v.tensor_tensor(eq, eq, bcast(tri, 1, TC), ALU.mult))
    ln(v.tensor_tensor(gt, gt, eq, ALU.add))
    ln(v.tensor_reduce(rank, gt, AX, ALU.add))
    ln(v.tensor_scalar(mask, rank, float(top), None, ALU.is_lt))


def mixture(k, name, E, UT, dest, kind, wr, br, wu, bu, wd, bd):
    nc = k.nc
    ctx = Stage(k)
    top = 4 if kind == "swiglu4" else 2
    N = E * UT
    BANKS = 4
    SLOTS = 8
    HELD = SLOTS // UT
    LAG = 1 if UT == 4 else 2
    YB = 2
    LINKS = {"gelu2": 12, "swiglu4": 13, "assign": 15}[kind]
    with ctx:
        sb, ps = buffers(nc, ctx)
        w_up = sb(f"{name}_w_up", [P, N, P])
        w_down = sb(f"{name}_w_down", [P, N, D])
        w_rt = sb(f"{name}_w_rt", [P, E])
        b_up = sb(f"{name}_b_up", [P, N])
        b_down = sb(f"{name}_b_down", [E, D])
        b_rt = sb(f"{name}_b_rt", [P, E])
        tri = sb(f"{name}_tri", [P, E, E])
        index = sb(f"{name}_index", [P, E])
        xs = sb(f"{name}_xs", [P, 2, CHUNK])
        hT = sb(f"{name}_hT", [P, SLOTS, CHUNK])
        clamped = sb(f"{name}_clamped", [P, 2, CHUNK])
        sig = sb(f"{name}_sig", [P, 2, CHUNK])
        lg = sb(f"{name}_lg", [P, TC, E])
        pr = sb(f"{name}_pr", [P, TC, E])
        gt = sb(f"{name}_gt", [P, TC, E, E])
        eq = sb(f"{name}_eq", [P, TC, E, E])
        rank = sb(f"{name}_rank", [P, TC, E])
        mask = sb(f"{name}_mask", [P, TC, E])
        mx = sb(f"{name}_mx", [P, TC])
        tot = sb(f"{name}_tot", [P, TC])
        wt = sb(f"{name}_wt", [P, 2, TC, E])
        wt8 = sb(f"{name}_wt8", [P, 2, TC, E])
        wtT = sb(f"{name}_wtT", [E, CHUNK])
        psH = ps(f"{name}_psH", [P, BANKS, CHUNK])
        psY = ps(f"{name}_psY", [P, YB, CHUNK])
        psR = ps(f"{name}_psR", [P, CHUNK])
        psB = ps(f"{name}_psB", [P, CHUNK])

        loaded = k.sem(f"{name}_loaded")
        xs_ready = k.sem(f"{name}_xs_ready")
        logits_ready = k.sem(f"{name}_logits_ready")
        shifted = k.sem(f"{name}_shifted")
        exp_done = k.sem(f"{name}_exp_done")
        weights_ready = k.sem(f"{name}_weights_ready")
        weights_turned = k.sem(f"{name}_weights_turned")
        weightsT_ready = k.sem(f"{name}_weightsT_ready")
        bias_summed = k.sem(f"{name}_bias_summed")
        bias_added = k.sem(f"{name}_bias_added")
        up_done = k.sem(f"{name}_up_done")
        clamp_done = k.sem(f"{name}_clamp_done")
        sigmoid_done = k.sem(f"{name}_sigmoid_done")
        act_done = k.sem(f"{name}_act_done")
        down_done = k.sem(f"{name}_down_done")
        mixed = k.sem(f"{name}_mixed")
        link = k.sem(f"{name}_link")
        LOADS = 7 + (br is not None)
        swiglu = kind == "swiglu4"
        ACT_FREE = 2 if swiglu else BANKS

        with nc.Block() as block:
            @block.sync
            def _(sp):
                sp.dma_start(w_rt[:], k.a[wr]).then_inc(loaded, 16)
                sp.dma_start(tri[:], k.a[f"tri{E}"].partition_broadcast(P)).then_inc(loaded, 16)
                sp.dma_start(index[:], k.a[f"index{E}"].partition_broadcast(P)).then_inc(loaded, 16)
                sp.dma_start(b_up[:], k.a[bu]).then_inc(loaded, 16)
                sp.dma_start(b_down[:], k.a[bd]).then_inc(loaded, 16)
                if br:
                    sp.dma_start(b_rt[:], k.a[br].partition_broadcast(P)).then_inc(loaded, 16)
                sp.dma_start(w_up[:], k.a[wu]).then_inc(loaded, 16)
                sp.dma_start(w_down[:], k.a[wd]).then_inc(loaded, 16)

            @block.gpsimd
            def _(g):
                if swiglu:
                    g.sem_inc(act_done, ACT_FREE)
                with g.Fori(0, CHUNKS // 2) as i:
                    for b in range(2):
                        c = i * 2 + b
                        g.wait_ge(logits_ready, c)
                        g.tensor_copy(xs[:, b, :], k.XT[:, ds(c * CHUNK, CHUNK)]).then_inc(xs_ready, 1)
                        for n in range(N if swiglu else 0):
                            g.wait_ge(sigmoid_done, c * N + n + 1)
                            g.wait_ge(down_done, c * E + n // UT + 1)
                            g.tensor_tensor(hT[:, n % SLOTS, :], clamped[:, n % 2, :], sig[:, n % 2, :],
                                            ALU.mult).then_inc(act_done, 1)

            @block.tensor
            def _(pe):
                pe.sem_inc(down_done, HELD)
                pe.wait_ge(loaded, LOADS * 16)
                with pe.Fori(0, CHUNKS // 2) as i:
                    for b in range(2):
                        c = i * 2 + b
                        pe.wait_ge(xs_ready, c + 1)
                        for t in range(TC):
                            mm = pe.matmul(psR[:, t * E:(t + 1) * E], xs[:, b, t * P:(t + 1) * P], w_rt[:],
                                           start=True, stop=True)
                        mm.then_inc(logits_ready, 1)

                        def up(e):
                            for u in range(UT):
                                n = e * UT + u
                                pe.wait_ge(clamp_done if swiglu else act_done, c * N + n + 1)
                                pe.matmul(psH[:, n % BANKS, :], w_up[:, n, :], xs[:, b, :],
                                          start=True, stop=True).then_inc(up_done, 1)

                        def down(e):
                            pe.wait_ge(act_done, c * N + (e + 1) * UT + ACT_FREE)
                            pe.wait_ge(mixed, c * E + e + 1)
                            for t in range(TC):
                                for u in range(UT):
                                    n = e * UT + u
                                    mm = pe.matmul(psY[:, e % YB, t * P:(t + 1) * P],
                                                   hT[:, n % SLOTS, t * P:(t + 1) * P], w_down[:, n, :],
                                                   start=(u == 0), stop=(u == UT - 1))
                            mm.then_inc(down_done, 1)

                        for e in range(E + LAG):
                            if e < E:
                                up(e)
                            if e >= LAG:
                                down(e - LAG)
                            if e == LAG + 1:
                                pe.wait_ge(weights_ready, c + 1)
                                for t in range(TC):
                                    mm = pe.transpose(psR[0:E, t * P:(t + 1) * P], wt[:, b, t, :], k.ident[:])
                                mm.then_inc(weights_turned, 1)
                            if e == LAG + 2:
                                pe.wait_ge(weightsT_ready, c + 1)
                                for t in range(TC):
                                    mm = pe.matmul(psB[:, t * P:(t + 1) * P], wtT[:, t * P:(t + 1) * P],
                                                   b_down[:], start=True, stop=True)
                                mm.then_inc(bias_summed, 1)

            @block.scalar
            def _(act):
                if not swiglu:
                    act.sem_inc(act_done, ACT_FREE)
                act.wait_ge(loaded, LOADS * 16)
                with act.Fori(0, CHUNKS // 2) as i:
                    for b in range(2):
                        c = i * 2 + b
                        act.wait_ge(shifted, c + 1)
                        act.activation(pr[:], lg[:], ACT.Exp).then_inc(exp_done, 1)
                        for n in range(N):
                            if swiglu:
                                act.wait_ge(clamp_done, c * N + n + 1 + BANKS)
                                act.wait_ge(act_done, c * N + n + 1)
                                act.activation(sig[:, n % 2, :], clamped[:, n % 2, :], ACT.Sigmoid,
                                               scale=1.702).then_inc(sigmoid_done, 1)
                            else:
                                act.wait_ge(up_done, c * N + n + 1)
                                act.wait_ge(down_done, c * E + n // UT + 1)
                                act.activation(hT[:, n % SLOTS, :], psH[:, n % BANKS, :], ACT.Gelu,
                                               bias=b_up[:, n:n + 1]).then_inc(act_done, 1)

            @block.vector
            def _(v):
                v.sem_inc(mixed, YB)
                if swiglu:
                    v.sem_inc(clamp_done, BANKS)
                v.wait_ge(loaded, LOADS * 16)
                with v.Fori(0, CHUNKS // 2) as i:
                    for b in range(2):
                        c = i * 2 + b
                        ln = Chain(v, link, c * LINKS, LINKS)
                        v.wait_ge(logits_ready, c + 1)
                        rt = psR[:, 0:TC * E].rearrange("p (t e) -> p t e", t=TC)
                        if br:
                            ln(v.tensor_tensor(lg[:], rt, bcast(b_rt[:], 1, TC), ALU.add))
                        else:
                            ln(v.tensor_copy(lg[:], rt))
                        if kind != "assign":
                            route(v, ln, lg[:], tri[:], gt[:], eq[:], rank[:], mask[:], top, E)
                        ln(v.tensor_reduce(mx[:], lg[:], AX, ALU.max))
                        v.tensor_tensor(lg[:], lg[:], bcast(mx[:], 2, E), ALU.subtract).then_inc(shifted, 1)
                        v.wait_ge(exp_done, c + 1)
                        if kind != "assign":
                            ln(v.tensor_tensor(pr[:], pr[:], mask[:], ALU.mult))
                        else:
                            ln(v.scalar_tensor_tensor(out=pr[:], in0=lg[:], scalar=LOG_TINY, in1=pr[:],
                                                      op0=ALU.is_ge, op1=ALU.mult))
                        ln(v.tensor_reduce(tot[:], pr[:], AX, ALU.add))
                        ln(v.reciprocal(tot[:], tot[:]))
                        if kind == "assign":
                            ln(v.tensor_tensor(pr[:], pr[:], bcast(tot[:], 2, E), ALU.mult))
                            route(v, ln, pr[:], tri[:], gt[:], eq[:], rank[:], mask[:], top, E)
                            ln(v.tensor_tensor(rank[:], mask[:], bcast(index[:], 1, TC), ALU.mult))
                            ln(v.tensor_reduce(mx[:], rank[:], AX, ALU.max))
                            ln(v.tensor_tensor(wt[:, b], bcast(index[:], 1, TC), bcast(mx[:], 2, E), ALU.is_equal))
                        else:
                            ln(v.tensor_tensor(wt[:, b], pr[:], bcast(tot[:], 2, E), ALU.mult))
                        if swiglu:
                            ln(v.tensor_scalar(wt8[:, b], wt[:, b], 8.0, None, ALU.mult))
                        v.tensor_copy(rank[:], wt[:, b]).then_inc(weights_ready, 1)
                        v.wait_ge(weights_ready, c + 1)
                        ln.done()
                        by = wt8 if swiglu else wt

                        def clamp(n):
                            v.wait_ge(up_done, c * N + n + 1)
                            v.wait_ge(act_done, c * N + n + 1)
                            v.tensor_scalar(clamped[:, n % 2, :], psH[:, n % BANKS, :], b_up[:, n:n + 1], 7.0,
                                            ALU.add, ALU.min).then_inc(clamp_done, 1)

                        for e in range(E + LAG):
                            if swiglu and e < E:
                                clamp(e)
                            if e < LAG:
                                continue
                            e -= LAG
                            v.wait_ge(down_done, c * E + e + 1 + HELD)
                            for t in range(TC):
                                at = dest[:, ds(c * CHUNK + t * P, P)]
                                mix = v.scalar_tensor_tensor(
                                    out=at, in0=psY[:, e % YB, t * P:(t + 1) * P],
                                    scalar=by[:, b, t, e:e + 1], in1=at, op0=ALU.mult, op1=ALU.add)
                            mix.then_inc(mixed, 1)
                            v.wait_ge(mixed, c * E + e + 1 + YB)
                            if e == 1:
                                v.wait_ge(weights_turned, c + 1)
                                v.tensor_copy(wtT[:], psR[0:E, :]).then_inc(weightsT_ready, 1)
                            if e == 3:
                                v.wait_ge(bias_summed, c + 1)
                                at = dest[:, ds(c * CHUNK, CHUNK)]
                                v.tensor_tensor(at, psB[:], at, ALU.add).then_inc(bias_added, 1)
                                v.wait_ge(bias_added, c + 1)



def depool(k):
    nc = k.nc
    ctx = Stage(k)
    with ctx:
        sb, ps = buffers(nc, ctx)
        lens_i = sb("dp_lens_i", [P, KEYS], I32)
        lens = sb("dp_lens", [P, KEYS])
        ones = sb("dp_ones", [P, KEYS])
        sums = sb("dp_sums", [P, KEYS])
        wrap = sb("dp_wrap", [P, KEYS])
        hits = sb("dp_hits", [P, S, KEYS])
        pos = sb("dp_pos", [P, S])
        slot = sb("dp_slot", [P, 1])
        part = sb("dp_part", [P, 1])
        bound = sb("dp_bound", [P, S])
        count = sb("dp_count", [P, S])
        plug = sb("dp_plug", [P, S])
        plug_all = sb("dp_plug_all", [P, TOK])
        onehot = sb("dp_onehot", [P, TOK])
        patch = sb("dp_patch", [P, TILES, C])
        square = sb("dp_square", [P, 2, C])
        sumsq = sb("dp_sumsq", [P, TILES])
        expo = sb("dp_expo", [P, TILES])
        rms = sb("dp_rms", [P, TILES])
        hp = sb("dp_hp", [P, TILES * D])
        decay = sb("dp_decay", [P, P])
        mix = sb("dp_mix", [P, 2, CHUNK])
        psG = ps("dp_psG", [P, 2, CHUNK])
        psD = ps("dp_psD", [P, 2, CHUNK])

        loaded = k.sem("dp_loaded")
        patch_loaded = k.sem("dp_patch_loaded")
        ones_set = k.sem("dp_ones_set")
        link = k.sem("dp_link")
        plug_ready = k.sem("dp_plug_ready")
        plug_stored = k.sem("dp_plug_stored")
        plug_spread = k.sem("dp_plug_spread")
        onehot_ready = k.sem("dp_onehot_ready")
        squared = k.sem("dp_squared")
        meansq_ready = k.sem("dp_meansq_ready")
        rms_ready = k.sem("dp_rms_ready")
        hp_ready = k.sem("dp_hp_ready")
        mixed = k.sem("dp_mixed")
        mix_copied = k.sem("dp_mix_copied")
        picked = k.sem("dp_picked")
        stored = k.sem("dp_stored")
        scratch = nc.dram_tensor("dp_plug_dram", (B, S), F32).ap()
        FREE = 2

        with nc.Block() as block:
            @block.sync
            def _(sp):
                sp.dma_start(lens_i[:], k.a["mask_BxS2_if0"]).then_inc(loaded, 16)
                sp.dma_start(pos[:], k.a["pos"].partition_broadcast(P)).then_inc(loaded, 16)
                sp.dma_start(slot[:], k.a["slot"]).then_inc(loaded, 16)
                sp.dma_start(part[:], k.a["part"]).then_inc(loaded, 16)
                sp.dma_start(decay[:], k.a["decay"]).then_inc(loaded, 16)
                for q in range(BT):
                    sp.dma_start(patch[q * S:(q + 1) * S],
                                 k.a["ctx"][q:B:BT, 0:S, :].rearrange("t p c -> p t c")).then_inc(patch_loaded, 16)
                sp.wait_ge(plug_ready, 1)
                sp.dma_start(scratch, plug[:]).then_inc(plug_stored, 16)
                sp.wait_ge(plug_stored, 16)
                sp.dma_start(plug_all[:], scratch.rearrange("b l -> (b l)").partition_broadcast(P))\
                    .then_inc(plug_spread, 16)

            @block.gpsimd
            def _(g):
                g.memset(ones[:], 1.0).then_inc(ones_set, 1)
                g.memset(expo[:], -0.5).then_inc(ones_set, 1)
                g.wait_ge(ones_set, 2)
                g.wait_ge(meansq_ready, 1)
                g.tensor_tensor(rms[:], sumsq[:], expo[:], ALU.pow).then_inc(rms_ready, 1)

            @block.scalar
            def _(act):
                act.wait_ge(patch_loaded, 16 * BT)
                for t in range(TILES):
                    if t >= 2:
                        act.wait_ge(squared, t - 1)
                    act.activation(square[:, t % 2], patch[:, t], ACT.Square,
                                   accum_out=sumsq[:, t:t + 1]).then_inc(squared, 1)
                act.sem_inc(mix_copied, FREE)
                act.sem_inc(stored, FREE)
                with act.Fori(0, CHUNKS // 2) as i:
                    for b in range(2):
                        c = i * 2 + b
                        act.wait_ge(mixed, c + 1)
                        act.wait_ge(picked, c + 1)
                        act.activation(mix[:, b], psG[:, b], ACT.Copy).then_inc(mix_copied, 1)
                        act.wait_ge(picked, c + 1 + FREE)
                        act.activation(k.DR[:, ds(c * CHUNK, CHUNK)], psD[:, b], ACT.Copy).then_inc(stored, 1)

            @block.vector
            def _(v):
                ln = Chain(v, link)
                v.wait_ge(loaded, 16 * 5)
                v.wait_ge(ones_set, 2)
                ln(v.tensor_copy(lens[:], lens_i[:]))
                ln(v.tensor_tensor_scan(sums[:], ones[:], lens[:], 0.0, ALU.mult, ALU.add))
                ln(v.tensor_scalar(sums[:], sums[:], 1.0, None, ALU.subtract))
                ln(v.tensor_scalar(wrap[:], sums[:], 0.0, float(S), ALU.is_lt, ALU.mult))
                ln(v.tensor_tensor(sums[:], sums[:], wrap[:], ALU.add))
                ln(v.tensor_tensor(hits[:], bcast(sums[:], 1, S), bcast(pos[:], 2, KEYS), ALU.is_equal))
                ln(v.tensor_reduce(bound[:], hits[:], AX, ALU.max))
                ln(v.tensor_tensor_scan(count[:], ones[:, 0:S], bound[:], 0.0, ALU.mult, ALU.add))
                ln(v.tensor_scalar(count[:], count[:], 1.0, 0.0, ALU.subtract, ALU.max))
                v.tensor_scalar(plug[:], count[:], slot[:, 0:1], None, ALU.add).then_inc(plug_ready, 1)
                v.wait_ge(squared, TILES)
                v.tensor_scalar(sumsq[:], sumsq[:], 1.0 / C, EPS, ALU.mult, ALU.add).then_inc(meansq_ready, 1)
                v.wait_ge(rms_ready, 1)
                ln(v.tensor_scalar(rms[:], rms[:], PATCH_GAIN, None, ALU.mult))
                for t in range(TILES):
                    v.tensor_scalar(hp[:, t * D:(t + 1) * D], patch[:, t, 0:D], rms[:, t:t + 1], None,
                                    ALU.mult).then_inc(hp_ready, 1)
                v.wait_ge(plug_spread, 16)
                v.tensor_scalar(onehot[:], plug_all[:], part[:, 0:1], None, ALU.is_equal).then_inc(onehot_ready, 1)

            @block.tensor
            def _(pe):
                pe.wait_ge(onehot_ready, 1)
                pe.wait_ge(hp_ready, TILES)
                pe.sem_inc(picked, FREE)
                with pe.Fori(0, CHUNKS // 2) as i:
                    for b in range(2):
                        c = i * 2 + b
                        pe.wait_ge(mix_copied, c + 1)
                        pe.matmul(psG[:, b], decay[:], onehot[:, ds(c * CHUNK, CHUNK)],
                                  start=True, stop=True).then_inc(mixed, 1)
                        pe.wait_ge(mix_copied, c + 1 + FREE)
                        pe.wait_ge(stored, c + 1)
                        for t in range(TC):
                            mm = pe.matmul(psD[:, b, t * P:(t + 1) * P], mix[:, b, t * P:(t + 1) * P],
                                           hp[:, ds(c * CHUNK + t * P, P)], start=True, stop=True)
                        mm.then_inc(picked, 1)


def depooled(k, name, prefix):
    nc = k.nc
    normalise(k, f"{name}n", k.X, gain=f"{prefix}_g_res", twice=True)
    ctx = Stage(k)
    with ctx:
        sb, ps = buffers(nc, ctx)
        w = sb(f"{name}_w", [P, D])
        b_row = sb(f"{name}_b_row", [P, D])
        g_row = sb(f"{name}_g_row", [P, D])
        xs = sb(f"{name}_xs", [P, 2, CHUNK])
        patch = sb(f"{name}_patch", [P, 2, TC, D])
        psP = ps(f"{name}_psP", [P, 2, CHUNK])
        loaded = k.sem(f"{name}_loaded")
        xs_ready = k.sem(f"{name}_xs_ready")
        projected = k.sem(f"{name}_projected")
        scaled = k.sem(f"{name}_scaled")
        patch_ready = k.sem(f"{name}_patch_ready")
        summed = k.sem(f"{name}_summed")
        added = k.sem(f"{name}_added")
        FREE = 2
        with nc.Block() as block:
            @block.sync
            def _(sp):
                sp.dma_start(w[:], k.a[f"{prefix}_wT"]).then_inc(loaded, 16)
                sp.dma_start(b_row[:], k.a[f"{prefix}_b_in"].partition_broadcast(P)).then_inc(loaded, 16)
                sp.dma_start(g_row[:], k.a[f"{prefix}_g_init"][0:D].partition_broadcast(P)).then_inc(loaded, 16)

            @block.scalar
            def _(act):
                act.sem_inc(xs_ready, FREE)
                with act.Fori(0, CHUNKS // 2) as i:
                    for b in range(2):
                        c = i * 2 + b
                        act.wait_ge(projected, c + 1)
                        act.activation(xs[:, b, :], k.XT[:, ds(c * CHUNK, CHUNK)], ACT.Copy).then_inc(xs_ready, 1)

            @block.tensor
            def _(pe):
                pe.sem_inc(projected, FREE)
                pe.wait_ge(loaded, 48)
                with pe.Fori(0, CHUNKS // 2) as i:
                    for b in range(2):
                        c = i * 2 + b
                        pe.wait_ge(xs_ready, c + 1 + FREE)
                        pe.wait_ge(added, c + 1)
                        for t in range(TC):
                            mm = pe.matmul(psP[:, b, t * P:(t + 1) * P], xs[:, b, t * P:(t + 1) * P], w[:],
                                           start=True, stop=True)
                        mm.then_inc(projected, 1)

            @block.gpsimd
            def _(g):
                g.wait_ge(loaded, 48)
                with g.Fori(0, CHUNKS // 2) as i:
                    for b in range(2):
                        c = i * 2 + b
                        g.wait_ge(added, c + 1)
                        at = k.DR[:, ds(c * CHUNK, CHUNK)].rearrange("p (t d) -> p t d", t=TC)
                        g.tensor_tensor(patch[:, b], at, bcast(g_row[:], 1, TC), ALU.mult).then_inc(scaled, 1)
                        g.wait_ge(scaled, c + 1)
                        g.tensor_tensor(patch[:, b], patch[:, b], bcast(b_row[:], 1, TC),
                                        ALU.add).then_inc(patch_ready, 1)

            @block.vector
            def _(v):
                v.sem_inc(added, FREE)
                with v.Fori(0, CHUNKS // 2) as i:
                    for b in range(2):
                        c = i * 2 + b
                        v.wait_ge(patch_ready, c + 1)
                        v.wait_ge(projected, c + 1 + FREE)
                        rows = patch[:, b].rearrange("p t d -> p (t d)")
                        v.tensor_tensor(rows, rows, psP[:, b], ALU.add).then_inc(summed, 1)
                        v.wait_ge(summed, c + 1)
                        at = k.X[:, ds(c * CHUNK, CHUNK)]
                        v.tensor_tensor(at, at, rows, ALU.add).then_inc(added, 1)



def layer1_attn(k):
    nc = k.nc
    normalise(k, "n1a", k.X)
    ctx = Stage(k)
    NS = 16
    LINKS = 10
    with ctx:
        sb, ps = buffers(nc, ctx)
        w_in = sb("m_w_in", [P, 4, P])
        w_conv = sb("m_w_conv", [P, 2, 4])
        b_conv = sb("m_b_conv", [P, 2])
        d_skip = sb("m_d_skip", [P, 2])
        w_dbc = sb("m_w_dbc", [P, 2, 4, NS])
        b_delta = sb("m_b_delta", [NS, 1])
        a_log = sb("m_a_log", [NS, 1])
        a_neg = sb("m_a_neg", [NS, 1])
        w_out = sb("m_w_out", [P, 2, D])
        ones = sb("m_ones", [NS, P])
        conv = sb("m_conv", [P, 2, CHUNK])
        xconv = sb("m_xconv", [P, 2, CHUNK])
        gate = sb("m_gate", [P, 2, CHUNK])
        gated = sb("m_gated", [P, 2, CHUNK])
        z = sb("m_z", [NS, CHUNK])
        absz = sb("m_absz", [NS, CHUNK])
        soft = sb("m_soft", [NS, CHUNK])
        delta = sb("m_delta", [NS, CHUNK])
        dA = sb("m_dA", [NS, CHUNK])
        dB = sb("m_dB", [NS, CHUNK])
        hs = sb("m_hs", [NS, CHUNK])
        hc = sb("m_hc", [NS, CHUNK])
        psI = ps("m_psI", [P, 4, CHUNK])
        psS = ps("m_psS", [P, 4, CHUNK])

        loaded = k.sem("m_loaded")
        ones_set = k.sem("m_ones_set")
        a_ready = k.sem("m_a_ready")
        projected = k.sem("m_projected")
        conv_started = k.sem("m_conv_started")
        conv_done = k.sem("m_conv_done")
        silu_done = k.sem("m_silu_done")
        states_in = k.sem("m_states_in")
        z_ready = k.sem("m_z_ready")
        abs_done = k.sem("m_abs_done")
        exp_done = k.sem("m_exp_done")
        log_done = k.sem("m_log_done")
        delta_ready = k.sem("m_delta_ready")
        decay_ready = k.sem("m_decay_ready")
        read_out = k.sem("m_read_out")
        spread = k.sem("m_spread")
        gated_ready = k.sem("m_gated_ready")
        out_done = k.sem("m_out_done")
        added = k.sem("m_added")
        link = k.sem("m_link")

        with nc.Block() as block:
            @block.sync
            def _(sp):
                for to, name in ((w_in, "L1_attn_w_in"), (w_conv, "L1_attn_w_conv"), (b_conv, "L1_attn_b_conv"),
                                 (d_skip, "L1_attn_d_skip"), (w_dbc, "L1_attn_w_dbc"), (w_out, "L1_attn_w_out")):
                    sp.dma_start(to[:], k.a[name]).then_inc(loaded, 16)
                sp.dma_start(b_delta[:], k.a["L1_attn_delta_b"].unsqueeze(1)).then_inc(loaded, 16)
                sp.dma_start(a_log[:], k.a["L1_attn_A_log"].unsqueeze(1)).then_inc(loaded, 16)

            @block.gpsimd
            def _(g):
                g.memset(ones[:], 1.0).then_inc(ones_set, 1)

            @block.tensor
            def _(pe):
                pe.wait_ge(loaded, 128)
                pe.wait_ge(ones_set, 1)
                with pe.Fori(0, CHUNKS) as i:
                    pe.wait_ge(added, i)
                    for f in range(4):
                        pe.matmul(psI[:, f], w_in[:, f], k.XT[:, ds(i * CHUNK, CHUNK)],
                                  start=True, stop=True).then_inc(projected, 1)
                    pe.wait_ge(silu_done, i * 4 + 4)
                    for g in range(4):
                        for f in range(2):
                            mm = pe.matmul(psS[0:NS, g], w_dbc[:, f, g], xconv[:, f], start=(f == 0), stop=(f == 1))
                    mm.then_inc(states_in, 1)
                    pe.wait_ge(read_out, i + 1)
                    pe.matmul(psI[:, 0], ones[:], hc[:], start=True, stop=True).then_inc(spread, 1)
                    pe.wait_ge(gated_ready, (i + 1) * 2)
                    for t in range(TC):
                        for f in range(2):
                            mm = pe.matmul(psI[:, 1, t * P:(t + 1) * P], gated[:, f, t * P:(t + 1) * P], w_out[:, f],
                                           start=(f == 0), stop=(f == 1))
                    mm.then_inc(out_done, 1)

            @block.scalar
            def _(act):
                act.wait_ge(loaded, 128)
                act.activation(a_neg[:], a_log[:], ACT.Exp).then_inc(a_ready, 1)
                act.wait_ge(a_ready, 2)
                with act.Fori(0, CHUNKS) as i:
                    for f in range(2):
                        act.wait_ge(projected, i * 4 + f + 1)
                        act.activation(conv[:, f], psI[:, f], ACT.Identity, scale=w_conv[:, f, 3:4],
                                       bias=b_conv[:, f:f + 1]).then_inc(conv_started, 1)
                    for f in range(2):
                        act.wait_ge(projected, i * 4 + f + 3)
                        act.activation(gate[:, f], psI[:, 2 + f], ACT.Silu).then_inc(silu_done, 1)
                    for f in range(2):
                        act.wait_ge(conv_done, i * 2 + f + 1)
                        act.activation(xconv[:, f], conv[:, f], ACT.Silu).then_inc(silu_done, 1)
                    act.wait_ge(z_ready, i + 1)
                    act.activation(absz[:], z[:], ACT.Abs).then_inc(abs_done, 1)
                    act.wait_ge(abs_done, i + 1)
                    act.activation(soft[:], absz[:], ACT.Exp, scale=-1.0).then_inc(exp_done, 1)
                    act.wait_ge(exp_done, i + 1)
                    act.activation(soft[:], soft[:], ACT.Ln, bias=1.0).then_inc(log_done, 1)
                    act.wait_ge(delta_ready, i + 1)
                    act.activation(dA[:], delta[:], ACT.Exp, scale=a_neg[:]).then_inc(decay_ready, 1)

            @block.vector
            def _(v):
                v.wait_ge(a_ready, 1)
                v.tensor_scalar(a_neg[:], a_neg[:], -1.0, None, ALU.mult).then_inc(a_ready, 1)
                with v.Fori(0, CHUNKS) as i:
                    ln = Chain(v, link, i * LINKS, LINKS)
                    for f in range(2):
                        v.wait_ge(conv_started, i * 2 + f + 1)
                        to = conv[:, f].rearrange("p (b l) -> p b l", l=S)
                        frm = psI[:, f].rearrange("p (b l) -> p b l", l=S)
                        for back in range(1, 4):
                            tap = v.scalar_tensor_tensor(
                                out=to[:, :, back:S], in0=frm[:, :, 0:S - back], scalar=w_conv[:, f, 3 - back:4 - back],
                                in1=to[:, :, back:S], op0=ALU.mult, op1=ALU.add)
                            if back < 3:
                                ln(tap)
                            else:
                                tap.then_inc(conv_done, 1)
                    v.wait_ge(states_in, i + 1)
                    v.tensor_scalar(z[:], psS[0:NS, 0], b_delta[:], None, ALU.add).then_inc(z_ready, 1)
                    v.wait_ge(log_done, i + 1)
                    v.scalar_tensor_tensor(out=delta[:], in0=z[:], scalar=0.0, in1=soft[:],
                                           op0=ALU.max, op1=ALU.add).then_inc(delta_ready, 1)
                    v.wait_ge(delta_ready, i + 1)
                    ln(v.tensor_tensor(dB[:], delta[:], psS[0:NS, 1], ALU.mult))
                    ln(v.tensor_tensor(dB[:], dB[:], psS[0:NS, 3], ALU.mult))
                    v.wait_ge(decay_ready, i + 1)
                    ln(v.memset(dA[:].rearrange("p (b l) -> p b l", l=S)[:, :, 0:1], 0.0))
                    ln(v.tensor_tensor_scan(hs[:], dA[:], dB[:], 0.0, ALU.mult, ALU.add))
                    v.tensor_tensor(hc[:], hs[:], psS[0:NS, 2], ALU.mult).then_inc(read_out, 1)
                    v.wait_ge(silu_done, (i + 1) * 4)
                    v.wait_ge(spread, i + 1)
                    for f in range(2):
                        ln(v.tensor_tensor(gated[:, f], gate[:, f], psI[:, 0], ALU.mult))
                        v.scalar_tensor_tensor(out=gated[:, f], in0=xconv[:, f], scalar=d_skip[:, f:f + 1],
                                               in1=gated[:, f], op0=ALU.mult, op1=ALU.add).then_inc(gated_ready, 1)
                    v.wait_ge(out_done, i + 1)
                    at = k.X[:, ds(i * CHUNK, CHUNK)]
                    v.tensor_tensor(at, at, psI[:, 1], ALU.add).then_inc(added, 1)
                    ln.done()



def network(k, name, wu, bu, wd, bd=None, wg=None, ternary=False):
    nc = k.nc
    N = 4
    ctx = Stage(k)
    with ctx:
        sb, ps = buffers(nc, ctx)
        w_up = sb(f"{name}_w_up", [P, N, P])
        w_down = sb(f"{name}_w_down", [P, N, D])
        w_gate = sb(f"{name}_w_gate", [P, D])
        b_up = sb(f"{name}_b_up", [P, N])
        b_row = sb(f"{name}_b_row", [P, D])
        low = sb(f"{name}_low", [P, N * D])
        rowsum = sb(f"{name}_rowsum", [P, 2])
        unit = sb(f"{name}_unit", [P, 2])
        mean = sb(f"{name}_mean", [P, P])
        xs = sb(f"{name}_xs", [P, 2, CHUNK])
        relu = sb(f"{name}_relu", [P, N, CHUNK])
        hT = sb(f"{name}_hT", [P, 2, N, CHUNK])
        gate = sb(f"{name}_gate", [P, 2, CHUNK])
        psH = ps(f"{name}_psH", [P, N, CHUNK])
        psY = ps(f"{name}_psY", [P, 2, CHUNK])
        psG = ps(f"{name}_psG", [P, 2, CHUNK])
        loaded = k.sem(f"{name}_loaded")
        mean_set = k.sem(f"{name}_mean_set")
        sums_ready = k.sem(f"{name}_sums_ready")
        sums_spread = k.sem(f"{name}_sums_spread")
        weights_ready = k.sem(f"{name}_weights_ready")
        link = k.sem(f"{name}_link")
        xs_ready = k.sem(f"{name}_xs_ready")
        up_done = k.sem(f"{name}_up_done")
        relu_done = k.sem(f"{name}_relu_done")
        hidden_ready = k.sem(f"{name}_hidden_ready")
        gate_in = k.sem(f"{name}_gate_in")
        gate_ready = k.sem(f"{name}_gate_ready")
        down_done = k.sem(f"{name}_down_done")
        scaled = k.sem(f"{name}_scaled")
        added = k.sem(f"{name}_added")
        FREE = 2
        LOADS = 2 + (bu is not None) + (bd is not None) + (wg is not None)
        gated = wg is not None

        with nc.Block() as block:
            @block.sync
            def _(sp):
                sp.dma_start(w_up[:], k.a[wu]).then_inc(loaded, 16)
                sp.dma_start(w_down[:], k.a[wd]).then_inc(loaded, 16)
                if bu:
                    sp.dma_start(b_up[:], k.a[bu]).then_inc(loaded, 16)
                if bd:
                    sp.dma_start(b_row[:], k.a[bd].partition_broadcast(P)).then_inc(loaded, 16)
                if gated:
                    sp.dma_start(w_gate[:], k.a[wg]).then_inc(loaded, 16)

            @block.gpsimd
            def _(g):
                if ternary:
                    g.memset(mean[:], 1.0 / (N * P * D)).then_inc(mean_set, 1)
                if gated:
                    with g.Fori(0, CHUNKS // 2) as i:
                        for b in range(2):
                            c = i * 2 + b
                            g.wait_ge(down_done, c + 1)
                            for n in range(N):
                                g.wait_ge(relu_done, c * N + n + 1)
                                g.tensor_tensor(hT[:, b, n], relu[:, n], relu[:, n],
                                                ALU.mult).then_inc(hidden_ready, 1)

            @block.tensor
            def _(pe):
                pe.sem_inc(down_done, FREE)
                pe.wait_ge(loaded, LOADS * 16)
                if ternary:
                    pe.wait_ge(mean_set, 1)
                    pe.wait_ge(sums_ready, 2)
                    pe.matmul(psG[:, 0, 0:2], mean[:], rowsum[:], start=True, stop=True).then_inc(sums_spread, 1)
                    pe.wait_ge(weights_ready, 2)
                with pe.Fori(0, CHUNKS // 2) as i:
                    for b in range(2):
                        c = i * 2 + b
                        pe.wait_ge(xs_ready, c + 1)
                        for n in range(N):
                            pe.wait_ge(relu_done, c * N)
                            pe.matmul(psH[:, n], w_up[:, n], xs[:, b], start=True, stop=True).then_inc(up_done, 1)
                        if gated:
                            pe.wait_ge(gate_ready, c)
                            for t in range(TC):
                                mm = pe.matmul(psG[:, b, t * P:(t + 1) * P], xs[:, b, t * P:(t + 1) * P], w_gate[:],
                                               start=True, stop=True)
                            mm.then_inc(gate_in, 1)
                        pe.wait_ge(hidden_ready if gated else relu_done, (c + 1) * N)
                        pe.wait_ge(added, c + 1)
                        for t in range(TC):
                            for n in range(N):
                                mm = pe.matmul(psY[:, b, t * P:(t + 1) * P], hT[:, b, n, t * P:(t + 1) * P],
                                               w_down[:, n], start=(n == 0), stop=(n == N - 1))
                        mm.then_inc(down_done, 1)

            @block.scalar
            def _(act):
                act.wait_ge(loaded, LOADS * 16)
                with act.Fori(0, CHUNKS // 2) as i:
                    for b in range(2):
                        c = i * 2 + b
                        act.wait_ge(down_done, c + 1)
                        act.activation(xs[:, b], k.XT[:, ds(c * CHUNK, CHUNK)], ACT.Copy).then_inc(xs_ready, 1)
                        for n in range(N):
                            act.wait_ge(up_done, c * N + n + 1)
                            if gated:
                                act.wait_ge(hidden_ready, c * N)
                            act.activation(relu[:, n] if gated else hT[:, b, n], psH[:, n], ACT.Relu,
                                           bias=b_up[:, n:n + 1] if bu else 0.0).then_inc(relu_done, 1)
                        if gated:
                            act.wait_ge(gate_in, c + 1)
                            act.wait_ge(added, c + 1)
                            act.activation(gate[:, b], psG[:, b], ACT.Sigmoid).then_inc(gate_ready, 1)

            @block.vector
            def _(v):
                ln = Chain(v, link)
                if ternary:
                    v.wait_ge(loaded, LOADS * 16)
                    for j, w in enumerate((w_up, w_down)):
                        flat = w[:].rearrange("p n d -> p (n d)")
                        ln(v.tensor_scalar(low[:], flat, -1.0, None, ALU.mult))
                        ln(v.tensor_tensor(low[:], low[:], flat, ALU.max))
                        v.tensor_reduce(rowsum[:, j:j + 1], low[:], AX, ALU.add).then_inc(sums_ready, 1)
                        v.wait_ge(sums_ready, j + 1)
                    v.wait_ge(sums_spread, 1)
                    ln(v.tensor_scalar(unit[:], psG[:, 0, 0:2], EPS, None, ALU.add))
                    ln(v.reciprocal(unit[:], unit[:]))
                    for j, w in enumerate((w_up, w_down)):
                        flat = w[:].rearrange("p n d -> p (n d)")
                        ln(v.tensor_scalar(flat, flat, unit[:, j:j + 1], None, ALU.mult))
                        ln(v.tensor_scalar(low[:], flat, -0.5, None, ALU.is_lt))
                        ln(v.tensor_scalar(flat, flat, 0.5, None, ALU.is_gt))
                        v.tensor_tensor(flat, flat, low[:], ALU.subtract).then_inc(weights_ready, 1)
                        v.wait_ge(weights_ready, j + 1)
                v.sem_inc(added, FREE)
                with v.Fori(0, CHUNKS // 2) as i:
                    for b in range(2):
                        c = i * 2 + b
                        v.wait_ge(down_done, c + 1 + FREE)
                        at = k.X[:, ds(c * CHUNK, CHUNK)]
                        if gated:
                            v.wait_ge(gate_ready, c + 1)
                            v.tensor_tensor(gate[:, b], gate[:, b], psY[:, b], ALU.mult).then_inc(scaled, 1)
                            v.wait_ge(scaled, c + 1)
                            v.tensor_tensor(at, at, gate[:, b], ALU.add).then_inc(added, 1)
                        else:
                            rows = gate[:, b].rearrange("p (t d) -> p t d", t=TC)
                            v.tensor_tensor(rows, psY[:, b].rearrange("p (t d) -> p t d", t=TC),
                                            bcast(b_row[:], 1, TC), ALU.add).then_inc(scaled, 1)
                            v.wait_ge(scaled, c + 1)
                            v.tensor_tensor(at, at, gate[:, b], ALU.add).then_inc(added, 1)


def layer3_ffn(k):
    normalise(k, "n3f", k.X)
    network(k, "f3", "L3_ffn_wu", "L3_ffn_bu", "L3_ffn_wd", bd="L3_ffn_b2", ternary=True)


def layer1_xattn(k):
    depool(k)
    depooled(k, "d1", "L1_xattn")


def layer3_xattn(k):
    depooled(k, "d3", "L3_xattn")



def layer2_attn(k):
    nc = k.nc
    normalise(k, "n2a", k.X, gain="L2_attn_ln1_w", bias="L2_attn_ln1_b", twice=True, keep=k.H)
    ctx = Stage(k)
    LINKS = 13
    WAY = 2 * BC
    with ctx:
        sb, ps = buffers(nc, ctx)
        w_rkv = sb("r_w_rkv", [P, 3, D])
        w_out = sb("r_w_out", [P, D])
        decay = sb("r_decay", [P, 1])
        w_neg = sb("r_w_neg", [P, 1])
        bonus = sb("r_bonus", [P, 1])
        w_step = sb("r_w_step", [P, WAY, S])
        r_sig = sb("r_sig", [P, CHUNK])
        kk = sb("r_kk", [P, WAY, S])
        vv = sb("r_vv", [P, WAY, S])
        uk = sb("r_uk", [P, WAY, S])
        pk = sb("r_pk", [P, WAY, S])
        qq = sb("r_qq", [P, WAY, S])
        e1 = sb("r_e1", [P, WAY, S])
        e2 = sb("r_e2", [P, WAY, S])
        f1 = sb("r_f1", [P, WAY, S])
        f2 = sb("r_f2", [P, WAY, S])
        e2v = sb("r_e2v", [P, WAY, S])
        f2v = sb("r_f2v", [P, WAY, S])
        num = sb("r_num", [P, WAY, S])
        den = sb("r_den", [P, WAY, S])
        both = sb("r_both", [P, BC, S])
        mixed = sb("r_mixed", [P, CHUNK])
        psI = ps("r_psI", [P, 3, CHUNK])
        psO = ps("r_psO", [P, CHUNK])

        loaded = k.sem("r_loaded")
        w_ready = k.sem("r_w_ready")
        projected = k.sem("r_projected")
        inputs_ready = k.sem("r_inputs_ready")
        arguments = k.sem("r_arguments")
        exps = k.sem("r_exps")
        products = k.sem("r_products")
        mix_ready = k.sem("r_mix_ready")
        out_done = k.sem("r_out_done")
        h_added = k.sem("r_h_added")
        x_added = k.sem("r_x_added")
        link = k.sem("r_link")
        flat = "p w l -> p (w l)"

        with nc.Block() as block:
            @block.sync
            def _(sp):
                sp.dma_start(w_rkv[:], k.a["L2_attn_w_rkv"]).then_inc(loaded, 16)
                sp.dma_start(w_out[:], k.a["L2_attn_w_out"]).then_inc(loaded, 16)
                sp.dma_start(decay[:], k.a["L2_attn_decay"].unsqueeze(1)).then_inc(loaded, 16)
                sp.dma_start(bonus[:], k.a["L2_attn_u"].unsqueeze(1)).then_inc(loaded, 16)

            @block.tensor
            def _(pe):
                pe.wait_ge(loaded, 64)
                with pe.Fori(0, CHUNKS) as i:
                    pe.wait_ge(inputs_ready, i * 6)
                    for j in range(3):
                        pe.matmul(psI[:, j], w_rkv[:, j], k.XT[:, ds(i * CHUNK, CHUNK)],
                                  start=True, stop=True).then_inc(projected, 1)
                    pe.wait_ge(mix_ready, i + 1)
                    pe.wait_ge(h_added, i)
                    for t in range(TC):
                        mm = pe.matmul(psO[:, t * P:(t + 1) * P], mixed[:, t * P:(t + 1) * P], w_out[:],
                                       start=True, stop=True)
                    mm.then_inc(out_done, 1)

            @block.scalar
            def _(act):
                act.wait_ge(loaded, 64)
                act.activation(w_neg[:], decay[:], ACT.Exp).then_inc(w_ready, 1)
                act.wait_ge(w_ready, 2 + 2)
                with act.Fori(0, CHUNKS) as i:
                    act.wait_ge(projected, i * 3 + 3)
                    act.wait_ge(mix_ready, i)
                    act.activation(r_sig[:], psI[:, 0], ACT.Sigmoid).then_inc(inputs_ready, 1)
                    for j, to in ((1, kk), (2, vv)):
                        seq = psI[:, j].rearrange("p (b l) -> p b l", l=S)
                        act.activation(to[:, 0:BC], seq, ACT.Copy).then_inc(inputs_ready, 1)
                        act.activation(to[:, BC:WAY], seq[:, :, ::-1], ACT.Copy).then_inc(inputs_ready, 1)
                    act.wait_ge(inputs_ready, i * 6 + 5)
                    act.activation(uk[:], kk[:], ACT.Identity, bias=bonus[:]).then_inc(inputs_ready, 1)
                    act.wait_ge(arguments, i + 1)
                    act.activation(f2[:], f2[:], ACT.Exp).then_inc(exps, 1)
                    act.activation(f1[:, :, 1:S], f1[:, :, 1:S], ACT.Exp, bias=w_neg[:]).then_inc(exps, 1)
                    act.activation(e2[:, :, 1:S], e2[:, :, 1:S], ACT.Exp).then_inc(exps, 1)
                    act.activation(e1[:, :, 1:S], e1[:, :, 1:S], ACT.Exp).then_inc(exps, 1)

            @block.gpsimd
            def _(g):
                with g.Fori(0, CHUNKS) as i:
                    g.wait_ge(exps, i * 4 + 1)
                    g.tensor_tensor(f2v[:], f2[:], vv[:], ALU.mult).then_inc(products, 1)
                    g.wait_ge(exps, i * 4 + 3)
                    g.tensor_tensor(e2v[:, :, 1:S], e2[:, :, 1:S], vv[:, :, 1:S], ALU.mult).then_inc(products, 1)
                    g.wait_ge(h_added, i + 1)
                    at = k.X[:, ds(i * CHUNK, CHUNK)]
                    g.tensor_tensor(at, at, k.H[:, ds(i * CHUNK, CHUNK)], ALU.add).then_inc(x_added, 1)

            @block.vector
            def _(v):
                v.wait_ge(w_ready, 1)
                v.tensor_scalar(w_neg[:], w_neg[:], -1.0, None, ALU.mult).then_inc(w_ready, 1)
                v.wait_ge(w_ready, 2)
                v.tensor_copy(w_step[:].rearrange(flat), w_neg[:].broadcast_to([P, WAY * S])).then_inc(w_ready, 1)
                v.wait_ge(w_ready, 3)
                v.memset(w_step[:, :, 0:1], -1e38).then_inc(w_ready, 1)
                v.wait_ge(w_ready, 4)
                with v.Fori(0, CHUNKS) as i:
                    ln = Chain(v, link, i * LINKS, LINKS)
                    v.wait_ge(inputs_ready, (i + 1) * 6)
                    ln(v.tensor_tensor_scan(pk[:].rearrange(flat), w_step[:].rearrange(flat), kk[:].rearrange(flat),
                                            -1e38, ALU.add, ALU.max))
                    ln(v.tensor_tensor(qq[:, :, 1:S], pk[:, :, 0:S - 1], uk[:, :, 1:S], ALU.max))
                    v.tensor_tensor(f2[:], kk[:], pk[:], ALU.subtract)
                    v.tensor_tensor(f1[:, :, 1:S], pk[:, :, 0:S - 1], pk[:, :, 1:S], ALU.subtract)
                    v.tensor_tensor(e2[:, :, 1:S], uk[:, :, 1:S], qq[:, :, 1:S], ALU.subtract)
                    v.tensor_tensor(e1[:, :, 1:S], pk[:, :, 0:S - 1], qq[:, :, 1:S], ALU.subtract)\
                        .then_inc(arguments, 1)
                    ln(v.memset(f1[:, :, 0:1], 0.0))
                    v.wait_ge(exps, i * 4 + 2)
                    ln(v.tensor_tensor_scan(den[:].rearrange(flat), f1[:].rearrange(flat), f2[:].rearrange(flat),
                                            0.0, ALU.mult, ALU.add))
                    v.wait_ge(products, i * 2 + 1)
                    ln(v.tensor_tensor_scan(num[:].rearrange(flat), f1[:].rearrange(flat), f2v[:].rearrange(flat),
                                            0.0, ALU.mult, ALU.add))
                    v.wait_ge(exps, i * 4 + 4)
                    ln(v.tensor_tensor(f2[:, :, 1:S], e1[:, :, 1:S], den[:, :, 0:S - 1], ALU.mult))
                    ln(v.tensor_tensor(f2[:, :, 1:S], f2[:, :, 1:S], e2[:, :, 1:S], ALU.add))
                    ln(v.tensor_tensor(e1[:, :, 1:S], e1[:, :, 1:S], num[:, :, 0:S - 1], ALU.mult))
                    v.wait_ge(products, i * 2 + 2)
                    ln(v.tensor_tensor(e1[:, :, 1:S], e1[:, :, 1:S], e2v[:, :, 1:S], ALU.add))
                    ln(v.reciprocal(f2[:, :, 1:S], f2[:, :, 1:S]))
                    ln(v.tensor_copy(num[:, :, 0:1], vv[:, :, 0:1]))
                    ln(v.tensor_tensor(num[:, :, 1:S], e1[:, :, 1:S], f2[:, :, 1:S], ALU.mult))
                    ln(v.tensor_tensor(both[:], num[:, 0:BC], num[:, BC:WAY, ::-1], ALU.add))
                    v.scalar_tensor_tensor(out=mixed[:], in0=both[:].rearrange(flat), scalar=0.5, in1=r_sig[:],
                                           op0=ALU.mult, op1=ALU.mult).then_inc(mix_ready, 1)
                    ln.done()
                    v.wait_ge(out_done, i + 1)
                    at = k.H[:, ds(i * CHUNK, CHUNK)]
                    v.tensor_tensor(at, at, psO[:], ALU.add).then_inc(h_added, 1)
    normalise(k, "n2b", k.H, gain="L2_attn_ln2_w", bias="L2_attn_ln2_b")
    network(k, "f2a", "L2_attn_wfk", None, "L2_attn_wfv", wg="L2_attn_wfr")



def layer3_attn(k):
    nc = k.nc
    normalise(k, "n3a", k.X)
    ctx = Stage(k)
    LINKS = 9
    G = 4
    W = TC * G * S
    with ctx:
        sb, ps = buffers(nc, ctx)
        w_qk = sb("a_w_qk", [P, 2, D])
        w_v = sb("a_w_v", [P, D])
        w_out = sb("a_w_out", [P, D])
        b_row = sb("a_b_row", [P, D])
        bias = sb("a_bias", [P, G, G * S])
        own_head = sb("a_own_head", [P, G])
        own_batch = sb("a_own_batch", [P, G])
        xs = sb("a_xs", [P, CHUNK])
        qs = sb("a_qs", [P, CHUNK])
        km = sb("a_km", [P, TC, G, P])
        vs = sb("a_vs", [P, CHUNK])
        vm = sb("a_vm", [P, TC, H16, G, DH])
        sc = sb("a_sc", [P, G, TC * G, S])
        mx = sb("a_mx", [P, G, TC * G])
        pt = sb("a_pt", [P, G, TC, G, S])
        ob = sb("a_ob", [S, TC, G, H16, DH])
        ot = sb("a_ot", [P, CHUNK])
        rows = sb("a_rows", [P, TC, D])
        psA = ps("a_psA", [P, 3, CHUNK])
        psS = ps("a_psS", [P, G, W])
        psO = ps("a_psO", [P, CHUNK])

        loaded = k.sem("a_loaded")
        xs_ready = k.sem("a_xs_ready")
        q_in = k.sem("a_q_in")
        k_in = k.sem("a_k_in")
        v_in = k.sem("a_v_in")
        q_ready = k.sem("a_q_ready")
        k_ready = k.sem("a_k_ready")
        v_ready = k.sem("a_v_ready")
        vm_ready = k.sem("a_vm_ready")
        scores_done = k.sem("a_scores_done")
        shifted = k.sem("a_shifted")
        exp_done = k.sem("a_exp_done")
        turned = k.sem("a_turned")
        context_done = k.sem("a_context_done")
        context_ready = k.sem("a_context_ready")
        context_turned = k.sem("a_context_turned")
        ot_ready = k.sem("a_ot_ready")
        out_done = k.sem("a_out_done")
        added = k.sem("a_added")
        link = k.sem("a_link")

        with nc.Block() as block:
            @block.sync
            def _(sp):
                for to, name in ((w_qk, "L3_attn_w_qk"), (w_v, "L3_attn_w_v"), (w_out, "L3_attn_w_outT"),
                                 (bias, "L3_attn_bias"), (own_head, "own_head"), (own_batch, "own_batch")):
                    sp.dma_start(to[:], k.a[name]).then_inc(loaded, 16)
                sp.dma_start(b_row[:], k.a["L3_attn_b_out"].partition_broadcast(P)).then_inc(loaded, 16)

            @block.tensor
            def _(pe):
                pe.wait_ge(loaded, 16 * 7)
                with pe.Fori(0, CHUNKS) as i:
                    pe.wait_ge(xs_ready, i + 1)
                    pe.wait_ge(added, i)
                    pe.matmul(psA[:, 0], w_qk[:, 0], xs[:], start=True, stop=True).then_inc(q_in, 1)
                    pe.matmul(psA[:, 1], w_qk[:, 1], xs[:], start=True, stop=True).then_inc(k_in, 1)
                    for t in range(TC):
                        mm = pe.matmul(psA[:, 2, t * P:(t + 1) * P], xs[:, t * P:(t + 1) * P], w_v[:],
                                       start=True, stop=True)
                    mm.then_inc(v_in, 1)
                    pe.wait_ge(q_ready, i + 1)
                    pe.wait_ge(k_ready, i + 1)
                    pe.nop(nofuse=True)
                    for t in range(TC):
                        for b in range(BT):
                            at = t * P + b * S
                            for r in range(G):
                                mm = pe.matmul(
                                    psS[b * S:(b + 1) * S, r, t * G * S:(t + 1) * G * S], qs[r * S:(r + 1) * S, at:at + S],
                                    km[r * S:(r + 1) * S, t, :, b * S:(b + 1) * S], start=True, stop=True)
                    mm.then_inc(scores_done, 1)
                    pe.wait_ge(turned, i + 1)
                    pe.wait_ge(vm_ready, i + 1)
                    for t in range(TC):
                        pe.wait_ge(context_ready, i * TC + t)
                        for h in range(H16):
                            mm = pe.matmul(psO[0:S, h * S:(h + 1) * S], pt[:, h // G, t, h % G, :],
                                           vm[:, t, h].rearrange("p b d -> p (b d)"), start=True, stop=True)
                        mm.then_inc(context_done, 1)
                    pe.wait_ge(context_ready, (i + 1) * TC)
                    pe.nop(nofuse=True)
                    for t in range(TC):
                        for b in range(BT):
                            at = t * P + b * S
                            mm = pe.transpose(psA[:, 0, at:at + S], ob[:, t, b].rearrange("p h d -> p (h d)"),
                                              k.ident[0:S, 0:S])
                    mm.then_inc(context_turned, 1)
                    pe.wait_ge(ot_ready, i + 1)
                    for t in range(TC):
                        mm = pe.matmul(psA[:, 1, t * P:(t + 1) * P], ot[:, t * P:(t + 1) * P], w_out[:],
                                       start=True, stop=True)
                    mm.then_inc(out_done, 1)

            @block.scalar
            def _(act):
                with act.Fori(0, CHUNKS) as i:
                    act.wait_ge(v_in, i)
                    act.activation(xs[:], k.XT[:, ds(i * CHUNK, CHUNK)], ACT.Copy).then_inc(xs_ready, 1)
                    act.wait_ge(q_in, i + 1)
                    act.activation(qs[:], psA[:, 0], ACT.Copy, scale=DH ** -0.5).then_inc(q_ready, 1)
                    act.wait_ge(v_in, i + 1)
                    act.activation(vs[:], psA[:, 2], ACT.Copy).then_inc(v_ready, 1)
                    act.wait_ge(shifted, i + 1)
                    act.activation(sc[:], sc[:], ACT.Exp).then_inc(exp_done, 1)
                    for t in range(TC):
                        act.wait_ge(context_done, i * TC + t + 1)
                        act.activation(ob[:, t].rearrange("p b h d -> p h b d"),
                                       psO[0:S, :].rearrange("p (h b d) -> p h b d", h=H16, b=G),
                                       ACT.Copy).then_inc(context_ready, 1)
                    act.wait_ge(context_turned, i + 1)
                    act.activation(ot[:], psA[:, 0], ACT.Copy).then_inc(ot_ready, 1)

            @block.gpsimd
            def _(g):
                g.wait_ge(loaded, 16 * 7)
                with g.Fori(0, CHUNKS) as i:
                    g.wait_ge(v_ready, i + 1)
                    g.wait_ge(context_done, i * TC)
                    g.nop(nofuse=True)
                    for t in range(TC):
                        for b in range(G):
                            val = g.tensor_scalar(vm[:, t, :, b, :],
                                                  vs[:, t * P:(t + 1) * P].rearrange("p (h d) -> p h d", d=DH),
                                                  own_batch[:, b:b + 1], None, ALU.mult)
                    val.then_inc(vm_ready, 1)

            @block.vector
            def _(v):
                v.wait_ge(loaded, 16 * 7)
                with v.Fori(0, CHUNKS) as i:
                    ln = Chain(v, link, i * LINKS, LINKS)
                    v.wait_ge(k_in, i + 1)
                    v.tensor_tensor(km[:].rearrange("p t q j -> p q t j"),
                                    bcast(psA[:, 1].rearrange("p (t j) -> p t j", t=TC), 1, G),
                                    bcast(bcast(own_head[:], 2, TC), 3, P), ALU.mult).then_inc(k_ready, 1)
                    v.wait_ge(scores_done, i + 1)
                    for r in range(G):
                        ln(v.tensor_tensor(sc[:, r].rearrange("p (t q) j -> p t (q j)", t=TC),
                                           psS[:, r].rearrange("p (t c) -> p t c", t=TC), bcast(bias[:, r], 1, TC),
                                           ALU.add))
                    ln(v.tensor_reduce(mx[:], sc[:], AX, ALU.max))
                    v.tensor_tensor(sc[:], sc[:], bcast(mx[:], 3, S), ALU.subtract).then_inc(shifted, 1)
                    v.wait_ge(exp_done, i + 1)
                    ln(v.tensor_reduce(mx[:], sc[:], AX, ALU.add))
                    ln(v.reciprocal(mx[:], mx[:]))
                    ln(v.tensor_tensor(sc[:], sc[:], bcast(mx[:], 3, S), ALU.mult))
                    v.transpose(pt[:].rearrange("p r t q i -> p (r t q i)"),
                                sc[:].rearrange("p r w j -> p (r w j)")).then_inc(turned, 1)
                    v.wait_ge(out_done, i + 1)
                    ln(v.tensor_tensor(rows[:], psA[:, 1].rearrange("p (t d) -> p t d", t=TC), bcast(b_row[:], 1, TC),
                                       ALU.add))
                    ln.done()
                    at = k.X[:, ds(i * CHUNK, CHUNK)]
                    v.tensor_tensor(at, at, rows[:].rearrange("p t d -> p (t d)"), ALU.add).then_inc(added, 1)


def project(k, name, w_name, b_name, dest):
    nc = k.nc
    ctx = Stage(k)
    with ctx:
        sb, ps = buffers(nc, ctx)
        w = sb(f"{name}_w", [P, D])
        b_row = sb(f"{name}_b_row", [P, D])
        xs = sb(f"{name}_xs", [P, 2, CHUNK])
        rows = sb(f"{name}_rows", [P, 2, TC, D])
        psP = ps(f"{name}_psP", [P, 2, CHUNK])
        loaded = k.sem(f"{name}_loaded")
        xs_ready = k.sem(f"{name}_xs_ready")
        projected = k.sem(f"{name}_projected")
        summed = k.sem(f"{name}_summed")
        added = k.sem(f"{name}_added")
        FREE = 2
        with nc.Block() as block:
            @block.sync
            def _(sp):
                sp.dma_start(w[:], k.a[w_name]).then_inc(loaded, 16)
                sp.dma_start(b_row[:], k.a[b_name].partition_broadcast(P)).then_inc(loaded, 16)

            @block.scalar
            def _(act):
                with act.Fori(0, CHUNKS // 2) as i:
                    for b in range(2):
                        c = i * 2 + b
                        act.wait_ge(projected, c + 1)
                        act.activation(xs[:, b, :], k.XT[:, ds(c * CHUNK, CHUNK)], ACT.Copy).then_inc(xs_ready, 1)

            @block.tensor
            def _(pe):
                pe.sem_inc(projected, FREE)
                pe.wait_ge(loaded, 32)
                with pe.Fori(0, CHUNKS // 2) as i:
                    for b in range(2):
                        c = i * 2 + b
                        pe.wait_ge(xs_ready, c + 1)
                        pe.wait_ge(added, c + 1)
                        for t in range(TC):
                            mm = pe.matmul(psP[:, b, t * P:(t + 1) * P], xs[:, b, t * P:(t + 1) * P], w[:],
                                           start=True, stop=True)
                        mm.then_inc(projected, 1)

            @block.vector
            def _(v):
                v.sem_inc(added, FREE)
                with v.Fori(0, CHUNKS // 2) as i:
                    for b in range(2):
                        c = i * 2 + b
                        v.wait_ge(projected, c + 1 + FREE)
                        v.wait_ge(added, c + 1)
                        v.tensor_tensor(rows[:, b], psP[:, b].rearrange("p (t d) -> p t d", t=TC),
                                        bcast(b_row[:], 1, TC), ALU.add).then_inc(summed, 1)
                        v.wait_ge(summed, c + 1)
                        at = dest[:, ds(c * CHUNK, CHUNK)]
                        v.tensor_tensor(at, at, rows[:, b].rearrange("p t d -> p (t d)"), ALU.add).then_inc(added, 1)



def batch_attention(k):
    nc = k.nc
    ctx = Stage(k)
    G = 4
    V = DH + 1
    with ctx:
        sb, ps = buffers(nc, ctx)
        w_qkv = sb("b_w_qkv", [P, 3, D])
        b_q = sb("b_b_q", [P, 1])
        b_k = sb("b_b_k", [P, 1])
        b_v = sb("b_b_v", [P, D])
        own_head = sb("b_own_head", [P, G])
        xs = sb("b_xs", [P, P])
        qs = sb("b_qs", [P, P])
        km = sb("b_km", [P, G, P])
        va = sb("b_va", [P, H16, V])
        mx = sb("b_mx", [P, H16])
        sc = sb("b_sc", [P, H16, P])
        pt = sb("b_pt", [P, H16, P])
        rec = sb("b_rec", [P, H16])
        ob = sb("b_ob", [P, H16, DH])
        psA = ps("b_psA", [P, CHUNK])
        psS = ps("b_psS", [P, G, CHUNK])
        psT = ps("b_psT", [P, 2, CHUNK])
        psO = ps("b_psO", [P, CHUNK])
        O = psO[:, 0:H16 * V].rearrange("p (h d) -> p h d", d=V)
        OT = psO[:, 256:256 + P]
        XTpos = k.XT[:].rearrange("p (b l) -> p l b", l=S)

        loaded = k.sem("b_loaded")
        consts_set = k.sem("b_consts_set")
        xs_ready = k.sem("b_xs_ready")
        qkv_in = k.sem("b_qkv_in")
        q_ready = k.sem("b_q_ready")
        k_ready = k.sem("b_k_ready")
        v_ready = k.sem("b_v_ready")
        scores_done = k.sem("b_scores_done")
        max_done = k.sem("b_max_done")
        shifted = k.sem("b_shifted")
        exp_done = k.sem("b_exp_done")
        turned = k.sem("b_turned")
        pt_ready = k.sem("b_pt_ready")
        context_done = k.sem("b_context_done")
        rec_ready = k.sem("b_rec_ready")
        context_ready = k.sem("b_context_ready")
        context_turned = k.sem("b_context_turned")
        stored = k.sem("b_stored")

        with nc.Block() as block:
            @block.sync
            def _(sp):
                sp.dma_start(w_qkv[:], k.a["L2_ffn_w_qkv"]).then_inc(loaded, 16)
                sp.dma_start(b_q[:], k.a["L2_ffn_in_proj_b"][0:D].unsqueeze(1)).then_inc(loaded, 16)
                sp.dma_start(b_k[:], k.a["L2_ffn_in_proj_b"][D:2 * D].unsqueeze(1)).then_inc(loaded, 16)
                sp.dma_start(b_v[:], k.a["L2_ffn_in_proj_b"][2 * D:].partition_broadcast(P)).then_inc(loaded, 16)
                sp.dma_start(own_head[:], k.a["own_head"]).then_inc(loaded, 16)

            @block.tensor
            def _(pe):
                pe.wait_ge(loaded, 80)

                def front(s):
                    pe.wait_ge(xs_ready, s + 1)
                    pe.wait_ge(v_ready, s)
                    pe.matmul(psA[:, 0:P], w_qkv[:, 0], xs[:], start=True, stop=True)
                    pe.matmul(psA[:, P:2 * P], w_qkv[:, 1], xs[:], start=True, stop=True)
                    pe.matmul(psA[:, 2 * P:3 * P], xs[:], w_qkv[:, 2], start=True, stop=True).then_inc(qkv_in, 1)
                    pe.wait_ge(q_ready, s + 1)
                    pe.wait_ge(k_ready, s + 1)
                    pe.wait_ge(shifted, s)
                    for r in range(G):
                        mm = pe.matmul(psS[:, r], qs[r * S:(r + 1) * S, :],
                                       km[r * S:(r + 1) * S].rearrange("p q j -> p (q j)"), start=True, stop=True)
                    mm.then_inc(scores_done, 1)

                def back(s):
                    pe.wait_ge(exp_done, s + 1)
                    for r in range(G):
                        pe.wait_ge(pt_ready, s * G + r + 1)
                        for q in range(G):
                            mm = pe.transpose(psT[:, r % 2, q * P:(q + 1) * P], sc[:, r * G + q], k.ident[:])
                        mm.then_inc(turned, 1)
                    pe.wait_ge(v_ready, s + 1)
                    pe.wait_ge(stored, s)
                    for h in range(H16):
                        if h % G == 0:
                            pe.wait_ge(pt_ready, s * G + h // G + 1 + 2)
                        mm = pe.matmul(O[:, h], pt[:, h], va[:, h], start=True, stop=True)
                    mm.then_inc(context_done, 1)
                    pe.wait_ge(context_ready, s + 1)
                    pe.transpose(OT, ob[:].rearrange("p h d -> p (h d)"), k.ident[:]).then_inc(context_turned, 1)

                front(0)
                with pe.Fori(0, S - 1) as i:
                    front(i + 1)
                    back(i)
                back(S - 1)

            @block.scalar
            def _(act):
                act.sem_inc(pt_ready, 2)
                act.wait_ge(consts_set, 2)

                def front(s):
                    act.wait_ge(qkv_in, s)
                    act.activation(xs[:], XTpos[:, ds(s, 1), :].rearrange("p l b -> p (l b)"),
                                   ACT.Copy).then_inc(xs_ready, 1)
                    act.wait_ge(qkv_in, s + 1)
                    act.wait_ge(scores_done, s)
                    act.activation(qs[:], psA[:, 0:P], ACT.Identity, scale=DH ** -0.5,
                                   bias=b_q[:]).then_inc(q_ready, 1)

                def back(s):
                    act.wait_ge(shifted, s + 1)
                    act.activation(sc[:], sc[:], ACT.Exp).then_inc(exp_done, 1)

                def turn(s):
                    for r in range(G):
                        act.wait_ge(turned, s * G + r + 1)
                        if r == 0:
                            act.wait_ge(context_done, s)
                        act.activation(pt[:, r * G:(r + 1) * G].rearrange("p h t -> p (h t)"), psT[:, r % 2],
                                       ACT.Copy).then_inc(pt_ready, 1)
                    act.wait_ge(context_turned, s + 1)
                    act.activation(XTpos[:, ds(s, 1), :].rearrange("p l b -> p (l b)"), OT,
                                   ACT.Copy).then_inc(stored, 1)

                front(0)
                with act.Fori(0, S - 1) as i:
                    back(i)
                    front(i + 1)
                    turn(i)
                back(S - 1)
                turn(S - 1)

            @block.vector
            def _(v):
                v.wait_ge(loaded, 80)
                v.memset(va[:], 1.0).then_inc(consts_set, 1)
                v.tensor_scalar(b_q[:], b_q[:], DH ** -0.5, None, ALU.mult).then_inc(consts_set, 1)
                v.wait_ge(consts_set, 2)

                def keys(s):
                    v.wait_ge(q_ready, s + 1)
                    v.wait_ge(scores_done, s)
                    for q in range(G):
                        key = v.tensor_scalar(km[:, q], psA[:, P:2 * P], b_k[:, 0:1], own_head[:, q:q + 1],
                                              ALU.add, ALU.mult)
                    key.then_inc(k_ready, 1)

                def shift(s):
                    v.wait_ge(scores_done, s + 1)
                    S16 = psS[:].rearrange("p r (q j) -> p (r q) j", q=G)
                    v.tensor_reduce(mx[:], S16, AX, ALU.max).then_inc(max_done, 1)
                    v.wait_ge(max_done, s + 1)
                    v.wait_ge(turned, s * G)
                    v.tensor_tensor(sc[:], S16, bcast(mx[:], 2, P), ALU.subtract).then_inc(shifted, 1)

                def values(s):
                    v.tensor_tensor(va[:, :, 0:DH], psA[:, 2 * P:3 * P].rearrange("p (h d) -> p h d", d=DH),
                                    b_v[:].rearrange("p (h d) -> p h d", d=DH), ALU.add).then_inc(v_ready, 1)

                def norm(s):
                    v.wait_ge(context_done, s + 1)
                    v.reciprocal(rec[:], O[:, :, DH]).then_inc(rec_ready, 1)
                    v.wait_ge(rec_ready, s + 1)
                    v.wait_ge(context_turned, s)
                    v.tensor_tensor(ob[:], O[:, :, 0:DH], bcast(rec[:], 2, DH), ALU.mult).then_inc(context_ready, 1)

                keys(0)
                shift(0)
                values(0)
                with v.Fori(0, S - 1) as i:
                    keys(i + 1)
                    shift(i + 1)
                    norm(i)
                    values(i + 1)
                norm(S - 1)


def layer2_ffn(k):
    normalise(k, "n2f", k.X, keep=k.H)
    batch_attention(k)
    project(k, "bp", "L2_ffn_out_wT", "L2_ffn_out_b", k.H)
    normalise(k, "n2g", k.H, gain="L2_ffn_ln1_g", bias="L2_ffn_ln1_b", keep=k.H, whole=True)
    mixture(k, "f2", 8, 1, k.H, "assign", "L2_ffn_wr", "L2_ffn_router_b", "L2_ffn_wu", "L2_ffn_bu", "L2_ffn_wd",
            "L2_ffn_b2")
    normalise(k, "n2h", k.H, gain="L2_ffn_ln2_g", bias="L2_ffn_ln2_b", add_to=k.X)



def layer2_xattn(k):
    nc = k.nc
    normalise(k, "n2x", k.X)
    ctx = Stage(k)
    G = 4
    V = DH + 1
    GROUPS = BC // G
    NK = KEYS + S
    KT = 3
    with ctx:
        sb, ps = buffers(nc, ctx)
        w_qk = sb("x_w_qk", [P, 2, D])
        w_v = sb("x_w_v", [P, D])
        w_proj = sb("x_w_proj", [P, D])
        b_row = sb("x_b_row", [P, D])
        own_head = sb("x_own_head", [P, G])
        own_row = sb("x_own_row", [P, G])
        klast = sb("x_klast", [P, B])
        xs = sb("x_xs", [P, CHUNK])
        qs = sb("x_qs", [P, CHUNK])
        qm = sb("x_qm", [P, BC, G, S])
        kc = sb("x_kc", [P, 2, G, NK])
        kown = sb("x_kown", [P, BC, S])
        vc = sb("x_vc", [P, 2, G, 2, P])
        va = sb("x_va", [P, 2, G, KT, H16, V])
        sc = sb("x_sc", [P, 2, G, NK])
        mx = sb("x_mx", [P, 2, G])
        pt = sb("x_pt", [P, KT, CHUNK])
        om = sb("x_om", [P, G, G, V])
        od = sb("x_od", [P, G, V])
        rec = sb("x_rec", [P, G])
        oc = sb("x_oc", [P, G, DH])
        ot = sb("x_ot", [P, CHUNK])
        rows = sb("x_rows", [P, TC, D])
        psA = ps("x_psA", [P, CHUNK])
        psS = ps("x_psS", [P, G, CHUNK])
        psT = ps("x_psT", [P, 2, CHUNK])
        psO = ps("x_psO", [P, CHUNK])
        O = psO[:, 0:G * G * V].rearrange("p (r q d) -> p r q d", r=G, q=G)

        loaded = k.sem("x_loaded")
        ones_set = k.sem("x_ones_set")
        kc_loaded = k.sem("x_kc_loaded")
        vc_loaded = k.sem("x_vc_loaded")
        vlast_loaded = k.sem("x_vlast_loaded")
        xs_ready = k.sem("x_xs_ready")
        in_done = k.sem("x_in_done")
        q_ready = k.sem("x_q_ready")
        qm_ready = k.sem("x_qm_ready")
        kself_ready = k.sem("x_kself_ready")
        klast_ready = k.sem("x_klast_ready")
        va_ready = k.sem("x_va_ready")
        vself_in = k.sem("x_vself_in")
        vself_ready = k.sem("x_vself_ready")
        scores_done = k.sem("x_scores_done")
        max_done = k.sem("x_max_done")
        negated = k.sem("x_negated")
        exp_done = k.sem("x_exp_done")
        turned = k.sem("x_turned")
        pt_ready = k.sem("x_pt_ready")
        pt2_ready = k.sem("x_pt2_ready")
        context_done = k.sem("x_context_done")
        link = k.sem("x_link")
        picked = k.sem("x_picked")
        ot_ready = k.sem("x_ot_ready")
        out_done = k.sem("x_out_done")
        summed = k.sem("x_summed")
        added = k.sem("x_added")
        LOADS = 7
        LINKS = 3 * BC

        with nc.Block() as block:
            @block.sync
            def _(sp):
                for to, name in ((w_qk, "L2_xattn_w_qk"), (w_v, "L2_xattn_w_v"), (w_proj, "L2_xattn_w_projT"),
                                 (own_head, "own_head"), (own_row, "own_batch")):
                    sp.dma_start(to[:], k.a[name]).then_inc(loaded, 16)
                sp.dma_start(klast[:], k.a["ctx_lastT"][0:P, :]).then_inc(loaded, 16)
                sp.dma_start(b_row[:], k.a["L2_xattn_b_proj"].partition_broadcast(P)).then_inc(loaded, 16)
                sp.wait_ge(ones_set, 1)

                def load(n, slot, back):
                    sp.wait_ge(scores_done, back * 2)
                    sp.nop(nofuse=True)
                    sp.wait_ge(klast_ready, n)
                    sp.nop(nofuse=True)
                    first = n * G
                    sp.dma_start(kc[:, slot, :, 0:2 * P],
                                 k.a["ctxT"][ds(first, G), 0:P, 0:2 * P].rearrange("b c n -> c b n"))\
                        .then_inc(kc_loaded, 16)
                    sp.wait_ge(va_ready, n)
                    sp.nop(nofuse=True)
                    for j in range(2):
                        sp.dma_start(vc[:, slot, :, j, :],
                                     k.a["ctx"][ds(first, G), j * P:(j + 1) * P, P:2 * P].rearrange("b n c -> n b c"))\
                            .then_inc(vc_loaded, 16)
                    sp.wait_ge(context_done, back)
                    sp.nop(nofuse=True)
                    for j in range(G):
                        sp.dma_start(va[S:S + 1, slot, j, 2, :, 0:DH],
                                     k.a["ctx_last"][ds(first + j, 1), P:2 * P].rearrange("b (h d) -> b h d", d=DH))\
                            .then_inc(vlast_loaded, 16)

                load(0, 0, 0)
                with sp.Fori(0, CHUNKS - 1) as i:
                    load(i * GROUPS + 1, 1, i * BC)
                    load(i * GROUPS + 2, 0, i * BC + G)
                    load(i * GROUPS + 3, 1, i * BC + 2 * G)
                    load(i * GROUPS + 4, 0, i * BC + 3 * G)
                last = (CHUNKS - 1) * BC
                for g in range(1, GROUPS):
                    load(last // G + g, g % 2, last + (g - 1) * G)

            @block.gpsimd
            def _(g):
                g.memset(va[:], 1.0).then_inc(ones_set, 1)
                g.wait_ge(loaded, LOADS * 16)
                g.wait_ge(ones_set, 1)
                with g.Fori(0, CHUNKS) as i:
                    for j in range(GROUPS):
                        n = i * GROUPS + j
                        g.wait_ge(kc_loaded, (n + 1) * 16)
                        g.wait_ge(kself_ready, i + 1)
                        g.nop(nofuse=True)
                        g.tensor_copy(kc[:, j % 2, :, 2 * P:NK - 1], kown[:, j * G:(j + 1) * G])
                        g.tensor_copy(kc[:, j % 2, :, NK - 1], klast[:, ds(n * G, G)]).then_inc(klast_ready, 1)
                        g.wait_ge(vc_loaded, (n + 1) * 32)
                        g.wait_ge(vlast_loaded, (n + 1) * 16 * G)
                        g.nop(nofuse=True)
                        g.tensor_copy(va[:, j % 2, :, 0:2, :, 0:DH],
                                      vc[:, j % 2].rearrange("p b t (h d) -> p b t h d", d=DH)).then_inc(va_ready, 1)

            @block.tensor
            def _(pe):
                pe.wait_ge(loaded, LOADS * 16)
                with pe.Fori(0, CHUNKS) as i:
                    pe.wait_ge(xs_ready, i + 1)
                    pe.wait_ge(added, i)
                    pe.matmul(psA[:], w_qk[:, 0], xs[:], start=True, stop=True).then_inc(in_done, 1)
                    pe.wait_ge(q_ready, i + 1)
                    pe.matmul(psA[:], w_qk[:, 1], xs[:], start=True, stop=True).then_inc(in_done, 1)
                    for b in range(BC + 1):
                        if b < BC:
                            g, j = b // G, b % G
                            if j == 0:
                                pe.wait_ge(klast_ready, i * GROUPS + g + 1)
                                pe.wait_ge(vself_ready, i * GROUPS + g)
                                pe.wait_ge(kself_ready, i + 1)
                                for jj in range(G):
                                    mm = pe.matmul(psA[0:S, jj * P:(jj + 1) * P],
                                                   xs[:, (b + jj) * S:(b + jj + 1) * S], w_v[:], start=True, stop=True)
                                mm.then_inc(vself_in, 1)
                            if b == 0:
                                pe.wait_ge(qm_ready, i + 1)
                            for half in range(2):
                                pe.wait_ge(exp_done, (i * BC + b) * G + half * 2 + 2)
                                pe.nop(nofuse=True)
                                for r in range(half * 2, half * 2 + 2):
                                    mm = pe.matmul(psS[:, r, 0:NK],
                                                   qm[r * S:(r + 1) * S, b].rearrange("p q i -> p (q i)"),
                                                   kc[r * S:(r + 1) * S, g % 2, j], start=True, stop=True)
                                mm.then_inc(scores_done, 1)
                        if b >= 1:
                            c = b - 1
                            g, j = c // G, c % G
                            pe.wait_ge(exp_done, (i * BC + c + 1) * G + G)
                            for t in range(KT):
                                n = c * KT + t
                                if t == 0:
                                    pe.wait_ge(pt_ready, (i * BC + c) * 2)
                                if t == 1:
                                    pe.wait_ge(pt2_ready, i * BC + c)
                                if t == 2:
                                    pe.wait_ge(pt_ready, (i * BC + c) * 2 + 1)
                                    pe.nop(nofuse=True)
                                rows_t = P if t < 2 else S + 1
                                for r in range(G):
                                    mm = pe.transpose(psT[0:rows_t, n % 2, r * P:(r + 1) * P],
                                                      sc[:, c % 2, r, t * P:t * P + rows_t], k.ident[:])
                                mm.then_inc(turned, 1)
                            pe.wait_ge(pt_ready, (i * BC + c + 1) * 2)
                            pe.wait_ge(pt2_ready, i * BC + c + 1)
                            pe.wait_ge(va_ready, i * GROUPS + g + 1)
                            pe.wait_ge(vself_ready, i * GROUPS + g + 1)
                            pe.wait_ge(picked, i * BC + c)
                            pe.nop(nofuse=True)
                            for r in range(G):
                                for t in range(KT):
                                    rows_t = P if t < 2 else S + 1
                                    mm = pe.matmul(O[:, r].rearrange("p q d -> p (q d)"),
                                                   pt[0:rows_t, t, r * P:(r + 1) * P],
                                                   va[0:rows_t, g % 2, j, t, r * G:(r + 1) * G, :]
                                                   .rearrange("p h d -> p (h d)"),
                                                   start=(t == 0), stop=(t == KT - 1))
                            mm.then_inc(context_done, 1)
                    pe.wait_ge(ot_ready, (i + 1) * BC)
                    pe.wait_ge(vself_ready, (i + 1) * GROUPS)
                    for t in range(TC):
                        mm = pe.matmul(psA[:, t * P:(t + 1) * P], ot[:, t * P:(t + 1) * P], w_proj[:],
                                       start=True, stop=True)
                    mm.then_inc(out_done, 1)

            @block.scalar
            def _(act):
                act.sem_inc(exp_done, G)
                act.wait_ge(loaded, LOADS * 16)
                act.wait_ge(ones_set, 1)
                with act.Fori(0, CHUNKS) as i:
                    act.wait_ge(vself_in, i * GROUPS)
                    act.activation(xs[:], k.XT[:, ds(i * CHUNK, CHUNK)], ACT.Copy).then_inc(xs_ready, 1)
                    act.wait_ge(in_done, i * 2 + 1)
                    act.activation(qs[:], psA[:], ACT.Copy, scale=DH ** -0.5).then_inc(q_ready, 1)
                    act.wait_ge(in_done, i * 2 + 2)

                    act.wait_ge(klast_ready, i * GROUPS)
                    act.activation(kown[:].rearrange("p b j -> p (b j)"), psA[:], ACT.Copy).then_inc(kself_ready, 1)
                    for b in range(BC):
                        g, j = b // G, b % G
                        if j == 0:
                            act.wait_ge(vself_in, i * GROUPS + g + 1)
                            act.wait_ge(context_done, i * BC + b - (G if b else 0))
                            act.activation(va[0:S, g % 2, :, 2, :, 0:DH],
                                           psA[0:S, :].rearrange("p (b h d) -> p b h d", b=G, d=DH),
                                           ACT.Copy).then_inc(vself_ready, 1)
                        for r in range(G):
                            act.wait_ge(negated, (i * BC + b) * 2 + r // 2 + 1)
                            if r == 0:
                                act.wait_ge(turned, (i * BC + max(b - 1, 0)) * KT)
                            act.activation(sc[:, b % 2, r], psS[:, r, 0:NK], ACT.Exp,
                                           bias=mx[:, b % 2, r:r + 1]).then_inc(exp_done, 1)
                        if b >= 1:
                            act.wait_ge(turned, (i * BC + b) * KT)
                            act.wait_ge(context_done, i * BC + b - 1)
                            act.activation(pt[0:S + 1, 2], psT[0:S + 1, ((b - 1) * KT + 2) % 2],
                                           ACT.Copy).then_inc(pt2_ready, 1)
                    act.wait_ge(turned, (i + 1) * BC * KT)
                    act.wait_ge(context_done, (i + 1) * BC - 1)
                    act.activation(pt[0:S + 1, 2], psT[0:S + 1, ((BC - 1) * KT + 2) % 2],
                                   ACT.Copy).then_inc(pt2_ready, 1)

            @block.vector
            def _(v):
                v.wait_ge(loaded, LOADS * 16)
                with v.Fori(0, CHUNKS) as i:
                    ln = Chain(v, link, i * LINKS, LINKS)
                    v.wait_ge(q_ready, i + 1)
                    v.tensor_tensor(qm[:].rearrange("p b q i -> p q b i"),
                                    bcast(qs[:].rearrange("p (b i) -> p b i", b=BC), 1, G),
                                    bcast(bcast(own_head[:], 2, BC), 3, S), ALU.mult).then_inc(qm_ready, 1)

                    def maxima(b):
                        for half in range(2):
                            v.wait_ge(scores_done, (i * BC + b) * 2 + half + 1)
                            two = mx[:, b % 2, half * 2:half * 2 + 2]
                            v.tensor_reduce(two, psS[:, half * 2:half * 2 + 2, 0:NK], AX, ALU.max)\
                                .then_inc(max_done, 1)
                            v.wait_ge(max_done, (i * BC + b) * 2 + half + 1)
                            v.tensor_scalar(two, two, -1.0, None, ALU.mult).then_inc(negated, 1)

                    def copies(c):
                        for t in range(2):
                            v.wait_ge(turned, (i * BC + c) * KT + t + 1)
                            v.wait_ge(context_done, i * BC + c)
                            v.tensor_copy(pt[:, t], psT[:, (c * KT + t) % 2]).then_inc(pt_ready, 1)

                    def pick(c):
                        v.wait_ge(context_done, i * BC + c + 1)
                        ln(v.tensor_tensor(om[:], O, bcast(bcast(own_row[:], 1, G), 3, V), ALU.mult))
                        v.tensor_reduce(od[:], om[:].rearrange("p r q d -> p r d q"), AX, ALU.add)\
                            .then_inc(picked, 1)
                        v.wait_ge(picked, i * BC + c + 1)
                        ln(v.reciprocal(rec[:], od[:, :, DH]))
                        ln(v.tensor_tensor(oc[:], od[:, :, 0:DH], bcast(rec[:], 2, DH), ALU.mult))
                        v.transpose(ot[:, c * S:(c + 1) * S], oc[:].rearrange("p r d -> p (r d)")).then_inc(ot_ready, 1)

                    for b in range(BC + 2):
                        if b < BC:
                            maxima(b)
                        if 1 <= b <= BC:
                            copies(b - 1)
                        if b >= 2:
                            pick(b - 2)
                    ln.done()
                    v.wait_ge(out_done, i + 1)
                    v.tensor_tensor(rows[:], psA[:].rearrange("p (t d) -> p t d", t=TC), bcast(b_row[:], 1, TC),
                                    ALU.add).then_inc(summed, 1)
                    v.wait_ge(summed, i + 1)
                    at = k.X[:, ds(i * CHUNK, CHUNK)]
                    v.tensor_tensor(at, at, rows[:].rearrange("p t d -> p (t d)"), ALU.add).then_inc(added, 1)



def layer0_attn(k):
    nc = k.nc
    normalise(k, "n0a", k.X)
    G = 4
    V = DH + 1
    REG = 1e-6
    NL = 64
    J = S + V
    k_dram = nc.dram_tensor("l_k_dram", (TILES, P, G, G * S), F32).ap()
    r_dram = nc.dram_tensor("l_r_dram", (B, S, H16 * V), F32).ap()
    y_dram = nc.dram_tensor("l_y_dram", (B, S, H16 * V), F32).ap()
    q_dram = nc.dram_tensor("l_q_dram", (CHUNKS, P, G * CHUNK), F32).ap()
    kernel_matrices(k, q_dram, k_dram, r_dram)
    landmark_solve(k, k_dram, r_dram, y_dram, REG, NL, J)
    landmark_read(k, q_dram, y_dram)


def kernel_matrices(k, q_dram, k_dram, r_dram):
    nc = k.nc
    G = 4
    V = DH + 1
    LINKS = 5
    ctx = Stage(k)
    with ctx:
        sb, ps = buffers(nc, ctx)
        w_kq = sb("l_w_kq", [P, 4, P])
        b_kq = sb("l_b_kq", [P, 4])
        b_kq2 = sb("l_b_kq2", [P, 4])
        w_tok = sb("l_w_tok", [P, 3 * D])
        b_tok = sb("l_b_tok", [P, 3 * D])
        own_head = sb("l_own_head", [P, G])
        own_batch = sb("l_own_batch", [P, G])
        temp = sb("l_temp", [P, 1])
        ninv = sb("l_ninv", [P, 1])
        xs = sb("l_xs", [P, CHUNK])
        kk = sb("l_kk", [P, 2, CHUNK])
        lk = sb("l_lk", [P, 4, CHUNK])
        rk = sb("l_rk", [P, 2, G, CHUNK])
        tok = sb("l_tok", [P, TC, 3 * D])
        sq = sb("l_sq", [P, TC, 2 * D])
        norm = sb("l_norm", [P, TC, 2, H16])
        dist = sb("l_dist", [P, 2, G, TC * G, S])
        turn = sb("l_turn", [P, G, TC * G, S])
        vm = sb("l_vm", [P, TC, H16, G, V])
        rb = sb("l_rb", [S, 2, G, H16, V])
        psA = ps("l_psA", [P, 2, CHUNK])
        psS = ps("l_psS", [P, G, CHUNK])
        psR = ps("l_psR", [P, 2, CHUNK])

        loaded = k.sem("l_loaded")
        consts_set = k.sem("l_consts_set")
        xs_ready = k.sem("l_xs_ready")
        in_done = k.sem("l_in_done")
        in_read = k.sem("l_in_read")
        tok_in = k.sem("l_tok_in")
        tok_read = k.sem("l_tok_read")
        squared = k.sem("l_squared")
        rk_ready = k.sem("l_rk_ready")
        vm_ready = k.sem("l_vm_ready")
        scores_done = k.sem("l_scores_done")
        dist_ready = k.sem("l_dist_ready")
        exp_done = k.sem("l_exp_done")
        turned = k.sem("l_turned")
        temp_ready = k.sem("l_temp_ready")
        right_done = k.sem("l_right_done")
        right_ready = k.sem("l_right_ready")
        k_stored = k.sem("l_k_stored")
        r_stored = [k.sem(f"l_r{n}_stored") for n in range(2)]
        q_stored = k.sem("l_q_stored")
        link = k.sem("l_link")

        with nc.Block() as block:
            @block.sync
            def _(sp):
                for to, name in ((w_kq, "L0_attn_w_kq"), (b_kq, "L0_attn_b_kq"), (w_tok, "L0_attn_w_tok"),
                                 (own_head, "own_head"), (own_batch, "own_batch")):
                    sp.dma_start(to[:], k.a[name]).then_inc(loaded, 16)
                sp.dma_start(b_tok[:], k.a["L0_attn_b_tok"].partition_broadcast(P)).then_inc(loaded, 16)
                sp.dma_start(temp[:], k.a["L0_attn_temperature"].partition_broadcast(P)).then_inc(loaded, 16)
                with sp.Fori(0, CHUNKS) as i:
                    sp.wait_ge(exp_done, i * 2 + 1)
                    sp.nop(nofuse=True)
                    for t in range(TC):
                        sp.dma_start(k_dram[ds(i * TC + t, 1)].rearrange("a p r c -> (a p) r c"),
                                     dist[:, 0, :, t * G:(t + 1) * G, :].rearrange("p r q j -> p r (q j)"))\
                            .then_inc(k_stored, 16)
                    for t in range(TC):
                        sp.wait_ge(right_ready, i * TC + t + 1)
                        sp.nop(nofuse=True)
                        sp.dma_start(r_dram[ds((i * TC + t) * BT, BT)].rearrange("b i c -> i b c"),
                                     rb[:, t % 2].rearrange("p b h d -> p b (h d)")).then_inc(r_stored[t % 2], 16)
                    sp.wait_ge(turned, i + 1)
                    sp.nop(nofuse=True)
                    sp.dma_start(q_dram[ds(i, 1)].rearrange("a p c -> (a p) c"),
                                 turn[:].rearrange("p r w j -> p (r w j)")).then_inc(q_stored, 16)
                sp.wait_ge(q_stored, 16 * CHUNKS)
                sp.wait_ge(k_stored, 16 * TILES)
                for half in range(2):
                    sp.wait_ge(r_stored[half], 16 * TILES // 2)

            @block.tensor
            def _(pe):
                pe.wait_ge(loaded, 112)
                pe.wait_ge(consts_set, 4)
                with pe.Fori(0, CHUNKS) as i:
                    pe.wait_ge(xs_ready, i + 1)
                    for f in range(4):
                        if f < 2:
                            pe.wait_ge(tok_read, i * TC)
                        else:
                            pe.wait_ge(in_read, i * 4 + f - 1)
                        pe.matmul(psA[:, f % 2], w_kq[:, f], xs[:], start=True, stop=True).then_inc(in_done, 1)
                    for t in range(TC):
                        pe.wait_ge(in_read, (i + 1) * 4)
                        if t >= 2:
                            pe.wait_ge(tok_read, i * TC + t - 1)
                        pe.matmul(psA[:, t % 2, 0:3 * D], xs[:, t * P:(t + 1) * P], w_tok[:],
                                  start=True, stop=True).then_inc(tok_in, 1)
                    pe.wait_ge(rk_ready, i + 1)
                    for m in range(2):
                        pe.wait_ge(dist_ready, i * 2 + m)
                        pe.nop(nofuse=True)
                        for t in range(TC):
                            for b in range(BT):
                                at = t * P + b * S
                                for r in range(G):
                                    low = r % 2 * 64
                                    mm = pe.matmul(psS[b * S:(b + 1) * S, r, t * P:(t + 1) * P],
                                                   lk[low:low + 64, m * 2 + r // 2, at:at + S],
                                                   rk[low:low + 64, r // 2, :, at:at + S], start=True, stop=True)
                        mm.then_inc(scores_done, 1)
                    pe.wait_ge(exp_done, i * 2 + 1)
                    pe.wait_ge(vm_ready, i + 1)
                    for t in range(TC):
                        pe.wait_ge(right_ready, i * TC + t)
                        pe.nop(nofuse=True)
                        for h in range(H16):
                            mm = pe.matmul(psR[0:S, h // 8, h % 8 * G * V:(h % 8 + 1) * G * V],
                                           dist[:, 0, h // G, t * G + h % G, :],
                                           vm[:, t, h].rearrange("p b d -> p (b d)"), start=True, stop=True)
                        mm.then_inc(right_done, 1)

            @block.scalar
            def _(act):
                act.wait_ge(loaded, 112)
                act.wait_ge(consts_set, 4)
                with act.Fori(0, CHUNKS) as i:
                    act.wait_ge(tok_in, i * TC)
                    act.activation(xs[:], k.XT[:, ds(i * CHUNK, CHUNK)], ACT.Copy).then_inc(xs_ready, 1)
                    act.wait_ge(scores_done, i * 2)
                    for f in range(4):
                        act.wait_ge(in_done, i * 4 + f + 1)
                        if f < 2:
                            act.wait_ge(rk_ready, i)
                            act.activation(kk[:, f], psA[:, f], ACT.Identity, bias=b_kq[:, f:f + 1])
                        for low in (0, 2 * S):
                            x = act.activation(lk[low:low + S, f], psA[low:low + S, f % 2], ACT.Identity,
                                               scale=-2.0, bias=b_kq2[low:low + S, f:f + 1])
                        x.then_inc(in_read, 1)
                    act.wait_ge(tok_read, (i + 1) * TC)
                    act.activation(sq[:], tok[:, :, 0:2 * D], ACT.Square).then_inc(squared, 1)
                    for m in range(2):
                        act.wait_ge(dist_ready, i * 2 + m + 1)
                        act.activation(dist[:, m], dist[:, m], ACT.Exp, scale=ninv[:]).then_inc(exp_done, 1)
                    for t in range(TC):
                        act.wait_ge(right_done, i * TC + t + 1)
                        act.wait_ge(r_stored[t % 2], (i * TC // 2 + t // 2) * 16)
                        for half in range(2):
                            x = act.activation(rb[:, t % 2, :, half * 8:half * 8 + 8].rearrange("p b h d -> p h b d"),
                                               psR[0:S, half, 0:8 * G * V].rearrange("p (h b d) -> p h b d", h=8, b=G),
                                               ACT.Copy)
                        x.then_inc(right_ready, 1)

            @block.gpsimd
            def _(g):
                g.wait_ge(consts_set, 4)
                g.wait_ge(loaded, 112)
                with g.Fori(0, CHUNKS) as i:
                    g.wait_ge(tok_read, (i + 1) * TC)
                    g.wait_ge(right_done, i * TC)
                    g.nop(nofuse=True)
                    for t in range(TC):
                        for b in range(G):
                            val = g.tensor_scalar(vm[:, t, :, b, 0:DH],
                                                  tok[:, t, 2 * D:].rearrange("p (h d) -> p h d", d=DH),
                                                  own_batch[:, b:b + 1], None, ALU.mult)
                    val.then_inc(vm_ready, 1)

            @block.vector
            def _(v):
                v.wait_ge(loaded, 112)
                v.tensor_scalar(b_kq2[:], b_kq[:], -2.0, None, ALU.mult).then_inc(consts_set, 1)
                v.memset(lk[:], 1.0).then_inc(consts_set, 1)
                v.tensor_copy(vm[:, :, :, :, DH].rearrange("p t h b -> p (t h) b"),
                              bcast(own_batch[:], 1, TC * H16)).then_inc(consts_set, 1)
                v.reciprocal(temp[:], temp[:]).then_inc(temp_ready, 1)
                v.wait_ge(temp_ready, 1)
                v.tensor_scalar(ninv[:], temp[:], -1.0, None, ALU.mult).then_inc(consts_set, 1)
                with v.Fori(0, CHUNKS) as i:
                    ln = Chain(v, link, i * LINKS, LINKS)
                    v.wait_ge(in_read, i * 4 + 2)
                    for low in (S, 3 * S):
                        ln(v.tensor_tensor(kk[low:low + S], kk[low:low + S], kk[low:low + S], ALU.mult))
                    v.wait_ge(scores_done, i * 2)
                    for f in range(2):
                        m = v.tensor_tensor(rk[:, f], bcast(kk[:, f], 1, G), bcast(own_head[:], 2, CHUNK), ALU.mult)
                    m.then_inc(rk_ready, 1)
                    v.wait_ge(vm_ready, i)
                    v.wait_ge(squared, i)
                    for t in range(TC):
                        v.wait_ge(tok_in, i * TC + t + 1)
                        v.tensor_tensor(tok[:, t], psA[:, t % 2, 0:3 * D], b_tok[:], ALU.add).then_inc(tok_read, 1)
                    v.wait_ge(squared, i + 1)
                    ln(v.tensor_reduce(norm[:].rearrange("p t m h -> p t (m h)"),
                                       sq[:].rearrange("p t (h d) -> p t h d", d=DH), AX, ALU.add))
                    for m in range(2):
                        v.wait_ge(scores_done, i * 2 + m + 1)
                        if m == 0:
                            v.wait_ge(right_done, i * TC)
                            v.wait_ge(k_stored, i * TC * 16)
                        for r in range(G):
                            x = v.tensor_tensor(
                                dist[:, m, r].rearrange("p (t q) j -> p t q j", t=TC),
                                psS[:, r].rearrange("p (t q j) -> p t q j", t=TC, q=G),
                                bcast(norm[:, :, 1 - m, r * G:(r + 1) * G], 3, S), ALU.add)
                            if r == G - 1:
                                ln(x)
                        v.tensor_scalar(dist[:, m], dist[:, m], 0.0, None, ALU.max).then_inc(dist_ready, 1)
                    v.wait_ge(exp_done, i * 2 + 2)
                    v.wait_ge(q_stored, i * 16)
                    v.transpose(turn[:].rearrange("p r w j -> p (r w j)"),
                                dist[:, 1].rearrange("p r w j -> p (r w j)")).then_inc(turned, 1)
                    ln.done()


def landmark_solve(k, k_dram, r_dram, y_dram, REG, NL, J):
    nc = k.nc
    V = DH + 1
    ctx = Stage(k)
    with ctx:
        sb, ps = buffers(nc, ctx)
        A = sb("s_A", [P, S, H16, J])
        rr = sb("s_rr", [P, S, H16 * V])
        tmp = sb("s_tmp", [P, S // 2, H16, J])
        idx_i = sb("s_idx_i", [P, NL], I32)
        idx = sb("s_idx", [P, NL])
        wrap = sb("s_wrap", [P, NL])
        pos = sb("s_pos", [P, S])
        hit = sb("s_hit", [P, S, NL])
        cnt = sb("s_cnt", [P, S])
        land = sb("s_land", [P, S])
        diag = sb("s_diag", [P, S])
        pair = sb("s_pair", [P, S, S])
        piv = sb("s_piv", [P, H16])
        loaded = k.sem("s_loaded")
        link = k.sem("s_link")
        solved = k.sem("s_solved")
        stored = k.sem("s_stored")
        with nc.Block() as block:
            @block.sync
            def _(sp):
                sp.dma_start(idx_i[:], k.a["L0_attn_landmark_idx"].partition_broadcast(P)).then_inc(loaded, 16)
                sp.dma_start(pos[:], k.a["pos"].partition_broadcast(P)).then_inc(loaded, 16)
                sp.dma_start(rr[:], r_dram).then_inc(loaded, 16)
                for i in range(S):
                    sp.dma_start(A[:, i, :, 0:S],
                                 k_dram.rearrange("t (b i) r (q j) -> (t b) i (r q) j", b=BT, q=4)[:, i])\
                        .then_inc(loaded, 16)
                sp.wait_ge(solved, 1)
                sp.dma_start(y_dram, rr[:]).then_inc(stored, 16)
                sp.wait_ge(stored, 16)

            @block.vector
            def _(v):
                ln = Chain(v, link)
                v.wait_ge(loaded, 16 * (3 + S))
                ln(v.tensor_copy(idx[:], idx_i[:]))
                ln(v.tensor_scalar(wrap[:], idx[:], 0.0, float(S), ALU.is_lt, ALU.mult))
                ln(v.tensor_tensor(idx[:], idx[:], wrap[:], ALU.add))
                ln(v.tensor_scalar(idx[:], idx[:], 0.0, float(S - 1), ALU.max, ALU.min))
                ln(v.tensor_tensor(hit[:], bcast(idx[:], 1, S), bcast(pos[:], 2, NL), ALU.is_equal))
                ln(v.tensor_reduce(cnt[:], hit[:], AX, ALU.add))
                ln(v.tensor_scalar(land[:], cnt[:], 1.0, None, ALU.min))
                ln(v.tensor_scalar(cnt[:], cnt[:], 1.0, None, ALU.max))
                ln(v.reciprocal(cnt[:], cnt[:]))
                ln(v.tensor_scalar(cnt[:], cnt[:], REG, -1.0, ALU.mult, ALU.add))
                ln(v.tensor_tensor(cnt[:], cnt[:], land[:], ALU.mult))
                ln(v.tensor_scalar(diag[:], cnt[:], 1.0, None, ALU.add))
                ln(v.tensor_tensor(pair[:], bcast(land[:], 1, S), bcast(land[:], 2, S), ALU.mult))
                ln(v.tensor_tensor(A[:, :, :, 0:S], A[:, :, :, 0:S], bcast(pair[:], 2, H16), ALU.mult))
                ln(v.tensor_tensor(A[:, :, :, S:J],
                                   rr[:].rearrange("p i (h d) -> p i h d", d=V),
                                   bcast(bcast(land[:], 2, H16), 3, V), ALU.mult))
                for n in range(S):
                    ln(v.tensor_scalar(piv[:], A[:, n, :, n], diag[:, n:n + 1], None, ALU.add))
                    ln(v.reciprocal(piv[:], piv[:]))
                    ln(v.tensor_tensor(A[:, n, :, n + 1:J], A[:, n, :, n + 1:J], bcast(piv[:], 2, J - n - 1),
                                       ALU.mult))
                    for lo, hi in ((n + 1, min(S, n + 1 + S // 2)), (n + 1 + S // 2, S)):
                        if lo >= hi:
                            continue
                        m = hi - lo
                        ln(v.tensor_tensor(tmp[:, 0:m, :, n + 1:J], bcast(A[:, lo:hi, :, n], 3, J - n - 1),
                                           bcast(A[:, n, :, n + 1:J], 1, m), ALU.mult))
                        ln(v.tensor_tensor(A[:, lo:hi, :, n + 1:J], A[:, lo:hi, :, n + 1:J],
                                           tmp[:, 0:m, :, n + 1:J], ALU.subtract))
                for n in range(S - 1, 0, -1):
                    for lo, hi in ((0, min(n, S // 2)), (S // 2, n)):
                        if lo >= hi:
                            continue
                        m = hi - lo
                        ln(v.tensor_tensor(tmp[:, 0:m, :, S:J], bcast(A[:, lo:hi, :, n], 3, V),
                                           bcast(A[:, n, :, S:J], 1, m), ALU.mult))
                        ln(v.tensor_tensor(A[:, lo:hi, :, S:J], A[:, lo:hi, :, S:J], tmp[:, 0:m, :, S:J],
                                           ALU.subtract))
                v.tensor_copy(rr[:].rearrange("p i (h d) -> p i h d", d=V), A[:, :, :, S:J]).then_inc(solved, 1)


def landmark_read(k, q_dram, y_dram):
    nc = k.nc
    G = 4
    V = DH + 1
    LINKS = TC * 2 + 1
    ctx = Stage(k)
    with ctx:
        sb, ps = buffers(nc, ctx)
        w_out = sb("y_w_out", [P, D])
        own_batch = sb("y_own_batch", [P, G])
        b_row = sb("y_b_row", [P, D])
        pt = sb("y_pt", [P, G, TC, G, S])
        yy = sb("y_yy", [P, TC, H16, V])
        ym = sb("y_ym", [P, TC, H16, G, V])
        rec = sb("y_rec", [S, H16, G])
        ob = sb("y_ob", [S, TC, G, H16, DH])
        ot = sb("y_ot", [P, CHUNK])
        rows = sb("y_rows", [P, TC, D])
        psO = ps("y_psO", [P, 2, 2, CHUNK])
        psT = ps("y_psT", [P, CHUNK])
        psP = ps("y_psP", [P, CHUNK])
        loaded = k.sem("y_loaded")
        y_loaded = k.sem("y_y_loaded")
        pt_loaded = k.sem("y_pt_loaded")
        ym_ready = k.sem("y_ym_ready")
        context_done = k.sem("y_context_done")
        context_ready = k.sem("y_context_ready")
        context_turned = k.sem("y_context_turned")
        ot_ready = k.sem("y_ot_ready")
        out_done = k.sem("y_out_done")
        added = k.sem("y_added")
        link = k.sem("y_link")
        with nc.Block() as block:
            @block.sync
            def _(sp):
                sp.dma_start(w_out[:], k.a["L0_attn_WoT"]).then_inc(loaded, 16)
                sp.dma_start(own_batch[:], k.a["own_batch"]).then_inc(loaded, 16)
                sp.dma_start(b_row[:], k.a["L0_attn_bo"].partition_broadcast(P)).then_inc(loaded, 16)
                with sp.Fori(0, CHUNKS) as i:
                    sp.wait_ge(context_done, i * TC)
                    sp.nop(nofuse=True)
                    sp.dma_start(pt[:].rearrange("p r t q i -> p (r t q i)"),
                                 q_dram[ds(i, 1)].rearrange("a p c -> (a p) c")).then_inc(pt_loaded, 16)
                    sp.wait_ge(ym_ready, i)
                    sp.nop(nofuse=True)
                    sp.dma_start(yy[:].rearrange("p t h d -> p t (h d)"),
                                 y_dram.rearrange("b j c -> (b j) c").rearrange("(t p) c -> p t c", p=P)
                                 [:, ds(i * TC, TC)]).then_inc(y_loaded, 16)

            @block.gpsimd
            def _(g):
                g.wait_ge(loaded, 48)
                with g.Fori(0, CHUNKS) as i:
                    g.wait_ge(y_loaded, (i + 1) * 16)
                    g.wait_ge(context_done, i * TC)
                    g.nop(nofuse=True)
                    for t in range(TC):
                        for b in range(G):
                            val = g.tensor_scalar(ym[:, t, :, b, :], yy[:, t], own_batch[:, b:b + 1], None, ALU.mult)
                    val.then_inc(ym_ready, 1)

            @block.tensor
            def _(pe):
                pe.wait_ge(loaded, 48)
                with pe.Fori(0, CHUNKS) as i:
                    pe.wait_ge(pt_loaded, (i + 1) * 16)
                    pe.wait_ge(ym_ready, i + 1)
                    for t in range(TC):
                        if t >= 2:
                            pe.wait_ge(context_ready, i * TC + t - 1)
                        for h in range(H16):
                            mm = pe.matmul(psO[0:S, t % 2, h // 8, h % 8 * G * V:(h % 8 + 1) * G * V],
                                           pt[:, h // G, t, h % G, :], ym[:, t, h].rearrange("p b d -> p (b d)"),
                                           start=True, stop=True)
                        mm.then_inc(context_done, 1)
                    pe.wait_ge(context_ready, (i + 1) * TC)
                    pe.nop(nofuse=True)
                    for t in range(TC):
                        for b in range(BT):
                            at = t * P + b * S
                            mm = pe.transpose(psT[:, at:at + S], ob[:, t, b].rearrange("p h d -> p (h d)"),
                                              k.ident[0:S, 0:S])
                    mm.then_inc(context_turned, 1)
                    pe.wait_ge(ot_ready, i + 1)
                    pe.wait_ge(added, i)
                    for t in range(TC):
                        mm = pe.matmul(psP[:, t * P:(t + 1) * P], ot[:, t * P:(t + 1) * P], w_out[:],
                                       start=True, stop=True)
                    mm.then_inc(out_done, 1)

            @block.scalar
            def _(act):
                with act.Fori(0, CHUNKS) as i:
                    act.wait_ge(context_turned, i + 1)
                    act.activation(ot[:], psT[:], ACT.Copy).then_inc(ot_ready, 1)

            @block.vector
            def _(v):
                v.wait_ge(loaded, 48)
                with v.Fori(0, CHUNKS) as i:
                    ln = Chain(v, link, i * LINKS, LINKS)
                    for t in range(TC):
                        v.wait_ge(context_done, i * TC + t + 1)
                        view = psO[0:S, t % 2, :, 0:8 * G * V].rearrange("p f (h b d) -> p f h b d", h=8, b=G)
                        ln(v.tensor_scalar(rec[:].rearrange("p (f h) b -> p f h b", f=2), view[:, :, :, :, DH],
                                           1e-10, None, ALU.max))
                        ln(v.reciprocal(rec[:], rec[:]))
                        v.wait_ge(context_turned, i)
                        for f in range(2):
                            x = v.tensor_tensor(ob[:, t, :, f * 8:f * 8 + 8].rearrange("p b h d -> p h b d"),
                                                view[:, f, :, :, 0:DH], bcast(rec[:, f * 8:f * 8 + 8], 3, DH),
                                                ALU.mult)
                        x.then_inc(context_ready, 1)
                        v.wait_ge(context_ready, i * TC + t + 1)
                    v.wait_ge(out_done, i + 1)
                    ln(v.tensor_tensor(rows[:], psP[:].rearrange("p (t d) -> p t d", t=TC), bcast(b_row[:], 1, TC),
                                       ALU.add))
                    ln.done()
                    at = k.X[:, ds(i * CHUNK, CHUNK)]
                    v.tensor_tensor(at, at, rows[:].rearrange("p t d -> p (t d)"), ALU.add).then_inc(added, 1)


def layer0_xattn(k):
    nc = k.nc
    normalise(k, "n0x", k.X)
    ctx = Stage(k)
    w256_dram = nc.dram_tensor("c_w256_dram", (B, H16 * D), F32).ap()
    with ctx:
        sb, ps = buffers(nc, ctx)
        att = sb("c_att", [P, TOK])
        kernel_layout = Stage(k)
        with kernel_layout:
            wsb, _ = buffers(nc, kernel_layout)
            w = {"m": wsb("c_m", [P, H16, C]),
                 "u": wsb("c_u", [P, 2, H16, D]),
                 "n": wsb("c_n", [P, H16]),
                 "nv": wsb("c_nv", [H16, D])}
            context_weights(k, w, w256_dram)
            context_attention(k, w, w256_dram, att)
        normalise(k, "n0y", att, gain="L0_xattn_ln_scale", bias="L0_xattn_ln_bias", add_to=k.X, eps=1e-6)


def context_weights(k, w, w256_dram):
    nc = k.nc
    DK = 64
    nv_dram = nc.dram_tensor("d_nv_dram", (1, H16 * D), F32).ap()
    ctx = Stage(k)
    with ctx:
        sb, ps = buffers(nc, ctx)
        wq = sb("d_wq", [DK, H16, D])
        wk = sb("d_wk", [DK, H16, C])
        wv = sb("d_wv", [DK, H16, C])
        wo = sb("d_wo", [DK, H16, D])
        null = sb("d_null", [DK, 2])
        last = sb("d_last", [P, 2, B])
        nrow = sb("d_nrow", [1, H16 * D])
        w256 = sb("d_w256", [P, H16 * D])
        psW = ps("d_psW", [P, 2, CHUNK])
        loaded = k.sem("d_loaded")
        filled = k.sem("d_filled")
        taken = k.sem("d_taken")
        stored = k.sem("d_stored")
        nv_stored = k.sem("d_nv_stored")
        nv_loaded = k.sem("d_nv_loaded")
        LOADS = 7
        M_AT, U_AT, N_AT, NV_AT, W_AT, END = 0, 8, 16, 17, 21, 25

        with nc.Block() as block:
            @block.sync
            def _(sp):
                for to, name in ((wq, "L0_xattn_wqT"), (wk, "L0_xattn_wkT"), (wv, "L0_xattn_wvT"),
                                 (wo, "L0_xattn_wo"), (null, "L0_xattn_nullT")):
                    sp.dma_start(to[:], k.a[name]).then_inc(loaded, 16)
                for half in range(2):
                    sp.dma_start(last[:, half], k.a["ctx_lastT"][half * P:(half + 1) * P, :]).then_inc(loaded, 16)
                sp.wait_ge(taken, W_AT)
                sp.dma_start(nv_dram, nrow[:]).then_inc(nv_stored, 16)
                sp.wait_ge(nv_stored, 16)
                sp.dma_start(w["nv"][:], nv_dram.rearrange("o (h d) -> (o h) d", d=D)).then_inc(nv_loaded, 16)
                sp.wait_ge(taken, END)
                sp.dma_start(w256_dram, w256[:]).then_inc(stored, 16)
                sp.wait_ge(nv_loaded, 16)
                sp.wait_ge(stored, 16)

            @block.tensor
            def _(pe):
                pe.wait_ge(loaded, LOADS * 16)
                for j in range(END):
                    bank = psW[:, j % 2]
                    if j >= 2:
                        pe.wait_ge(taken, j - 1)
                    if j < U_AT:
                        for h in (2 * j, 2 * j + 1):
                            mm = pe.matmul(bank[:, h % 2 * C:(h % 2 + 1) * C], wq[:, h], wk[:, h],
                                           start=True, stop=True)
                    elif j < N_AT:
                        half, four = (j - U_AT) // 4, (j - U_AT) % 4
                        for q in range(4):
                            mm = pe.matmul(bank[:, q * D:(q + 1) * D], wv[:, four * 4 + q, half * P:(half + 1) * P],
                                           wo[:, four * 4 + q], start=True, stop=True)
                    elif j < NV_AT:
                        for h in range(H16):
                            mm = pe.matmul(bank[:, h:h + 1], wq[:, h], null[:, 0:1], start=True, stop=True)
                    elif j < W_AT:
                        four = j - NV_AT
                        mm = pe.matmul(bank[0:1], null[:, 1:2],
                                       wo[:, four * 4:four * 4 + 4].rearrange("p h d -> p (h d)"),
                                       start=True, stop=True)
                    else:
                        four = j - W_AT
                        for half in range(2):
                            mm = pe.matmul(bank, last[:, half],
                                           w["u"][:, half, four * 4:four * 4 + 4].rearrange("p h d -> p (h d)"),
                                           start=(half == 0), stop=(half == 1))
                    mm.then_inc(filled, 1)

            @block.scalar
            def _(act):
                for j in range(END):
                    bank = psW[:, j % 2]
                    act.wait_ge(filled, j + 1)
                    if j < U_AT:
                        x = act.activation(w["m"][:, 2 * j:2 * j + 2].rearrange("p h c -> p (h c)"), bank, ACT.Copy,
                                           scale=DK ** -0.5)
                    elif j < N_AT:
                        half, four = (j - U_AT) // 4, (j - U_AT) % 4
                        x = act.activation(w["u"][:, half, four * 4:four * 4 + 4].rearrange("p h d -> p (h d)"),
                                           bank, ACT.Copy)
                    elif j < NV_AT:
                        x = act.activation(w["n"][:], bank[:, 0:H16], ACT.Copy, scale=DK ** -0.5)
                    elif j < W_AT:
                        four = j - NV_AT
                        x = act.activation(nrow[:, four * CHUNK:(four + 1) * CHUNK], bank[0:1], ACT.Copy)
                    else:
                        four = j - W_AT
                        x = act.activation(w256[:, four * CHUNK:(four + 1) * CHUNK], bank, ACT.Copy)
                    x.then_inc(taken, 1)


def context_attention(k, w, w256_dram, att):
    nc = k.nc
    G = 4
    NI = B // 8
    NB = 8
    TOKS = NB * S
    NK = KEYS + 1
    GROUPS = NB // 2
    KT = 3
    FILLS = 17
    TURNS = NB * KT // 2
    q_dram = nc.dram_tensor("c_q_dram", (H16, TOKS), F32).ap()
    t_dram = nc.dram_tensor("c_t_dram", (2, BT * H16 * S), F32).ap()
    ctx = Stage(k)
    with ctx:
        sb, ps = buffers(nc, ctx)
        qt = sb("c_qt", [P, 2, NB, H16, S])
        one = sb("c_one", [1, 1])
        qn = sb("c_qn", [H16, TOKS])
        qrow = sb("c_qrow", [1, NB, H16, S])
        kc = sb("c_kc", [P, 2, 2, 2, KEYS])
        vc = sb("c_vc", [P, 2, 2, 2, C])
        sc = sb("c_sc", [P, 2, G, NK])
        mx = sb("c_mx", [P, 2, G])
        sm = sb("c_sm", [P, 2, G])
        pt = sb("c_pt", [P, 2, 2, CHUNK])
        tail = sb("c_tail", [2, BT, H16, S])
        p256 = sb("c_p256", [H16, BT, S])
        pnull = sb("c_pnull", [H16, P])
        w256 = sb("c_w256", [H16, NB, D])
        ot = sb("c_ot", [P, 2, H16, BT, S])
        psS = ps("c_psS", [P, G, CHUNK])
        psT = ps("c_psT", [P, 2, CHUNK])
        psW = ps("c_psW", [P, 2, CHUNK])

        one_set = k.sem("c_one_set")
        kc_loaded = [k.sem(f"c_kc{n}_loaded") for n in range(2)]
        vc_loaded = [k.sem(f"c_vc{n}_loaded") for n in range(2)]
        w256_loaded = k.sem("c_w256_loaded")
        wide_full = [k.sem(f"c_wide{n}_full") for n in range(2)]
        wide_read = [k.sem(f"c_wide{n}_read") for n in range(2)]
        turn_full = [k.sem(f"c_turn{n}_full") for n in range(2)]
        turn_read = [k.sem(f"c_turn{n}_read") for n in range(2)]
        null_in = k.sem("c_null_in")
        qn_ready = k.sem("c_qn_ready")
        qn_stored = k.sem("c_qn_stored")
        qrow_loaded = k.sem("c_qrow_loaded")
        scores_done = k.sem("c_scores_done")
        max_done = k.sem("c_max_done")
        negated = k.sem("c_negated")
        exp_done = k.sem("c_exp_done")
        sum_done = k.sem("c_sum_done")
        rec_done = k.sem("c_rec_done")
        scaled = k.sem("c_scaled")
        context_done = k.sem("c_context_done")
        tail_ready = k.sem("c_tail_ready")
        tail_stored = k.sem("c_tail_stored")
        tails_loaded = k.sem("c_tails_loaded")
        out_done = k.sem("c_out_done")

        def wide(c, half):
            return H16 + 2 * c + half + (1 if c >= BT else 0)

        def wide_out(t):
            return H16 + (t + 1) * 2 * BT + t

        with nc.Block() as block:
            @block.sync
            def _(sp):
                def load(n, slot, back):
                    if back is not None:
                        sp.wait_ge(scores_done, back * 2)
                        sp.nop(nofuse=True)
                    for j in range(2):
                        sp.dma_start(kc[:, slot, j],
                                     k.a["ctxT"][ds(n * 2 + j, 1)].rearrange("b (f p) n -> p (b f) n", p=P))\
                            .then_inc(kc_loaded[slot], 16)
                    if back is not None:
                        sp.wait_ge(context_done, back)
                        sp.nop(nofuse=True)
                    for j in range(2):
                        sp.dma_start(vc[:, slot, j],
                                     k.a["ctx"][ds(n * 2 + j, 1), 0:2 * P].rearrange("b (t p) c -> p (b t) c", p=P))\
                            .then_inc(vc_loaded[slot], 16)

                def load_last(i):
                    sp.dma_start(w256[:], w256_dram[ds(i * NB, NB)].rearrange("b (h d) -> h b d", d=D))\
                        .then_inc(w256_loaded, 16)

                load(0, 0, None)
                load(1, 1, None)
                load_last(0)
                with sp.Fori(0, NI - 1) as i:
                    for g in range(GROUPS):
                        load(i * GROUPS + 2 + g, g % 2, (i * GROUPS + 1 + g) * 2)
                    sp.wait_ge(out_done, (i + 1) * 2)
                    sp.nop(nofuse=True)
                    load_last(i + 1)
                for g in range(2):
                    n = (NI - 1) * GROUPS + 2 + g
                    load(n, g, (n - 1) * 2)

            @block.gpsimd
            def _(g):
                g.memset(one[:], 1.0).then_inc(one_set, 1)
                with g.Fori(0, NI) as i:
                    g.wait_ge(qn_ready, i + 1)
                    g.wait_ge(qrow_loaded, i * 16)
                    g.nop(nofuse=True)
                    g.dma_start(q_dram, qn[:]).then_inc(qn_stored, 16)
                    g.wait_ge(qn_stored, (i + 1) * 16)
                    g.wait_ge(scores_done, i * NB * 2)
                    g.nop(nofuse=True)
                    g.dma_start(qrow[:], q_dram.rearrange("h (b i) -> b h i", i=S).unsqueeze(0)).then_inc(qrow_loaded, 16)
                    for t in range(2):
                        g.wait_ge(tail_ready, i * NB + (t + 1) * BT)
                        g.wait_ge(tails_loaded, (i * 2 + t) * 32)
                        g.nop(nofuse=True)
                        g.dma_start(t_dram, tail[:].rearrange("k b h i -> k (b h i)")).then_inc(tail_stored, 16)
                        g.wait_ge(tail_stored, (i * 2 + t + 1) * 16)
                        g.wait_ge(out_done, i * 2 + t)
                        g.nop(nofuse=True)
                        for key, to in ((0, p256[:]), (1, pnull[:].rearrange("h (b i) -> h b i", i=S))):
                            g.dma_start(to, t_dram[key:key + 1].rearrange("k (b h i) -> h (k b) i", b=BT, h=H16))\
                                .then_inc(tails_loaded, 16)

            @block.tensor
            def _(pe):
                pe.wait_ge(one_set, 1)

                def fill(i, u):
                    pe.wait_ge(wide_read[u % 2], i * FILLS + u // 2)
                    pe.nop(nofuse=True)
                    return psW[:, u % 2]

                def output(i, t):
                    u = wide_out(t)
                    bank = fill(i, u)[:, 0:D]
                    before = wide(t * BT + BT - 1, 0)
                    for n in (before, before + 1):
                        pe.wait_ge(wide_read[n % 2], i * FILLS + n // 2 + 1)
                    pe.nop(nofuse=True)
                    for half in range(2):
                        for h in range(H16):
                            pe.matmul(bank, ot[:, half, h].rearrange("p b i -> p (b i)"), w["u"][:, half, h],
                                      start=(half == 0 and h == 0), stop=False)
                    pe.wait_ge(tails_loaded, (i * 2 + t + 1) * 32)
                    pe.wait_ge(w256_loaded, (i + 1) * 16)
                    pe.nop(nofuse=True)
                    pe.matmul(bank, pnull[:], w["nv"][:], start=False, stop=False)
                    for b in range(BT):
                        mm = pe.matmul(bank[b * S:(b + 1) * S], p256[:, b], w256[:, t * BT + b],
                                       start=False, stop=True)
                    mm.then_inc(wide_full[u % 2], 1)
                    pe.wait_ge(wide_full[u % 2], i * FILLS + u // 2 + 1)
                    pe.sem_inc(out_done, 1)

                with pe.Fori(0, NI) as i:
                    x = k.XT[:, ds(i * TOKS, TOKS)]
                    pe.wait_ge(exp_done, i * NB * G)
                    pe.matmul(psS[0:H16, 0, 0:TOKS], w["n"][:], x, start=True, stop=True).then_inc(null_in, 1)
                    pe.wait_ge(scores_done, i * NB * 2)
                    for u in range(H16):
                        bank = fill(i, u)
                        half, pair = u // 8, u % 8
                        for q in range(2):
                            mm = pe.matmul(bank[:, q * TOKS:(q + 1) * TOKS],
                                           w["m"][:, pair * 2 + q, half * P:(half + 1) * P], x,
                                           start=True, stop=True)
                        mm.then_inc(wide_full[u % 2], 1)
                    pe.wait_ge(qrow_loaded, (i + 1) * 16)
                    for n in range(2):
                        pe.wait_ge(wide_read[n], i * FILLS + H16 // 2)
                    pe.wait_ge(qn_ready, i + 1)
                    for b in range(NB + 2):
                        if b < NB:
                            g, j = b // 2, b % 2
                            pe.wait_ge(kc_loaded[g % 2], (i * 2 + g // 2 + 1) * 32)
                            for two in range(2):
                                pe.wait_ge(exp_done, (i * NB + b) * G - (G - two * 2 - 2 if b else 0))
                                pe.nop(nofuse=True)
                                for r in range(two * 2, two * 2 + 2):
                                    for half in range(2):
                                        pe.matmul(psS[:, r, 0:KEYS],
                                                  qt[:, half, b, r * G:(r + 1) * G].rearrange("p h i -> p (h i)"),
                                                  kc[:, g % 2, j, half], start=(half == 0), stop=(half == 1))
                                    mm = pe.matmul(psS[:, r, KEYS:NK],
                                                   qrow[:, b, r * G:(r + 1) * G].rearrange("p h i -> p (h i)"),
                                                   one[:], start=True, stop=True)
                                mm.then_inc(scores_done, 1)
                        if 1 <= b <= NB:
                            c = b - 1
                            pe.wait_ge(scaled, i * NB + c + 1)
                            for t in range(KT):
                                u = c * KT + t
                                keys = P if t < 2 else 2
                                pe.wait_ge(turn_read[u % 2], i * TURNS + u // 2)
                                pe.nop(nofuse=True)
                                for r in range(G):
                                    mm = pe.transpose(psT[0:keys, u % 2, r * P:(r + 1) * P],
                                                      sc[:, c % 2, r, t * P:t * P + keys], k.ident[:])
                                mm.then_inc(turn_full[u % 2], 1)
                        if b >= 2:
                            c = b - 2
                            if c == BT:
                                output(i, 0)
                            g, j = c // 2, c % 2
                            pe.wait_ge(vc_loaded[g % 2], (i * 2 + g // 2 + 1) * 32)
                            for t in range(2):
                                u = c * KT + t
                                pe.wait_ge(turn_read[u % 2], i * TURNS + u // 2 + 1)
                            for half in range(2):
                                u = wide(c, half)
                                bank = fill(i, u)
                                for t in range(2):
                                    mm = pe.matmul(bank, vc[:, g % 2, j, t, half * P:(half + 1) * P], pt[:, c % 2, t],
                                                   start=(t == 0), stop=(t == 1))
                                mm.then_inc(wide_full[u % 2], 1)
                                if half == 1:
                                    pe.wait_ge(wide_full[u % 2], i * FILLS + u // 2 + 1)
                                    pe.sem_inc(context_done, 1)
                    output(i, 1)

            @block.scalar
            def _(act):
                with act.Fori(0, NI) as i:
                    act.wait_ge(null_in, i + 1)
                    act.wait_ge(qn_stored, i * 16)
                    act.activation(qn[:], psS[0:H16, 0, 0:TOKS], ACT.Copy).then_inc(qn_ready, 1)
                    for u in range(1, H16, 2):
                        half, pair = u // 8, u % 8
                        act.wait_ge(wide_full[1], i * FILLS + u // 2 + 1)
                        act.activation(qt[:, half, :, pair * 2:pair * 2 + 2].rearrange("p b h i -> p h b i"),
                                       psW[:, 1].rearrange("p (h b i) -> p h b i", h=2, i=S),
                                       ACT.Copy).then_inc(wide_read[1], 1)

                    def read_output(t):
                        u = wide_out(t)
                        act.wait_ge(wide_full[u % 2], i * FILLS + u // 2 + 1)
                        act.activation(att[:, ds((i * 2 + t) * D, D)], psW[:, u % 2, 0:D],
                                       ACT.Copy).then_inc(wide_read[u % 2], 1)

                    for b in range(NB + 2):
                        if b < NB:
                            for r in range(G):
                                act.wait_ge(negated, (i * NB + b) * 2 + r // 2 + 1)
                                if r == 0:
                                    for n in range(2):
                                        last = (b - 1) * KT - 1 if b >= 1 else -1
                                        last -= (last - n) % 2
                                        act.wait_ge(turn_full[n], i * TURNS + (last // 2 + 1 if last >= 0 else 0))
                                act.activation(sc[:, b % 2, r], psS[:, r, 0:NK], ACT.Exp,
                                               bias=mx[:, b % 2, r:r + 1]).then_inc(exp_done, 1)
                        if 1 <= b <= NB:
                            c = b - 1
                            u = c * KT + 2
                            act.wait_ge(turn_full[u % 2], i * TURNS + u // 2 + 1)
                            if c % BT == 0:
                                act.wait_ge(tail_stored, (i * 2 + c // BT) * 16)
                            act.activation(tail[:, c % BT].rearrange("k h i -> k (h i)"), psT[0:2, u % 2],
                                           ACT.Copy).then_inc(tail_ready, 1)
                            act.wait_ge(tail_ready, i * NB + c + 1)
                            act.sem_inc(turn_read[u % 2], 1)
                        if b >= 2:
                            c = b - 2
                            if c == BT:
                                read_output(0)
                            if c % BT == 0:
                                act.wait_ge(out_done, i * 2 + c // BT)
                            for half in range(2):
                                u = wide(c, half)
                                act.wait_ge(wide_full[u % 2], i * FILLS + u // 2 + 1)
                                act.activation(ot[:, half, :, c % BT],
                                               psW[:, u % 2].rearrange("p (h i) -> p h i", i=S),
                                               ACT.Copy).then_inc(wide_read[u % 2], 1)
                    read_output(1)

            @block.vector
            def _(v):
                with v.Fori(0, NI) as i:
                    for u in range(0, H16, 2):
                        half, pair = u // 8, u % 8
                        v.wait_ge(wide_full[0], i * FILLS + u // 2 + 1)
                        v.tensor_copy(qt[:, half, :, pair * 2:pair * 2 + 2].rearrange("p b h i -> p h b i"),
                                      psW[:, 0].rearrange("p (h b i) -> p h b i", h=2, i=S))\
                            .then_inc(wide_read[0], 1)
                    for b in range(NB + 1):
                        if b < NB:
                            for two in range(2):
                                n = (i * NB + b) * 2 + two + 1
                                v.wait_ge(scores_done, n)
                                m = mx[:, b % 2, two * 2:two * 2 + 2]
                                v.tensor_reduce(m, psS[:, two * 2:two * 2 + 2, 0:NK], AX, ALU.max)\
                                    .then_inc(max_done, 1)
                                v.wait_ge(max_done, n)
                                v.tensor_scalar(m, m, -1.0, None, ALU.mult).then_inc(negated, 1)
                        if b >= 1:
                            c = b - 1
                            for t in range(2):
                                u = c * KT + t
                                v.wait_ge(turn_full[u % 2], i * TURNS + u // 2 + 1)
                                if t == 0:
                                    v.wait_ge(context_done, i * NB + max(c - 1, 0))
                                v.tensor_copy(pt[:, c % 2, t], psT[:, u % 2]).then_inc(turn_read[u % 2], 1)
                        if b < NB:
                            n = i * NB + b + 1
                            v.wait_ge(exp_done, n * G)
                            v.tensor_reduce(sm[:, b % 2], sc[:, b % 2], AX, ALU.add).then_inc(sum_done, 1)
                            v.wait_ge(sum_done, n)
                            v.reciprocal(sm[:, b % 2], sm[:, b % 2]).then_inc(rec_done, 1)
                            v.wait_ge(rec_done, n)
                            v.tensor_tensor(sc[:, b % 2], sc[:, b % 2], bcast(sm[:, b % 2], 2, NK), ALU.mult)\
                                .then_inc(scaled, 1)



def program(nc, args, out, phases=None):
    ctx = ExitStack()
    with ctx:
        k = Core(nc, ctx, args)

        def sb(name, shape, dt=F32):
            return ctx.enter_context(nc.sbuf_tensor(name, list(shape), dt))

        k.X = sb("X", [P, TOK])
        k.XT = sb("XT", [P, TOK])
        k.ident = sb("ident", [P, P])
        x_in = ctx.enter_context(nc.semaphore("x_in"))
        x_out = ctx.enter_context(nc.semaphore("x_out"))
        with nc.Block() as block:
            @block.sync
            def _(sp):
                sp.dma_start(k.X[:].rearrange("p (t d) -> p t d", t=TILES),
                             args["x"].rearrange("(t p) d -> p t d", p=P)).then_inc(x_in, 16)
                sp.dma_start(k.ident[:], args["ident"]).then_inc(x_in, 16)
                sp.wait_ge(x_in, 32)

        for phase in PHASES:
            if phases is None or phase.__name__ in phases:
                if phase not in (layer0_xattn, layer0_attn) and not hasattr(k, "H"):
                    k.H = sb("H", [P, TOK])
                    k.DR = sb("DR", [P, TOK])
                phase(k)

        with nc.Block() as block:
            @block.sync
            def _(sp):
                sp.dma_start(out.rearrange("(t p) d -> p t d", p=P),
                             k.X[:].rearrange("p (t d) -> p t d", t=TILES)).then_inc(x_out, 16)
                sp.wait_ge(x_out, 16)


def layer0_ffn(k):
    normalise(k, "n0f", k.X)
    mixture(k, "f0", 8, 4, k.X, "gelu2", "L0_ffn_wr", None, "L0_ffn_wu", "L0_ffn_bu", "L0_ffn_wd", "L0_ffn_b_down")


def layer1_ffn(k):
    normalise(k, "n1f", k.X, gain="L1_ffn_scale", twice=True, residual=True)
    mixture(k, "f1", 16, 1, k.X, "swiglu4", "L1_ffn_wr", "L1_ffn_gate_b", "L1_ffn_wu", "L1_ffn_bu", "L1_ffn_wd",
            "L1_ffn_mlp2_b")


PHASES = [layer0_xattn, layer0_attn, layer0_ffn, layer1_xattn, layer1_attn, layer1_ffn, layer2_xattn, layer2_attn, layer2_ffn, layer3_xattn, layer3_attn, layer3_ffn]



def layout(inp):
    c = np.ascontiguousarray
    a = {"x": c(inp["x"]).reshape(TOK, D)}
    for name, v in inp.items():
        if name not in ("x", "ctx_2048") and v.ndim and v.size <= 1 << 17:
            a[name] = c(v)
    a["ident"] = np.eye(P, dtype=np.float32)
    for e in (8, 16):
        a[f"tri{e}"] = np.tril(np.ones((e, e), np.float32), -1)
        a[f"index{e}"] = np.arange(e, dtype=np.float32)
    a["L0_ffn_wr"] = c(inp["L0_ffn_w_router"].T)
    a["L0_ffn_wu"] = c(inp["L0_ffn_w_up"].reshape(8 * 4, P, D).transpose(2, 0, 1))
    a["L0_ffn_bu"] = c(inp["L0_ffn_b_up"].reshape(8 * 4, P).T)
    a["L0_ffn_wd"] = c(inp["L0_ffn_w_down"].reshape(8, D, 4, P).transpose(3, 0, 2, 1).reshape(P, 32, D))
    a["L1_ffn_wr"] = c(inp["L1_ffn_gate_w"].T)
    a["L1_ffn_wu"] = c(inp["L1_ffn_mlp1_w"][:, 0::2, :].transpose(2, 0, 1))
    a["L1_ffn_bu"] = c(inp["L1_ffn_mlp1_b"][:, 0::2].T)
    a["L1_ffn_wd"] = c(inp["L1_ffn_mlp2_w"].transpose(2, 0, 1))
    a["pos"] = np.arange(S, dtype=np.float32)
    a["part"] = np.arange(P, dtype=np.float32)[:, None]
    a["slot"] = (np.arange(P) % BT * S).astype(np.float32)[:, None]
    d = np.arange(S)[:, None] - np.arange(S)[None, :]
    a["decay"] = np.kron(np.eye(BT), np.where(d >= 0, PATCH_DECAY ** np.maximum(d, 0.0), 0.0)).astype(np.float32)
    a["ctx"] = c(inp["ctx_2048"])
    for layer in (1, 3):
        a[f"L{layer}_xattn_wT"] = c(inp[f"L{layer}_xattn_W_in"].T)
    a["L1_attn_w_in"] = c(inp["L1_attn_in_proj_w"].T.reshape(D, 4, P))
    a["L1_attn_w_conv"] = c(inp["L1_attn_conv_weight"].reshape(2, P, 4).transpose(1, 0, 2))
    a["L1_attn_b_conv"] = c(inp["L1_attn_conv_bias"].reshape(2, P).T)
    a["L1_attn_d_skip"] = c(inp["L1_attn_D"].reshape(2, P).T)
    mean = np.full((16, 2 * P), 1.0 / (2 * P), np.float32)
    dbc = np.stack([inp["L1_attn_delta_w"], inp["L1_attn_B_w"], inp["L1_attn_C_w"], mean])
    a["L1_attn_w_dbc"] = c(dbc.reshape(4, 16, 2, P).transpose(3, 2, 0, 1))
    a["L1_attn_w_out"] = c(inp["L1_attn_out_proj_w"].T.reshape(2, P, D).transpose(1, 0, 2))
    w = np.stack([inp["L2_attn_Wr"], inp["L2_attn_Wk"], inp["L2_attn_Wv"]])
    a["L2_attn_w_rkv"] = c(w.transpose(2, 0, 1))
    a["L2_attn_w_out"] = c(inp["L2_attn_Wo"].T)
    a["L2_attn_wfk"] = c(inp["L2_attn_Wfk"].T.reshape(D, 4, P))
    a["L2_attn_wfv"] = c(inp["L2_attn_Wfv"].T.reshape(4, P, D).transpose(1, 0, 2))
    a["L2_attn_wfr"] = c(inp["L2_attn_Wfr"].T)
    a["L2_ffn_w_qkv"] = c(inp["L2_ffn_in_proj_w"].T.reshape(D, 3, D))
    a["L2_ffn_out_wT"] = c(inp["L2_ffn_out_w"].T)
    a["L2_ffn_wr"] = c(inp["L2_ffn_router_w"].T)
    a["L2_ffn_wu"] = c(inp["L2_ffn_w1"].transpose(2, 0, 1))
    a["L2_ffn_bu"] = c(inp["L2_ffn_b1"].T)
    a["L2_ffn_wd"] = c(inp["L2_ffn_w2"].transpose(2, 0, 1))
    a["ctxT"] = c(inp["ctx_2048"].transpose(0, 2, 1))
    a["ctx_last"] = c(inp["ctx_2048"][:, KEYS - 1, :])
    a["ctx_lastT"] = c(inp["ctx_2048"][:, KEYS - 1, :].T)
    a["L0_xattn_wqT"] = c(inp["L0_xattn_Wq"].reshape(D, H16, 64).transpose(2, 1, 0))
    wkv = inp["L0_xattn_Wkv"].reshape(C, 2, H16, 64).transpose(1, 3, 2, 0)
    a["L0_xattn_wkT"], a["L0_xattn_wvT"] = c(wkv[0]), c(wkv[1])
    a["L0_xattn_wo"] = c(inp["L0_xattn_Wout"].reshape(H16, 64, D).transpose(1, 0, 2))
    a["L0_xattn_nullT"] = c(inp["L0_xattn_null_kv"].T)
    w = inp["L2_xattn_w_qkv"].T
    a["L2_xattn_w_qk"] = c(w[:, 0:2 * D].reshape(D, 2, D))
    a["L2_xattn_w_v"] = c(w[:, 2 * D:])
    a["L2_xattn_w_projT"] = c(inp["L2_xattn_w_proj"].T.reshape(4, 4, DH, D).transpose(1, 0, 2, 3).reshape(D, D))

    def doubled(w, bias):
        order = np.concatenate([np.tile(np.arange(r * S, r * S + S), 2) for r in range(4)])
        return w.T[:, order].reshape(D, 2, P), bias[order].reshape(2, P).T

    wk, bk = doubled(inp["L0_attn_Wk"], inp["L0_attn_bk"])
    wq, bq = doubled(inp["L0_attn_Wq"], inp["L0_attn_bq"])
    a["L0_attn_w_kq"] = c(np.concatenate([wk, wq], 1))
    a["L0_attn_b_kq"] = c(np.concatenate([bk, bq], 1))
    a["L0_attn_w_tok"] = c(np.concatenate([inp["L0_attn_Wq"].T, inp["L0_attn_Wk"].T, inp["L0_attn_Wv"].T], 1))
    a["L0_attn_b_tok"] = c(np.concatenate([inp["L0_attn_bq"], inp["L0_attn_bk"], inp["L0_attn_bv"]]))
    a["L0_attn_WoT"] = c(inp["L0_attn_Wo"].T)
    a["L0_attn_temperature"] = c(inp["L0_attn_temperature"]).reshape(1)
    qkv = inp["L3_attn_W_qkv"].T
    a["L3_attn_w_qk"] = c(qkv[:, 0:2 * D].reshape(D, 2, D))
    a["L3_attn_w_v"] = c(qkv[:, 2 * D:])
    a["L3_attn_w_outT"] = c(inp["L3_attn_W_out"].T)
    dist = np.clip(np.arange(S)[None, :] - np.arange(S)[:, None], -128, 128) + 128
    rel = inp["L3_attn_rel_emb"][dist].transpose(0, 2, 1).reshape(S, 4, 4 * S)
    a["L3_attn_bias"] = c(np.tile(rel, (BT, 1, 1)))
    part = np.arange(P)
    a["own_head"] = (part[:, None] // DH % 4 == np.arange(4)).astype(np.float32)
    a["own_batch"] = (part[:, None] // S == np.arange(4)).astype(np.float32)
    a["L3_ffn_wu"] = c(inp["L3_ffn_W1"].T.reshape(D, 4, P))
    a["L3_ffn_bu"] = c(inp["L3_ffn_b1"].reshape(4, P).T)
    a["L3_ffn_wd"] = c(inp["L3_ffn_W2"].T.reshape(4, P, D).transpose(1, 0, 2))
    return a


def build(nc, arrays, phases=None):
    args = {n: nc.dram_tensor(f"in_{n}", a.shape, mybir.dt.from_np(a.dtype), kind="ExternalInput").ap()
            for n, a in arrays.items()}
    out = nc.dram_tensor("out_x", (TOK, D), F32, kind="ExternalOutput").ap()
    program(nc, args, out, phases)


def kernel(**inputs):
    from concourse import bacc
    from concourse.bass_utils import run_bass_kernel_spmd

    arrays = layout({n: np.asarray(v) for n, v in inputs.items()})
    nc = bacc.Bacc("TRN2", target_bir_lowering=False, num_devices=1)
    build(nc, arrays)
    r = run_bass_kernel_spmd(nc, [{f"in_{n}": a for n, a in arrays.items()}], core_ids=[0])
    return r.results[0]["out_x"].reshape(B, S, D)
```

```python
from contextlib import ExitStack

import numpy as np

import concourse.bass as bass
from concourse import mybir

ALU = mybir.AluOpType
ACT = mybir.ActivationFunctionType
F32 = mybir.dt.float32
I32 = mybir.dt.int32
AX = mybir.AxisListType.X
ds = bass.ds

B, S, D = 128, 32, 128
TOK = B * S
P = 128
TILES = TOK // P
BT = P // S
CHUNK = 512
TC = CHUNK // P
CHUNKS = TOK // CHUNK
BC = CHUNK // S
KEYS = 257
C = 256
H16 = 16
DH = 8
EPS = 1e-5
LOG_TINY = -87.33654
LOG_PASS = -1e-3
PATCH_DECAY = float(-np.expm1(LOG_PASS))
PATCH_GAIN = float(np.exp(LOG_PASS))


class Chain:

    def __init__(self, eng, sem, base=0, per=None):
        self.eng, self.sem, self.base, self.per, self.n = eng, sem, base, per, 0

    def __call__(self, ins):
        self.n += 1
        ins.then_inc(self.sem, 1)
        self.eng.wait_ge(self.sem, self.base + self.n)

    def done(self):
        assert self.per is None or self.n == self.per, f"chain {self.sem} has {self.n} links, not {self.per}"


class Core:

    def __init__(self, nc, ctx, args):
        self.nc, self.ctx, self.a = nc, ctx, args

        self.sems = []

    def sem(self, name):
        self.sems.append(self.nc.alloc_semaphore(name=name))
        return self.sems[-1]


class Stage(ExitStack):

    def __init__(self, k):
        super().__init__()
        self.k = k

    def __exit__(self, *exc):
        super().__exit__(*exc)
        self.k.nc.clear_and_free_semaphores(self.k.sems)
        self.k.nc.all_engine_barrier()
        self.k.sems = []


def buffers(nc, ctx):
    def sb(name, shape, dt=F32):
        return ctx.enter_context(nc.sbuf_tensor(name, list(shape), dt))

    def ps(name, shape):
        return ctx.enter_context(nc.psum_tensor(name, list(shape), F32))

    return sb, ps


def bcast(ap, axis, n):
    ap = ap.unsqueeze(axis)
    shape = list(ap.shape)
    shape[axis] = n
    return ap.broadcast_to(shape)



def normalise(k, name, src, gain=None, bias=None, twice=False, keep=None,
              add_to=None, residual=False, whole=False, eps=EPS):
    nc = k.nc
    ctx = Stage(k)
    with ctx:
        sb, ps = buffers(nc, ctx)
        stats = sb(f"{name}_stats", [P, TILES, 6])
        mean = sb(f"{name}_mean", [P, TILES])
        diff = sb(f"{name}_diff", [P, TILES])
        var = sb(f"{name}_var", [P, TILES])
        var2 = sb(f"{name}_var2", [P, TILES])
        rstd = sb(f"{name}_rstd", [P, TILES])
        rstd2 = sb(f"{name}_rstd2", [P, TILES])
        total = sb(f"{name}_total", [P, TILES])
        expo = sb(f"{name}_expo", [P, TILES])
        cols = sb(f"{name}_cols", [P, 2])
        rows = sb(f"{name}_rows", [P, 2, D])
        xn = sb(f"{name}_xn", [P, 2, TC, D])
        once = sb(f"{name}_once", [P, 2, TC, D])
        psT = ps(f"{name}_psT", [P, 2, CHUNK])

        loaded = k.sem(f"{name}_loaded")
        expo_set = k.sem(f"{name}_expo_set")
        stats_done = k.sem(f"{name}_stats_done")
        link = k.sem(f"{name}_link")
        var_done = k.sem(f"{name}_var_done")
        rstd_done = k.sem(f"{name}_rstd_done")
        var2_done = k.sem(f"{name}_var2_done")
        rstd2_done = k.sem(f"{name}_rstd2_done")
        applied = k.sem(f"{name}_applied")
        turned = k.sem(f"{name}_turned")
        stored = k.sem(f"{name}_stored")
        kept = k.sem(f"{name}_kept")
        affine_done = k.sem(f"{name}_affine_done")
        res_ready = k.sem(f"{name}_res_ready")
        res_added = k.sem(f"{name}_res_added")
        FREE = 2
        RUN = 4
        HALF = TC * RUN
        by_rows = add_to is not None or whole
        by_cols = gain is not None and not by_rows
        ADD_LINKS = RUN * (1 if whole else 3)

        with nc.Block() as block:
            @block.sync
            def _(sp):
                if by_rows:
                    sp.dma_start(rows[:, 0, :], k.a[gain].unsqueeze(0).broadcast_to([P, D])).then_inc(loaded, 16)
                    sp.dma_start(rows[:, 1, :], k.a[bias].unsqueeze(0).broadcast_to([P, D])).then_inc(loaded, 16)
                elif gain:
                    sp.dma_start(cols[:, 0:1], k.a[gain].unsqueeze(1)).then_inc(loaded, 16)
                    if bias:
                        sp.dma_start(cols[:, 1:2], k.a[bias].unsqueeze(1)).then_inc(loaded, 16)

            @block.vector
            def _(v):
                with v.Fori(0, 2) as h:
                    for t in range(HALF):
                        v.bn_stats(stats[:, ds(h * HALF + t, 1), :],
                                   src[:, ds((h * HALF + t) * D, D)]).then_inc(stats_done, 1)
                    v.wait_ge(stats_done, (h + 1) * HALF)
                    ln = Chain(v, link, h * 7, 7)
                    part = ds(h * HALF, HALF)
                    st = stats[:, part, :]
                    ln(v.tensor_tensor(mean[:, part], st[:, :, 1], st[:, :, 4], ALU.add))
                    ln(v.tensor_scalar(mean[:, part], mean[:, part], 0.5, None, ALU.mult))
                    ln(v.tensor_tensor(diff[:, part], st[:, :, 1], st[:, :, 4], ALU.subtract))
                    ln(v.tensor_tensor(diff[:, part], diff[:, part], diff[:, part], ALU.mult))
                    ln(v.tensor_tensor(var[:, part], st[:, :, 2], st[:, :, 5], ALU.add))
                    ln(v.tensor_scalar(var[:, part], var[:, part], 1.0 / D, None, ALU.mult))
                    ln(v.scalar_tensor_tensor(out=var[:, part], in0=diff[:, part], scalar=0.25, in1=var[:, part],
                                              op0=ALU.mult, op1=ALU.add))
                    ln.done()
                    v.tensor_scalar(var2[:, part], var[:, part], eps, None, ALU.add).then_inc(var_done, 1)
                links = 14
                if twice:
                    with v.Fori(0, 2) as h:
                        ln = Chain(v, link, links + h * 2, 2)
                        part = ds(h * HALF, HALF)
                        v.wait_ge(rstd_done, h + 1)
                        ln(v.tensor_tensor(diff[:, part], rstd[:, part], rstd[:, part], ALU.mult))
                        ln(v.tensor_tensor(diff[:, part], diff[:, part], var[:, part], ALU.mult))
                        ln.done()
                        v.tensor_scalar(var2[:, part], diff[:, part], EPS, None, ALU.add).then_inc(var2_done, 1)
                    links += 4
                scale = total if twice else rstd
                if by_rows:
                    v.wait_ge(loaded, 32)
                with v.Fori(0, CHUNKS // RUN) as i:
                    if twice:
                        v.wait_ge(rstd2_done, i + 1)
                        part = ds(i * HALF, HALF)
                        both = Chain(v, link, links + i * (1 + (ADD_LINKS if by_rows else 0)), 1)
                        both(v.tensor_tensor(total[:, part], rstd[:, part], rstd2[:, part], ALU.mult))
                        add = Chain(v, link, links + 1 + i * (1 + ADD_LINKS), ADD_LINKS)
                    else:
                        v.wait_ge(rstd_done, i + 1)
                        add = Chain(v, link, links + i * ADD_LINKS, ADD_LINKS)
                    for b in range(RUN):
                        if add_to is None:
                            v.wait_ge(turned, i * RUN + b + 1)
                        if whole:
                            v.wait_ge(kept, i * RUN + b + 1)
                        for t in range(TC):
                            n = (i * RUN + b) * TC + t
                            v.tensor_scalar(xn[:, b % 2, t, :], src[:, ds(n * D, D)], mean[:, ds(n, 1)],
                                            scale[:, ds(n, 1)], ALU.subtract, ALU.mult).then_inc(applied, 1)
                            if residual:
                                if t == 0:
                                    v.wait_ge(res_added, i * RUN + b + 1)
                                v.tensor_scalar(once[:, b % 2, t, :], src[:, ds(n * D, D)], mean[:, ds(n, 1)],
                                                rstd[:, ds(n, 1)], ALU.subtract, ALU.mult).then_inc(res_ready, 1)
                            if keep is not None and not whole:
                                v.tensor_scalar(keep[:, ds(n * D, D)], src[:, ds(n * D, D)], mean[:, ds(n, 1)],
                                                rstd[:, ds(n, 1)], ALU.subtract, ALU.mult).then_inc(kept, 1)
                        if whole:
                            v.wait_ge(applied, ((i * RUN + b) + 1) * TC)
                            add(v.tensor_tensor(xn[:, b % 2], xn[:, b % 2], bcast(rows[:, 0, :], 1, TC), ALU.mult))
                            v.tensor_tensor(xn[:, b % 2], xn[:, b % 2], bcast(rows[:, 1, :], 1, TC),
                                            ALU.add).then_inc(affine_done, 1)
                        if add_to is not None:
                            v.wait_ge(applied, ((i * RUN + b) + 1) * TC)
                            at = add_to[:, ds((i * RUN + b) * CHUNK, CHUNK)].rearrange("p (t d) -> p t d", t=TC)
                            add(v.tensor_tensor(xn[:, b % 2], xn[:, b % 2], bcast(rows[:, 0, :], 1, TC), ALU.mult))
                            add(v.tensor_tensor(xn[:, b % 2], xn[:, b % 2], bcast(rows[:, 1, :], 1, TC), ALU.add))
                            add(v.tensor_tensor(at, at, xn[:, b % 2], ALU.add))
                    if by_rows:
                        add.done()

            @block.gpsimd
            def _(g):
                g.memset(expo[:], -0.5).then_inc(expo_set, 1)
                g.wait_ge(expo_set, 1)
                with g.Fori(0, 2) as h:
                    part = ds(h * HALF, HALF)
                    g.wait_ge(var_done, h + 1)
                    g.tensor_tensor(rstd[:, part], var2[:, part], expo[:, part], ALU.pow).then_inc(rstd_done, 1)
                if twice:
                    with g.Fori(0, 2) as h:
                        part = ds(h * HALF, HALF)
                        g.wait_ge(var2_done, h + 1)
                        g.tensor_tensor(rstd2[:, part], var2[:, part], expo[:, part], ALU.pow)\
                            .then_inc(rstd2_done, 1)
                if whole:
                    g.sem_inc(kept, FREE)
                    with g.Fori(0, CHUNKS // RUN) as i:
                        for b in range(RUN):
                            g.wait_ge(affine_done, i * RUN + b + 1)
                            g.tensor_copy(keep[:, ds((i * RUN + b) * CHUNK, CHUNK)],
                                          xn[:, b % 2].rearrange("p t d -> p (t d)")).then_inc(kept, 1)
                if residual:
                    g.sem_inc(res_added, FREE)
                    with g.Fori(0, CHUNKS // RUN) as i:
                        for b in range(RUN):
                            g.wait_ge(res_ready, (i * RUN + b + 1) * TC)
                            at = src[:, ds((i * RUN + b) * CHUNK, CHUNK)]
                            g.tensor_tensor(at, at, once[:, b % 2].rearrange("p t d -> p (t d)"),
                                            ALU.add).then_inc(res_added, 1)

            if add_to is None:
                @block.tensor
                def _(pe):
                    pe.sem_inc(turned, FREE)
                    with pe.Fori(0, CHUNKS // RUN) as i:
                        for b in range(RUN):
                            pe.wait_ge(affine_done if whole else applied, (i * RUN + b + 1) * (1 if whole else TC))
                            pe.wait_ge(stored, i * RUN + b + 1)
                            for t in range(TC):
                                mm = pe.transpose(psT[:, b % 2, t * P:(t + 1) * P], xn[:, b % 2, t, :], k.ident[:])
                            mm.then_inc(turned, 1)

                @block.scalar
                def _(act):
                    act.sem_inc(stored, FREE)
                    if by_cols:
                        act.wait_ge(loaded, 32 if bias else 16)
                    with act.Fori(0, CHUNKS // RUN) as i:
                        for b in range(RUN):
                            act.wait_ge(turned, i * RUN + b + 1 + FREE)
                            act.activation(k.XT[:, ds((i * RUN + b) * CHUNK, CHUNK)], psT[:, b % 2, :], ACT.Identity,
                                           scale=cols[:, 0:1] if by_cols else 1.0,
                                           bias=cols[:, 1:2] if by_cols and bias else 0.0).then_inc(stored, 1)



def route(v, ln, logits, tri, gt, eq, rank, mask, top, experts):
    other = bcast(logits, 2, experts)
    own = bcast(logits, 3, experts)
    ln(v.tensor_tensor(gt, other, own, ALU.is_gt))
    ln(v.tensor_tensor(eq, other, own, ALU.is_equal))
    ln(v.tensor_tensor(eq, eq, bcast(tri, 1, TC), ALU.mult))
    ln(v.tensor_tensor(gt, gt, eq, ALU.add))
    ln(v.tensor_reduce(rank, gt, AX, ALU.add))
    ln(v.tensor_scalar(mask, rank, float(top), None, ALU.is_lt))


def mixture(k, name, E, UT, dest, kind, wr, br, wu, bu, wd, bd):
    nc = k.nc
    ctx = Stage(k)
    top = 4 if kind == "swiglu4" else 2
    N = E * UT
    BANKS = 4
    SLOTS = 8
    HELD = SLOTS // UT
    LAG = 1 if UT == 4 else 2
    YB = 2
    LINKS = {"gelu2": 12, "swiglu4": 13, "assign": 15}[kind]
    with ctx:
        sb, ps = buffers(nc, ctx)
        w_up = sb(f"{name}_w_up", [P, N, P])
        w_down = sb(f"{name}_w_down", [P, N, D])
        w_rt = sb(f"{name}_w_rt", [P, E])
        b_up = sb(f"{name}_b_up", [P, N])
        b_down = sb(f"{name}_b_down", [E, D])
        b_rt = sb(f"{name}_b_rt", [P, E])
        tri = sb(f"{name}_tri", [P, E, E])
        index = sb(f"{name}_index", [P, E])
        xs = sb(f"{name}_xs", [P, 2, CHUNK])
        hT = sb(f"{name}_hT", [P, SLOTS, CHUNK])
        clamped = sb(f"{name}_clamped", [P, 2, CHUNK])
        sig = sb(f"{name}_sig", [P, 2, CHUNK])
        lg = sb(f"{name}_lg", [P, TC, E])
        pr = sb(f"{name}_pr", [P, TC, E])
        gt = sb(f"{name}_gt", [P, TC, E, E])
        eq = sb(f"{name}_eq", [P, TC, E, E])
        rank = sb(f"{name}_rank", [P, TC, E])
        mask = sb(f"{name}_mask", [P, TC, E])
        mx = sb(f"{name}_mx", [P, TC])
        tot = sb(f"{name}_tot", [P, TC])
        wt = sb(f"{name}_wt", [P, 2, TC, E])
        wt8 = sb(f"{name}_wt8", [P, 2, TC, E])
        wtT = sb(f"{name}_wtT", [E, CHUNK])
        psH = ps(f"{name}_psH", [P, BANKS, CHUNK])
        psY = ps(f"{name}_psY", [P, YB, CHUNK])
        psR = ps(f"{name}_psR", [P, CHUNK])
        psB = ps(f"{name}_psB", [P, CHUNK])

        loaded = k.sem(f"{name}_loaded")
        xs_ready = k.sem(f"{name}_xs_ready")
        logits_ready = k.sem(f"{name}_logits_ready")
        shifted = k.sem(f"{name}_shifted")
        exp_done = k.sem(f"{name}_exp_done")
        weights_ready = k.sem(f"{name}_weights_ready")
        weights_turned = k.sem(f"{name}_weights_turned")
        weightsT_ready = k.sem(f"{name}_weightsT_ready")
        bias_summed = k.sem(f"{name}_bias_summed")
        bias_added = k.sem(f"{name}_bias_added")
        up_done = k.sem(f"{name}_up_done")
        clamp_done = k.sem(f"{name}_clamp_done")
        sigmoid_done = k.sem(f"{name}_sigmoid_done")
        act_done = k.sem(f"{name}_act_done")
        down_done = k.sem(f"{name}_down_done")
        mixed = k.sem(f"{name}_mixed")
        link = k.sem(f"{name}_link")
        LOADS = 7 + (br is not None)
        swiglu = kind == "swiglu4"
        ACT_FREE = 2 if swiglu else BANKS

        with nc.Block() as block:
            @block.sync
            def _(sp):
                sp.dma_start(w_rt[:], k.a[wr]).then_inc(loaded, 16)
                sp.dma_start(tri[:], k.a[f"tri{E}"].partition_broadcast(P)).then_inc(loaded, 16)
                sp.dma_start(index[:], k.a[f"index{E}"].partition_broadcast(P)).then_inc(loaded, 16)
                sp.dma_start(b_up[:], k.a[bu]).then_inc(loaded, 16)
                sp.dma_start(b_down[:], k.a[bd]).then_inc(loaded, 16)
                if br:
                    sp.dma_start(b_rt[:], k.a[br].partition_broadcast(P)).then_inc(loaded, 16)
                sp.dma_start(w_up[:], k.a[wu]).then_inc(loaded, 16)
                sp.dma_start(w_down[:], k.a[wd]).then_inc(loaded, 16)

            @block.gpsimd
            def _(g):
                if swiglu:
                    g.sem_inc(act_done, ACT_FREE)
                with g.Fori(0, CHUNKS // 2) as i:
                    for b in range(2):
                        c = i * 2 + b
                        g.wait_ge(logits_ready, c)
                        g.tensor_copy(xs[:, b, :], k.XT[:, ds(c * CHUNK, CHUNK)]).then_inc(xs_ready, 1)
                        for n in range(N if swiglu else 0):
                            g.wait_ge(sigmoid_done, c * N + n + 1)
                            g.wait_ge(down_done, c * E + n // UT + 1)
                            g.tensor_tensor(hT[:, n % SLOTS, :], clamped[:, n % 2, :], sig[:, n % 2, :],
                                            ALU.mult).then_inc(act_done, 1)

            @block.tensor
            def _(pe):
                pe.sem_inc(down_done, HELD)
                pe.wait_ge(loaded, LOADS * 16)
                with pe.Fori(0, CHUNKS // 2) as i:
                    for b in range(2):
                        c = i * 2 + b
                        pe.wait_ge(xs_ready, c + 1)
                        for t in range(TC):
                            mm = pe.matmul(psR[:, t * E:(t + 1) * E], xs[:, b, t * P:(t + 1) * P], w_rt[:],
                                           start=True, stop=True)
                        mm.then_inc(logits_ready, 1)

                        def up(e):
                            for u in range(UT):
                                n = e * UT + u
                                pe.wait_ge(clamp_done if swiglu else act_done, c * N + n + 1)
                                pe.matmul(psH[:, n % BANKS, :], w_up[:, n, :], xs[:, b, :],
                                          start=True, stop=True).then_inc(up_done, 1)

                        def down(e):
                            pe.wait_ge(act_done, c * N + (e + 1) * UT + ACT_FREE)
                            pe.wait_ge(mixed, c * E + e + 1)
                            for t in range(TC):
                                for u in range(UT):
                                    n = e * UT + u
                                    mm = pe.matmul(psY[:, e % YB, t * P:(t + 1) * P],
                                                   hT[:, n % SLOTS, t * P:(t + 1) * P], w_down[:, n, :],
                                                   start=(u == 0), stop=(u == UT - 1))
                            mm.then_inc(down_done, 1)

                        for e in range(E + LAG):
                            if e < E:
                                up(e)
                            if e >= LAG:
                                down(e - LAG)
                            if e == LAG + 1:
                                pe.wait_ge(weights_ready, c + 1)
                                for t in range(TC):
                                    mm = pe.transpose(psR[0:E, t * P:(t + 1) * P], wt[:, b, t, :], k.ident[:])
                                mm.then_inc(weights_turned, 1)
                            if e == LAG + 2:
                                pe.wait_ge(weightsT_ready, c + 1)
                                for t in range(TC):
                                    mm = pe.matmul(psB[:, t * P:(t + 1) * P], wtT[:, t * P:(t + 1) * P],
                                                   b_down[:], start=True, stop=True)
                                mm.then_inc(bias_summed, 1)

            @block.scalar
            def _(act):
                if not swiglu:
                    act.sem_inc(act_done, ACT_FREE)
                act.wait_ge(loaded, LOADS * 16)
                with act.Fori(0, CHUNKS // 2) as i:
                    for b in range(2):
                        c = i * 2 + b
                        act.wait_ge(shifted, c + 1)
                        act.activation(pr[:], lg[:], ACT.Exp).then_inc(exp_done, 1)
                        for n in range(N):
                            if swiglu:
                                act.wait_ge(clamp_done, c * N + n + 1 + BANKS)
                                act.wait_ge(act_done, c * N + n + 1)
                                act.activation(sig[:, n % 2, :], clamped[:, n % 2, :], ACT.Sigmoid,
                                               scale=1.702).then_inc(sigmoid_done, 1)
                            else:
                                act.wait_ge(up_done, c * N + n + 1)
                                act.wait_ge(down_done, c * E + n // UT + 1)
                                act.activation(hT[:, n % SLOTS, :], psH[:, n % BANKS, :], ACT.Gelu,
                                               bias=b_up[:, n:n + 1]).then_inc(act_done, 1)

            @block.vector
            def _(v):
                v.sem_inc(mixed, YB)
                if swiglu:
                    v.sem_inc(clamp_done, BANKS)
                v.wait_ge(loaded, LOADS * 16)
                with v.Fori(0, CHUNKS // 2) as i:
                    for b in range(2):
                        c = i * 2 + b
                        ln = Chain(v, link, c * LINKS, LINKS)
                        v.wait_ge(logits_ready, c + 1)
                        rt = psR[:, 0:TC * E].rearrange("p (t e) -> p t e", t=TC)
                        if br:
                            ln(v.tensor_tensor(lg[:], rt, bcast(b_rt[:], 1, TC), ALU.add))
                        else:
                            ln(v.tensor_copy(lg[:], rt))
                        if kind != "assign":
                            route(v, ln, lg[:], tri[:], gt[:], eq[:], rank[:], mask[:], top, E)
                        ln(v.tensor_reduce(mx[:], lg[:], AX, ALU.max))
                        v.tensor_tensor(lg[:], lg[:], bcast(mx[:], 2, E), ALU.subtract).then_inc(shifted, 1)
                        v.wait_ge(exp_done, c + 1)
                        if kind != "assign":
                            ln(v.tensor_tensor(pr[:], pr[:], mask[:], ALU.mult))
                        else:
                            ln(v.scalar_tensor_tensor(out=pr[:], in0=lg[:], scalar=LOG_TINY, in1=pr[:],
                                                      op0=ALU.is_ge, op1=ALU.mult))
                        ln(v.tensor_reduce(tot[:], pr[:], AX, ALU.add))
                        ln(v.reciprocal(tot[:], tot[:]))
                        if kind == "assign":
                            ln(v.tensor_tensor(pr[:], pr[:], bcast(tot[:], 2, E), ALU.mult))
                            route(v, ln, pr[:], tri[:], gt[:], eq[:], rank[:], mask[:], top, E)
                            ln(v.tensor_tensor(rank[:], mask[:], bcast(index[:], 1, TC), ALU.mult))
                            ln(v.tensor_reduce(mx[:], rank[:], AX, ALU.max))
                            ln(v.tensor_tensor(wt[:, b], bcast(index[:], 1, TC), bcast(mx[:], 2, E), ALU.is_equal))
                        else:
                            ln(v.tensor_tensor(wt[:, b], pr[:], bcast(tot[:], 2, E), ALU.mult))
                        if swiglu:
                            ln(v.tensor_scalar(wt8[:, b], wt[:, b], 8.0, None, ALU.mult))
                        v.tensor_copy(rank[:], wt[:, b]).then_inc(weights_ready, 1)
                        v.wait_ge(weights_ready, c + 1)
                        ln.done()
                        by = wt8 if swiglu else wt

                        def clamp(n):
                            v.wait_ge(up_done, c * N + n + 1)
                            v.wait_ge(act_done, c * N + n + 1)
                            v.tensor_scalar(clamped[:, n % 2, :], psH[:, n % BANKS, :], b_up[:, n:n + 1], 7.0,
                                            ALU.add, ALU.min).then_inc(clamp_done, 1)

                        for e in range(E + LAG):
                            if swiglu and e < E:
                                clamp(e)
                            if e < LAG:
                                continue
                            e -= LAG
                            v.wait_ge(down_done, c * E + e + 1 + HELD)
                            for t in range(TC):
                                at = dest[:, ds(c * CHUNK + t * P, P)]
                                mix = v.scalar_tensor_tensor(
                                    out=at, in0=psY[:, e % YB, t * P:(t + 1) * P],
                                    scalar=by[:, b, t, e:e + 1], in1=at, op0=ALU.mult, op1=ALU.add)
                            mix.then_inc(mixed, 1)
                            v.wait_ge(mixed, c * E + e + 1 + YB)
                            if e == 1:
                                v.wait_ge(weights_turned, c + 1)
                                v.tensor_copy(wtT[:], psR[0:E, :]).then_inc(weightsT_ready, 1)
                            if e == 3:
                                v.wait_ge(bias_summed, c + 1)
                                at = dest[:, ds(c * CHUNK, CHUNK)]
                                v.tensor_tensor(at, psB[:], at, ALU.add).then_inc(bias_added, 1)
                                v.wait_ge(bias_added, c + 1)



def depool(k):
    nc = k.nc
    ctx = Stage(k)
    with ctx:
        sb, ps = buffers(nc, ctx)
        lens_i = sb("dp_lens_i", [P, KEYS], I32)
        lens = sb("dp_lens", [P, KEYS])
        ones = sb("dp_ones", [P, KEYS])
        sums = sb("dp_sums", [P, KEYS])
        wrap = sb("dp_wrap", [P, KEYS])
        hits = sb("dp_hits", [P, S, KEYS])
        pos = sb("dp_pos", [P, S])
        slot = sb("dp_slot", [P, 1])
        part = sb("dp_part", [P, 1])
        bound = sb("dp_bound", [P, S])
        count = sb("dp_count", [P, S])
        plug = sb("dp_plug", [P, S])
        plug_all = sb("dp_plug_all", [P, TOK])
        onehot = sb("dp_onehot", [P, TOK])
        patch = sb("dp_patch", [P, TILES, C])
        square = sb("dp_square", [P, 2, C])
        sumsq = sb("dp_sumsq", [P, TILES])
        expo = sb("dp_expo", [P, TILES])
        rms = sb("dp_rms", [P, TILES])
        hp = sb("dp_hp", [P, TILES * D])
        decay = sb("dp_decay", [P, P])
        mix = sb("dp_mix", [P, 2, CHUNK])
        psG = ps("dp_psG", [P, 2, CHUNK])
        psD = ps("dp_psD", [P, 2, CHUNK])

        loaded = k.sem("dp_loaded")
        patch_loaded = k.sem("dp_patch_loaded")
        ones_set = k.sem("dp_ones_set")
        link = k.sem("dp_link")
        plug_ready = k.sem("dp_plug_ready")
        plug_stored = k.sem("dp_plug_stored")
        plug_spread = k.sem("dp_plug_spread")
        onehot_ready = k.sem("dp_onehot_ready")
        squared = k.sem("dp_squared")
        meansq_ready = k.sem("dp_meansq_ready")
        rms_ready = k.sem("dp_rms_ready")
        hp_ready = k.sem("dp_hp_ready")
        mixed = k.sem("dp_mixed")
        mix_copied = k.sem("dp_mix_copied")
        picked = k.sem("dp_picked")
        stored = k.sem("dp_stored")
        scratch = nc.dram_tensor("dp_plug_dram", (B, S), F32).ap()
        FREE = 2

        with nc.Block() as block:
            @block.sync
            def _(sp):
                sp.dma_start(lens_i[:], k.a["mask_BxS2_if0"]).then_inc(loaded, 16)
                sp.dma_start(pos[:], k.a["pos"].partition_broadcast(P)).then_inc(loaded, 16)
                sp.dma_start(slot[:], k.a["slot"]).then_inc(loaded, 16)
                sp.dma_start(part[:], k.a["part"]).then_inc(loaded, 16)
                sp.dma_start(decay[:], k.a["decay"]).then_inc(loaded, 16)
                for q in range(BT):
                    sp.dma_start(patch[q * S:(q + 1) * S],
                                 k.a["ctx"][q:B:BT, 0:S, :].rearrange("t p c -> p t c")).then_inc(patch_loaded, 16)
                sp.wait_ge(plug_ready, 1)
                sp.dma_start(scratch, plug[:]).then_inc(plug_stored, 16)
                sp.wait_ge(plug_stored, 16)
                sp.dma_start(plug_all[:], scratch.rearrange("b l -> (b l)").partition_broadcast(P))\
                    .then_inc(plug_spread, 16)

            @block.gpsimd
            def _(g):
                g.memset(ones[:], 1.0).then_inc(ones_set, 1)
                g.memset(expo[:], -0.5).then_inc(ones_set, 1)
                g.wait_ge(ones_set, 2)
                g.wait_ge(meansq_ready, 1)
                g.tensor_tensor(rms[:], sumsq[:], expo[:], ALU.pow).then_inc(rms_ready, 1)

            @block.scalar
            def _(act):
                act.wait_ge(patch_loaded, 16 * BT)
                for t in range(TILES):
                    if t >= 2:
                        act.wait_ge(squared, t - 1)
                    act.activation(square[:, t % 2], patch[:, t], ACT.Square,
                                   accum_out=sumsq[:, t:t + 1]).then_inc(squared, 1)
                act.sem_inc(mix_copied, FREE)
                act.sem_inc(stored, FREE)
                with act.Fori(0, CHUNKS // 2) as i:
                    for b in range(2):
                        c = i * 2 + b
                        act.wait_ge(mixed, c + 1)
                        act.wait_ge(picked, c + 1)
                        act.activation(mix[:, b], psG[:, b], ACT.Copy).then_inc(mix_copied, 1)
                        act.wait_ge(picked, c + 1 + FREE)
                        act.activation(k.DR[:, ds(c * CHUNK, CHUNK)], psD[:, b], ACT.Copy).then_inc(stored, 1)

            @block.vector
            def _(v):
                ln = Chain(v, link)
                v.wait_ge(loaded, 16 * 5)
                v.wait_ge(ones_set, 2)
                ln(v.tensor_copy(lens[:], lens_i[:]))
                ln(v.tensor_tensor_scan(sums[:], ones[:], lens[:], 0.0, ALU.mult, ALU.add))
                ln(v.tensor_scalar(sums[:], sums[:], 1.0, None, ALU.subtract))
                ln(v.tensor_scalar(wrap[:], sums[:], 0.0, float(S), ALU.is_lt, ALU.mult))
                ln(v.tensor_tensor(sums[:], sums[:], wrap[:], ALU.add))
                ln(v.tensor_tensor(hits[:], bcast(sums[:], 1, S), bcast(pos[:], 2, KEYS), ALU.is_equal))
                ln(v.tensor_reduce(bound[:], hits[:], AX, ALU.max))
                ln(v.tensor_tensor_scan(count[:], ones[:, 0:S], bound[:], 0.0, ALU.mult, ALU.add))
                ln(v.tensor_scalar(count[:], count[:], 1.0, 0.0, ALU.subtract, ALU.max))
                v.tensor_scalar(plug[:], count[:], slot[:, 0:1], None, ALU.add).then_inc(plug_ready, 1)
                v.wait_ge(squared, TILES)
                v.tensor_scalar(sumsq[:], sumsq[:], 1.0 / C, EPS, ALU.mult, ALU.add).then_inc(meansq_ready, 1)
                v.wait_ge(rms_ready, 1)
                ln(v.tensor_scalar(rms[:], rms[:], PATCH_GAIN, None, ALU.mult))
                for t in range(TILES):
                    v.tensor_scalar(hp[:, t * D:(t + 1) * D], patch[:, t, 0:D], rms[:, t:t + 1], None,
                                    ALU.mult).then_inc(hp_ready, 1)
                v.wait_ge(plug_spread, 16)
                v.tensor_scalar(onehot[:], plug_all[:], part[:, 0:1], None, ALU.is_equal).then_inc(onehot_ready, 1)

            @block.tensor
            def _(pe):
                pe.wait_ge(onehot_ready, 1)
                pe.wait_ge(hp_ready, TILES)
                pe.sem_inc(picked, FREE)
                with pe.Fori(0, CHUNKS // 2) as i:
                    for b in range(2):
                        c = i * 2 + b
                        pe.wait_ge(mix_copied, c + 1)
                        pe.matmul(psG[:, b], decay[:], onehot[:, ds(c * CHUNK, CHUNK)],
                                  start=True, stop=True).then_inc(mixed, 1)
                        pe.wait_ge(mix_copied, c + 1 + FREE)
                        pe.wait_ge(stored, c + 1)
                        for t in range(TC):
                            mm = pe.matmul(psD[:, b, t * P:(t + 1) * P], mix[:, b, t * P:(t + 1) * P],
                                           hp[:, ds(c * CHUNK + t * P, P)], start=True, stop=True)
                        mm.then_inc(picked, 1)


def depooled(k, name, prefix):
    nc = k.nc
    normalise(k, f"{name}n", k.X, gain=f"{prefix}_g_res", twice=True)
    ctx = Stage(k)
    with ctx:
        sb, ps = buffers(nc, ctx)
        w = sb(f"{name}_w", [P, D])
        b_row = sb(f"{name}_b_row", [P, D])
        g_row = sb(f"{name}_g_row", [P, D])
        xs = sb(f"{name}_xs", [P, 2, CHUNK])
        patch = sb(f"{name}_patch", [P, 2, TC, D])
        psP = ps(f"{name}_psP", [P, 2, CHUNK])
        loaded = k.sem(f"{name}_loaded")
        xs_ready = k.sem(f"{name}_xs_ready")
        projected = k.sem(f"{name}_projected")
        scaled = k.sem(f"{name}_scaled")
        patch_ready = k.sem(f"{name}_patch_ready")
        summed = k.sem(f"{name}_summed")
        added = k.sem(f"{name}_added")
        FREE = 2
        with nc.Block() as block:
            @block.sync
            def _(sp):
                sp.dma_start(w[:], k.a[f"{prefix}_wT"]).then_inc(loaded, 16)
                sp.dma_start(b_row[:], k.a[f"{prefix}_b_in"].partition_broadcast(P)).then_inc(loaded, 16)
                sp.dma_start(g_row[:], k.a[f"{prefix}_g_init"][0:D].partition_broadcast(P)).then_inc(loaded, 16)

            @block.scalar
            def _(act):
                act.sem_inc(xs_ready, FREE)
                with act.Fori(0, CHUNKS // 2) as i:
                    for b in range(2):
                        c = i * 2 + b
                        act.wait_ge(projected, c + 1)
                        act.activation(xs[:, b, :], k.XT[:, ds(c * CHUNK, CHUNK)], ACT.Copy).then_inc(xs_ready, 1)

            @block.tensor
            def _(pe):
                pe.sem_inc(projected, FREE)
                pe.wait_ge(loaded, 48)
                with pe.Fori(0, CHUNKS // 2) as i:
                    for b in range(2):
                        c = i * 2 + b
                        pe.wait_ge(xs_ready, c + 1 + FREE)
                        pe.wait_ge(added, c + 1)
                        for t in range(TC):
                            mm = pe.matmul(psP[:, b, t * P:(t + 1) * P], xs[:, b, t * P:(t + 1) * P], w[:],
                                           start=True, stop=True)
                        mm.then_inc(projected, 1)

            @block.gpsimd
            def _(g):
                g.wait_ge(loaded, 48)
                with g.Fori(0, CHUNKS // 2) as i:
                    for b in range(2):
                        c = i * 2 + b
                        g.wait_ge(added, c + 1)
                        at = k.DR[:, ds(c * CHUNK, CHUNK)].rearrange("p (t d) -> p t d", t=TC)
                        g.tensor_tensor(patch[:, b], at, bcast(g_row[:], 1, TC), ALU.mult).then_inc(scaled, 1)
                        g.wait_ge(scaled, c + 1)
                        g.tensor_tensor(patch[:, b], patch[:, b], bcast(b_row[:], 1, TC),
                                        ALU.add).then_inc(patch_ready, 1)

            @block.vector
            def _(v):
                v.sem_inc(added, FREE)
                with v.Fori(0, CHUNKS // 2) as i:
                    for b in range(2):
                        c = i * 2 + b
                        v.wait_ge(patch_ready, c + 1)
                        v.wait_ge(projected, c + 1 + FREE)
                        rows = patch[:, b].rearrange("p t d -> p (t d)")
                        v.tensor_tensor(rows, rows, psP[:, b], ALU.add).then_inc(summed, 1)
                        v.wait_ge(summed, c + 1)
                        at = k.X[:, ds(c * CHUNK, CHUNK)]
                        v.tensor_tensor(at, at, rows, ALU.add).then_inc(added, 1)



def layer1_attn(k):
    nc = k.nc
    normalise(k, "n1a", k.X)
    ctx = Stage(k)
    NS = 16
    LINKS = 6
    with ctx:
        sb, ps = buffers(nc, ctx)
        w_in = sb("m_w_in", [P, 4, P])
        w_conv = sb("m_w_conv", [P, 2, 4])
        b_conv = sb("m_b_conv", [P, 2])
        d_skip = sb("m_d_skip", [P, 2])
        w_dbc = sb("m_w_dbc", [P, 2, 4, NS])
        b_delta = sb("m_b_delta", [NS, 1])
        a_log = sb("m_a_log", [NS, 1])
        a_neg = sb("m_a_neg", [NS, 1])
        w_out = sb("m_w_out", [P, 2, D])
        ones = sb("m_ones", [NS, P])
        conv = sb("m_conv", [P, 2, CHUNK])
        xconv = sb("m_xconv", [P, 2, 2, CHUNK])
        gate = sb("m_gate", [P, 2, 2, CHUNK])
        gated = sb("m_gated", [P, 2, CHUNK])
        z = sb("m_z", [NS, CHUNK])
        absz = sb("m_absz", [NS, CHUNK])
        soft = sb("m_soft", [NS, CHUNK])
        delta = sb("m_delta", [NS, CHUNK])
        dA = sb("m_dA", [NS, CHUNK])
        dB = sb("m_dB", [NS, CHUNK])
        hs = sb("m_hs", [NS, CHUNK])
        hc = sb("m_hc", [NS, CHUNK])
        psI = ps("m_psI", [P, 4, CHUNK])
        psS = ps("m_psS", [P, 4, CHUNK])

        loaded = k.sem("m_loaded")
        ones_set = k.sem("m_ones_set")
        a_ready = k.sem("m_a_ready")
        projected = k.sem("m_projected")
        conv_done = k.sem("m_conv_done")
        gate_done = k.sem("m_gate_done")
        xconv_done = k.sem("m_xconv_done")
        states_in = k.sem("m_states_in")
        z_ready = k.sem("m_z_ready")
        abs_done = k.sem("m_abs_done")
        exp_done = k.sem("m_exp_done")
        log_done = k.sem("m_log_done")
        delta_ready = k.sem("m_delta_ready")
        decay_ready = k.sem("m_decay_ready")
        read_out = k.sem("m_read_out")
        spread = k.sem("m_spread")
        gated_ready = k.sem("m_gated_ready")
        out_done = k.sem("m_out_done")
        added = k.sem("m_added")
        link = k.sem("m_link")
        conv_link = k.sem("m_conv_link")
        FREE = 4

        with nc.Block() as block:
            @block.sync
            def _(sp):
                for to, name in ((w_in, "L1_attn_w_in"), (w_conv, "L1_attn_w_conv"), (b_conv, "L1_attn_b_conv"),
                                 (d_skip, "L1_attn_d_skip"), (w_dbc, "L1_attn_w_dbc"), (w_out, "L1_attn_w_out")):
                    sp.dma_start(to[:], k.a[name]).then_inc(loaded, 16)
                sp.dma_start(b_delta[:], k.a["L1_attn_delta_b"].unsqueeze(1)).then_inc(loaded, 16)
                sp.dma_start(a_log[:], k.a["L1_attn_A_log"].unsqueeze(1)).then_inc(loaded, 16)

            @block.gpsimd
            def _(g):
                g.memset(ones[:], 1.0).then_inc(ones_set, 1)

            @block.tensor
            def _(pe):
                pe.wait_ge(loaded, 128)
                pe.wait_ge(ones_set, 1)

                def project(j):
                    pe.wait_ge(conv_done, j * 2)
                    pe.wait_ge(gate_done, j * 2)
                    for f in range(4):
                        pe.matmul(psI[:, f], w_in[:, f], k.XT[:, ds(j * CHUNK, CHUNK)],
                                  start=True, stop=True).then_inc(projected, 1)

                def states(j, p):
                    pe.wait_ge(xconv_done, j * 2 + 2)
                    pe.wait_ge(added, j)
                    for g in range(4):
                        for f in range(2):
                            mm = pe.matmul(psS[0:NS, g], w_dbc[:, f, g], xconv[:, p, f], start=(f == 0), stop=(f == 1))
                    mm.then_inc(states_in, 1)

                def output(j):
                    pe.wait_ge(read_out, j + 1)
                    pe.matmul(psS[:, 0], ones[:], hc[:], start=True, stop=True).then_inc(spread, 1)
                    pe.wait_ge(gated_ready, j * 2 + 2 + FREE)
                    for t in range(TC):
                        for f in range(2):
                            mm = pe.matmul(psS[:, 1, t * P:(t + 1) * P], gated[:, f, t * P:(t + 1) * P], w_out[:, f],
                                           start=(f == 0), stop=(f == 1))
                    mm.then_inc(out_done, 1)

                project(0)
                with pe.Fori(0, CHUNKS // 2 - 1) as i:
                    for p in range(2):
                        states(i * 2 + p, p)
                        project(i * 2 + p + 1)
                        output(i * 2 + p)
                states(CHUNKS - 2, 0)
                project(CHUNKS - 1)
                output(CHUNKS - 2)
                states(CHUNKS - 1, 1)
                output(CHUNKS - 1)

            @block.scalar
            def _(act):
                act.wait_ge(loaded, 128)
                act.activation(a_neg[:], a_log[:], ACT.Exp).then_inc(a_ready, 1)
                act.wait_ge(a_ready, 2)

                def inputs(j, p):
                    for f in range(2):
                        act.wait_ge(projected, j * 4 + f + 3)
                        act.wait_ge(gated_ready, j * 2 + FREE - 2)
                        act.activation(gate[:, p, f], psI[:, 2 + f], ACT.Silu).then_inc(gate_done, 1)
                    for f in range(2):
                        act.wait_ge(conv_done, j * 2 + f + 1)
                        act.activation(xconv[:, p, f], conv[:, f], ACT.Silu).then_inc(xconv_done, 1)

                def softplus(j):
                    act.wait_ge(z_ready, j + 1)
                    act.activation(absz[:], z[:], ACT.Abs).then_inc(abs_done, 1)
                    act.wait_ge(abs_done, j + 1)
                    act.activation(soft[:], absz[:], ACT.Exp, scale=-1.0).then_inc(exp_done, 1)
                    act.wait_ge(exp_done, j + 1)
                    act.activation(soft[:], soft[:], ACT.Ln, bias=1.0).then_inc(log_done, 1)
                    act.wait_ge(delta_ready, j + 1)
                    act.activation(dA[:], delta[:], ACT.Exp, scale=a_neg[:]).then_inc(decay_ready, 1)

                inputs(0, 0)
                with act.Fori(0, CHUNKS // 2 - 1) as i:
                    for p in range(2):
                        softplus(i * 2 + p)
                        inputs(i * 2 + p + 1, 1 - p)
                softplus(CHUNKS - 2)
                inputs(CHUNKS - 1, 1)
                softplus(CHUNKS - 1)

            @block.vector
            def _(v):
                v.wait_ge(a_ready, 1)
                v.tensor_scalar(a_neg[:], a_neg[:], -1.0, None, ALU.mult).then_inc(a_ready, 1)
                v.sem_inc(gated_ready, FREE)
                v.wait_ge(loaded, 128)

                def convolve(j):
                    ln = Chain(v, conv_link, j * 6, 6)
                    for f in range(2):
                        v.wait_ge(projected, j * 4 + f + 1)
                        v.wait_ge(xconv_done, j * 2)
                        ln(v.tensor_scalar(conv[:, f], psI[:, f], w_conv[:, f, 3:4], b_conv[:, f:f + 1],
                                           ALU.mult, ALU.add))
                        to = conv[:, f].rearrange("p (b l) -> p b l", l=S)
                        frm = psI[:, f].rearrange("p (b l) -> p b l", l=S)
                        for back in range(1, 4):
                            tap = v.scalar_tensor_tensor(
                                out=to[:, :, back:S], in0=frm[:, :, 0:S - back], scalar=w_conv[:, f, 3 - back:4 - back],
                                in1=to[:, :, back:S], op0=ALU.mult, op1=ALU.add)
                            if back < 3:
                                ln(tap)
                            else:
                                tap.then_inc(conv_done, 1)
                    ln.done()

                def step(j, p, convolved):
                    ln = Chain(v, link, j * LINKS, LINKS)
                    v.wait_ge(states_in, j + 1)
                    v.tensor_scalar(z[:], psS[0:NS, 0], b_delta[:], None, ALU.add).then_inc(z_ready, 1)
                    if convolved is not None:
                        convolve(convolved)
                    v.wait_ge(log_done, j + 1)
                    v.scalar_tensor_tensor(out=delta[:], in0=z[:], scalar=0.0, in1=soft[:],
                                           op0=ALU.max, op1=ALU.add).then_inc(delta_ready, 1)
                    v.wait_ge(delta_ready, j + 1)
                    ln(v.tensor_tensor(dB[:], delta[:], psS[0:NS, 1], ALU.mult))
                    ln(v.tensor_tensor(dB[:], dB[:], psS[0:NS, 3], ALU.mult))
                    v.wait_ge(decay_ready, j + 1)
                    ln(v.memset(dA[:].rearrange("p (b l) -> p b l", l=S)[:, :, 0:1], 0.0))
                    ln(v.tensor_tensor_scan(hs[:], dA[:], dB[:], 0.0, ALU.mult, ALU.add))
                    v.tensor_tensor(hc[:], hs[:], psS[0:NS, 2], ALU.mult).then_inc(read_out, 1)
                    v.wait_ge(gate_done, j * 2 + 2)
                    v.wait_ge(xconv_done, j * 2 + 2)
                    v.wait_ge(spread, j + 1)
                    for f in range(2):
                        ln(v.tensor_tensor(gated[:, f], gate[:, p, f], psS[:, 0], ALU.mult))
                        v.scalar_tensor_tensor(out=gated[:, f], in0=xconv[:, p, f], scalar=d_skip[:, f:f + 1],
                                               in1=gated[:, f], op0=ALU.mult, op1=ALU.add).then_inc(gated_ready, 1)
                    v.wait_ge(out_done, j + 1)
                    at = k.X[:, ds(j * CHUNK, CHUNK)]
                    v.tensor_tensor(at, at, psS[:, 1], ALU.add).then_inc(added, 1)
                    ln.done()

                convolve(0)
                with v.Fori(0, CHUNKS // 2 - 1) as i:
                    for p in range(2):
                        step(i * 2 + p, p, i * 2 + p + 1)
                step(CHUNKS - 2, 0, CHUNKS - 1)
                step(CHUNKS - 1, 1, None)



def network(k, name, wu, bu, wd, bd=None, wg=None, ternary=False):
    nc = k.nc
    N = 4
    ctx = Stage(k)
    with ctx:
        sb, ps = buffers(nc, ctx)
        w_up = sb(f"{name}_w_up", [P, N, P])
        w_down = sb(f"{name}_w_down", [P, N, D])
        w_gate = sb(f"{name}_w_gate", [P, D])
        b_up = sb(f"{name}_b_up", [P, N])
        b_row = sb(f"{name}_b_row", [P, D])
        low = sb(f"{name}_low", [P, N * D])
        rowsum = sb(f"{name}_rowsum", [P, 2])
        unit = sb(f"{name}_unit", [P, 2])
        mean = sb(f"{name}_mean", [P, P])
        xs = sb(f"{name}_xs", [P, 2, CHUNK])
        relu = sb(f"{name}_relu", [P, N, CHUNK])
        hT = sb(f"{name}_hT", [P, 2, N, CHUNK])
        gate = sb(f"{name}_gate", [P, 2, CHUNK])
        psH = ps(f"{name}_psH", [P, N, CHUNK])
        psY = ps(f"{name}_psY", [P, 2, CHUNK])
        psG = ps(f"{name}_psG", [P, 2, CHUNK])
        loaded = k.sem(f"{name}_loaded")
        mean_set = k.sem(f"{name}_mean_set")
        sums_ready = k.sem(f"{name}_sums_ready")
        sums_spread = k.sem(f"{name}_sums_spread")
        weights_ready = k.sem(f"{name}_weights_ready")
        link = k.sem(f"{name}_link")
        xs_ready = k.sem(f"{name}_xs_ready")
        up_done = k.sem(f"{name}_up_done")
        relu_done = k.sem(f"{name}_relu_done")
        hidden_ready = k.sem(f"{name}_hidden_ready")
        gate_in = k.sem(f"{name}_gate_in")
        gate_ready = k.sem(f"{name}_gate_ready")
        down_done = k.sem(f"{name}_down_done")
        scaled = k.sem(f"{name}_scaled")
        added = k.sem(f"{name}_added")
        FREE = 2
        LOADS = 2 + (bu is not None) + (bd is not None) + (wg is not None)
        gated = wg is not None

        with nc.Block() as block:
            @block.sync
            def _(sp):
                sp.dma_start(w_up[:], k.a[wu]).then_inc(loaded, 16)
                sp.dma_start(w_down[:], k.a[wd]).then_inc(loaded, 16)
                if bu:
                    sp.dma_start(b_up[:], k.a[bu]).then_inc(loaded, 16)
                if bd:
                    sp.dma_start(b_row[:], k.a[bd].partition_broadcast(P)).then_inc(loaded, 16)
                if gated:
                    sp.dma_start(w_gate[:], k.a[wg]).then_inc(loaded, 16)

            @block.gpsimd
            def _(g):
                if ternary:
                    g.memset(mean[:], 1.0 / (N * P * D)).then_inc(mean_set, 1)
                if gated:
                    with g.Fori(0, CHUNKS // 2) as i:
                        for b in range(2):
                            c = i * 2 + b
                            g.wait_ge(down_done, c + 1)
                            for n in range(N):
                                g.wait_ge(relu_done, c * N + n + 1)
                                g.tensor_tensor(hT[:, b, n], relu[:, n], relu[:, n],
                                                ALU.mult).then_inc(hidden_ready, 1)

            @block.tensor
            def _(pe):
                pe.sem_inc(down_done, FREE)
                pe.wait_ge(loaded, LOADS * 16)
                if ternary:
                    pe.wait_ge(mean_set, 1)
                    pe.wait_ge(sums_ready, 2)
                    pe.matmul(psG[:, 0, 0:2], mean[:], rowsum[:], start=True, stop=True).then_inc(sums_spread, 1)
                    pe.wait_ge(weights_ready, 2)
                with pe.Fori(0, CHUNKS // 2) as i:
                    for b in range(2):
                        c = i * 2 + b
                        pe.wait_ge(xs_ready, c + 1)
                        for n in range(N):
                            pe.wait_ge(relu_done, c * N)
                            pe.matmul(psH[:, n], w_up[:, n], xs[:, b], start=True, stop=True).then_inc(up_done, 1)
                        if gated:
                            pe.wait_ge(gate_ready, c)
                            for t in range(TC):
                                mm = pe.matmul(psG[:, b, t * P:(t + 1) * P], xs[:, b, t * P:(t + 1) * P], w_gate[:],
                                               start=True, stop=True)
                            mm.then_inc(gate_in, 1)
                        pe.wait_ge(hidden_ready if gated else relu_done, (c + 1) * N)
                        pe.wait_ge(added, c + 1)
                        for t in range(TC):
                            for n in range(N):
                                mm = pe.matmul(psY[:, b, t * P:(t + 1) * P], hT[:, b, n, t * P:(t + 1) * P],
                                               w_down[:, n], start=(n == 0), stop=(n == N - 1))
                        mm.then_inc(down_done, 1)

            @block.scalar
            def _(act):
                act.wait_ge(loaded, LOADS * 16)
                with act.Fori(0, CHUNKS // 2) as i:
                    for b in range(2):
                        c = i * 2 + b
                        act.wait_ge(down_done, c + 1)
                        act.activation(xs[:, b], k.XT[:, ds(c * CHUNK, CHUNK)], ACT.Copy).then_inc(xs_ready, 1)
                        for n in range(N):
                            act.wait_ge(up_done, c * N + n + 1)
                            if gated:
                                act.wait_ge(hidden_ready, c * N)
                            act.activation(relu[:, n] if gated else hT[:, b, n], psH[:, n], ACT.Relu,
                                           bias=b_up[:, n:n + 1] if bu else 0.0).then_inc(relu_done, 1)
                        if gated:
                            act.wait_ge(gate_in, c + 1)
                            act.wait_ge(added, c + 1)
                            act.activation(gate[:, b], psG[:, b], ACT.Sigmoid).then_inc(gate_ready, 1)

            @block.vector
            def _(v):
                ln = Chain(v, link)
                if ternary:
                    v.wait_ge(loaded, LOADS * 16)
                    for j, w in enumerate((w_up, w_down)):
                        flat = w[:].rearrange("p n d -> p (n d)")
                        ln(v.tensor_scalar(low[:], flat, -1.0, None, ALU.mult))
                        ln(v.tensor_tensor(low[:], low[:], flat, ALU.max))
                        v.tensor_reduce(rowsum[:, j:j + 1], low[:], AX, ALU.add).then_inc(sums_ready, 1)
                        v.wait_ge(sums_ready, j + 1)
                    v.wait_ge(sums_spread, 1)
                    ln(v.tensor_scalar(unit[:], psG[:, 0, 0:2], EPS, None, ALU.add))
                    ln(v.reciprocal(unit[:], unit[:]))
                    for j, w in enumerate((w_up, w_down)):
                        flat = w[:].rearrange("p n d -> p (n d)")
                        ln(v.tensor_scalar(flat, flat, unit[:, j:j + 1], None, ALU.mult))
                        ln(v.tensor_scalar(low[:], flat, -0.5, None, ALU.is_lt))
                        ln(v.tensor_scalar(flat, flat, 0.5, None, ALU.is_gt))
                        v.tensor_tensor(flat, flat, low[:], ALU.subtract).then_inc(weights_ready, 1)
                        v.wait_ge(weights_ready, j + 1)
                v.sem_inc(added, FREE)
                with v.Fori(0, CHUNKS // 2) as i:
                    for b in range(2):
                        c = i * 2 + b
                        v.wait_ge(down_done, c + 1 + FREE)
                        at = k.X[:, ds(c * CHUNK, CHUNK)]
                        if gated:
                            v.wait_ge(gate_ready, c + 1)
                            v.tensor_tensor(gate[:, b], gate[:, b], psY[:, b], ALU.mult).then_inc(scaled, 1)
                            v.wait_ge(scaled, c + 1)
                            v.tensor_tensor(at, at, gate[:, b], ALU.add).then_inc(added, 1)
                        else:
                            rows = gate[:, b].rearrange("p (t d) -> p t d", t=TC)
                            v.tensor_tensor(rows, psY[:, b].rearrange("p (t d) -> p t d", t=TC),
                                            bcast(b_row[:], 1, TC), ALU.add).then_inc(scaled, 1)
                            v.wait_ge(scaled, c + 1)
                            v.tensor_tensor(at, at, gate[:, b], ALU.add).then_inc(added, 1)


def layer3_ffn(k):
    normalise(k, "n3f", k.X)
    network(k, "f3", "L3_ffn_wu", "L3_ffn_bu", "L3_ffn_wd", bd="L3_ffn_b2", ternary=True)


def layer1_xattn(k):
    depool(k)
    depooled(k, "d1", "L1_xattn")


def layer3_xattn(k):
    depooled(k, "d3", "L3_xattn")



def layer2_attn(k):
    nc = k.nc
    normalise(k, "n2a", k.X, gain="L2_attn_ln1_w", bias="L2_attn_ln1_b", twice=True, keep=k.H)
    ctx = Stage(k)
    LINKS = 13
    WAY = 2 * BC
    with ctx:
        sb, ps = buffers(nc, ctx)
        w_rkv = sb("r_w_rkv", [P, 3, D])
        w_out = sb("r_w_out", [P, D])
        decay = sb("r_decay", [P, 1])
        w_neg = sb("r_w_neg", [P, 1])
        bonus = sb("r_bonus", [P, 1])
        w_step = sb("r_w_step", [P, WAY, S])
        r_sig = sb("r_sig", [P, 2, CHUNK])
        kk = sb("r_kk", [P, WAY, S])
        vv = sb("r_vv", [P, 2, WAY, S])
        uk = sb("r_uk", [P, WAY, S])
        pk = sb("r_pk", [P, WAY, S])
        qq = sb("r_qq", [P, WAY, S])
        e1 = sb("r_e1", [P, WAY, S])
        e2 = sb("r_e2", [P, WAY, S])
        f1 = sb("r_f1", [P, WAY, S])
        f2 = sb("r_f2", [P, WAY, S])
        e2v = sb("r_e2v", [P, WAY, S])
        f2v = sb("r_f2v", [P, WAY, S])
        num = sb("r_num", [P, WAY, S])
        den = sb("r_den", [P, WAY, S])
        both = sb("r_both", [P, BC, S])
        mixed = sb("r_mixed", [P, CHUNK])
        psI = ps("r_psI", [P, 3, CHUNK])
        psO = ps("r_psO", [P, CHUNK])

        loaded = k.sem("r_loaded")
        w_ready = k.sem("r_w_ready")
        projected = k.sem("r_projected")
        inputs_ready = k.sem("r_inputs_ready")
        arguments = k.sem("r_arguments")
        exps = k.sem("r_exps")
        products = k.sem("r_products")
        mix_ready = k.sem("r_mix_ready")
        out_done = k.sem("r_out_done")
        h_added = k.sem("r_h_added")
        x_added = k.sem("r_x_added")
        link = k.sem("r_link")
        flat = "p w l -> p (w l)"
        FREE = 1

        def pairs(eng, step):
            with eng.Fori(0, CHUNKS // 2 - 1) as i:
                for p in range(2):
                    step(i * 2 + p, p, i * 2 + p + 1)
            step(CHUNKS - 2, 0, CHUNKS - 1)
            step(CHUNKS - 1, 1, None)

        with nc.Block() as block:
            @block.sync
            def _(sp):
                sp.dma_start(w_rkv[:], k.a["L2_attn_w_rkv"]).then_inc(loaded, 16)
                sp.dma_start(w_out[:], k.a["L2_attn_w_out"]).then_inc(loaded, 16)
                sp.dma_start(decay[:], k.a["L2_attn_decay"].unsqueeze(1)).then_inc(loaded, 16)
                sp.dma_start(bonus[:], k.a["L2_attn_u"].unsqueeze(1)).then_inc(loaded, 16)

            @block.tensor
            def _(pe):
                pe.wait_ge(loaded, 64)

                def project(j):
                    pe.wait_ge(inputs_ready, j * 6)
                    for f in range(3):
                        pe.matmul(psI[:, f], w_rkv[:, f], k.XT[:, ds(j * CHUNK, CHUNK)],
                                  start=True, stop=True).then_inc(projected, 1)

                def step(j, p, after):
                    if after is not None:
                        project(after)
                    pe.wait_ge(mix_ready, j + 1 + FREE)
                    pe.wait_ge(h_added, j)
                    for t in range(TC):
                        mm = pe.matmul(psO[:, t * P:(t + 1) * P], mixed[:, t * P:(t + 1) * P], w_out[:],
                                       start=True, stop=True)
                    mm.then_inc(out_done, 1)

                project(0)
                pairs(pe, step)

            @block.scalar
            def _(act):
                act.wait_ge(loaded, 64)
                act.activation(w_neg[:], decay[:], ACT.Exp).then_inc(w_ready, 1)
                act.wait_ge(w_ready, 2 + 2)

                def inputs(j, p):
                    act.wait_ge(projected, j * 3 + 3)
                    act.wait_ge(mix_ready, j - 1 + FREE)
                    act.activation(r_sig[:, p], psI[:, 0], ACT.Sigmoid).then_inc(inputs_ready, 1)
                    for f, to in ((1, kk[:]), (2, vv[:, p])):
                        seq = psI[:, f].rearrange("p (b l) -> p b l", l=S)
                        act.activation(to[:, 0:BC], seq, ACT.Copy).then_inc(inputs_ready, 1)
                        act.activation(to[:, BC:WAY], seq[:, :, ::-1], ACT.Copy).then_inc(inputs_ready, 1)
                    act.wait_ge(inputs_ready, j * 6 + 5)
                    act.activation(uk[:], kk[:], ACT.Identity, bias=bonus[:]).then_inc(inputs_ready, 1)

                def step(j, p, after):
                    act.wait_ge(arguments, j + 1)
                    act.activation(f2[:], f2[:], ACT.Exp).then_inc(exps, 1)
                    act.activation(f1[:, :, 1:S], f1[:, :, 1:S], ACT.Exp, bias=w_neg[:]).then_inc(exps, 1)
                    act.activation(e2[:, :, 1:S], e2[:, :, 1:S], ACT.Exp).then_inc(exps, 1)
                    act.activation(e1[:, :, 1:S], e1[:, :, 1:S], ACT.Exp).then_inc(exps, 1)
                    if after is not None:
                        inputs(after, 1 - p)

                inputs(0, 0)
                pairs(act, step)

            @block.gpsimd
            def _(g):
                def step(j, p, after):
                    g.wait_ge(exps, j * 4 + 1)
                    g.tensor_tensor(f2v[:], f2[:], vv[:, p], ALU.mult).then_inc(products, 1)
                    g.wait_ge(exps, j * 4 + 3)
                    g.tensor_tensor(e2v[:, :, 1:S], e2[:, :, 1:S], vv[:, p, :, 1:S], ALU.mult).then_inc(products, 1)

                pairs(g, step)
                with g.Fori(0, CHUNKS) as i:
                    g.wait_ge(h_added, i + 1)
                    at = k.X[:, ds(i * CHUNK, CHUNK)]
                    g.tensor_tensor(at, at, k.H[:, ds(i * CHUNK, CHUNK)], ALU.add).then_inc(x_added, 1)

            @block.vector
            def _(v):
                v.wait_ge(w_ready, 1)
                v.tensor_scalar(w_neg[:], w_neg[:], -1.0, None, ALU.mult).then_inc(w_ready, 1)
                v.wait_ge(w_ready, 2)
                v.tensor_copy(w_step[:].rearrange(flat), w_neg[:].broadcast_to([P, WAY * S])).then_inc(w_ready, 1)
                v.wait_ge(w_ready, 3)
                v.memset(w_step[:, :, 0:1], -1e38).then_inc(w_ready, 1)
                v.wait_ge(w_ready, 4)
                v.sem_inc(mix_ready, FREE)

                def add(i):
                    v.wait_ge(out_done, i)
                    at = k.H[:, ds((i - 1) * CHUNK, CHUNK)]
                    v.tensor_tensor(at, at, psO[:], ALU.add).then_inc(h_added, 1)

                def step(i, p, after, first=False):
                    ln = Chain(v, link, i * LINKS, LINKS)
                    v.wait_ge(inputs_ready, (i + 1) * 6)
                    ln(v.tensor_tensor_scan(pk[:].rearrange(flat), w_step[:].rearrange(flat), kk[:].rearrange(flat),
                                            -1e38, ALU.add, ALU.max))
                    ln(v.tensor_tensor(qq[:, :, 1:S], pk[:, :, 0:S - 1], uk[:, :, 1:S], ALU.max))
                    v.tensor_tensor(f2[:], kk[:], pk[:], ALU.subtract)
                    v.tensor_tensor(f1[:, :, 1:S], pk[:, :, 0:S - 1], pk[:, :, 1:S], ALU.subtract)
                    v.tensor_tensor(e2[:, :, 1:S], uk[:, :, 1:S], qq[:, :, 1:S], ALU.subtract)
                    v.tensor_tensor(e1[:, :, 1:S], pk[:, :, 0:S - 1], qq[:, :, 1:S], ALU.subtract)\
                        .then_inc(arguments, 1)
                    ln(v.memset(f1[:, :, 0:1], 0.0))
                    if not first:
                        add(i)
                    v.wait_ge(exps, i * 4 + 2)
                    ln(v.tensor_tensor_scan(den[:].rearrange(flat), f1[:].rearrange(flat), f2[:].rearrange(flat),
                                            0.0, ALU.mult, ALU.add))
                    v.wait_ge(products, i * 2 + 1)
                    ln(v.tensor_tensor_scan(num[:].rearrange(flat), f1[:].rearrange(flat), f2v[:].rearrange(flat),
                                            0.0, ALU.mult, ALU.add))
                    v.wait_ge(exps, i * 4 + 4)
                    ln(v.tensor_tensor(f2[:, :, 1:S], e1[:, :, 1:S], den[:, :, 0:S - 1], ALU.mult))
                    ln(v.tensor_tensor(f2[:, :, 1:S], f2[:, :, 1:S], e2[:, :, 1:S], ALU.add))
                    ln(v.tensor_tensor(e1[:, :, 1:S], e1[:, :, 1:S], num[:, :, 0:S - 1], ALU.mult))
                    v.wait_ge(products, i * 2 + 2)
                    ln(v.tensor_tensor(e1[:, :, 1:S], e1[:, :, 1:S], e2v[:, :, 1:S], ALU.add))
                    ln(v.reciprocal(f2[:, :, 1:S], f2[:, :, 1:S]))
                    ln(v.tensor_copy(num[:, :, 0:1], vv[:, p, :, 0:1]))
                    ln(v.tensor_tensor(num[:, :, 1:S], e1[:, :, 1:S], f2[:, :, 1:S], ALU.mult))
                    ln(v.tensor_tensor(both[:], num[:, 0:BC], num[:, BC:WAY, ::-1], ALU.add))
                    v.scalar_tensor_tensor(out=mixed[:], in0=both[:].rearrange(flat), scalar=0.5, in1=r_sig[:, p],
                                           op0=ALU.mult, op1=ALU.mult).then_inc(mix_ready, 1)
                    ln.done()

                step(0, 0, None, first=True)
                step(1, 1, None)
                with v.Fori(1, CHUNKS // 2) as i:
                    for p in range(2):
                        step(i * 2 + p, p, None)
                add(CHUNKS)
    normalise(k, "n2b", k.H, gain="L2_attn_ln2_w", bias="L2_attn_ln2_b")
    network(k, "f2a", "L2_attn_wfk", None, "L2_attn_wfv", wg="L2_attn_wfr")



def layer3_attn(k):
    nc = k.nc
    normalise(k, "n3a", k.X)
    ctx = Stage(k)
    LINKS = 4
    G = 4
    W = TC * G * S
    with ctx:
        sb, ps = buffers(nc, ctx)
        w_qk = sb("a_w_qk", [P, 2, D])
        w_v = sb("a_w_v", [P, D])
        w_out = sb("a_w_out", [P, D])
        b_row = sb("a_b_row", [P, D])
        bias = sb("a_bias", [P, G, G * S])
        own_head = sb("a_own_head", [P, G])
        own_batch = sb("a_own_batch", [P, G])
        xs = sb("a_xs", [P, CHUNK])
        qs = sb("a_qs", [P, CHUNK])
        km = sb("a_km", [P, TC, G, P])
        vs = sb("a_vs", [P, CHUNK])
        vm = sb("a_vm", [P, TC, H16, G, DH])
        sc = sb("a_sc", [P, G, TC * G, S])
        mx = sb("a_mx", [P, G, TC * G])
        pt = sb("a_pt", [P, G, TC, G, S])
        ob = sb("a_ob", [S, TC, G, H16, DH])
        ot = sb("a_ot", [P, CHUNK])
        rows = sb("a_rows", [P, TC, D])
        psA = ps("a_psA", [P, 3, CHUNK])
        psS = ps("a_psS", [P, G, W])
        psO = ps("a_psO", [P, CHUNK])

        loaded = k.sem("a_loaded")
        xs_ready = k.sem("a_xs_ready")
        q_in = k.sem("a_q_in")
        k_in = k.sem("a_k_in")
        v_in = k.sem("a_v_in")
        q_ready = k.sem("a_q_ready")
        k_ready = k.sem("a_k_ready")
        v_ready = k.sem("a_v_ready")
        vm_ready = k.sem("a_vm_ready")
        scores_done = k.sem("a_scores_done")
        shifted = k.sem("a_shifted")
        exp_done = k.sem("a_exp_done")
        turned = k.sem("a_turned")
        context_done = k.sem("a_context_done")
        context_ready = k.sem("a_context_ready")
        context_turned = k.sem("a_context_turned")
        ot_ready = k.sem("a_ot_ready")
        out_done = k.sem("a_out_done")
        added = k.sem("a_added")
        link = k.sem("a_link")
        scores_read = [k.sem(f"a_scores{r}_read") for r in range(G)]
        summed = k.sem("a_summed")

        with nc.Block() as block:
            @block.sync
            def _(sp):
                for to, name in ((w_qk, "L3_attn_w_qk"), (w_v, "L3_attn_w_v"), (w_out, "L3_attn_w_outT"),
                                 (bias, "L3_attn_bias"), (own_head, "own_head"), (own_batch, "own_batch")):
                    sp.dma_start(to[:], k.a[name]).then_inc(loaded, 16)
                sp.dma_start(b_row[:], k.a["L3_attn_b_out"].partition_broadcast(P)).then_inc(loaded, 16)

            @block.tensor
            def _(pe):
                pe.wait_ge(loaded, 16 * 7)

                def scores(i):
                    pe.wait_ge(xs_ready, i + 1)
                    pe.wait_ge(k_ready, i)
                    pe.matmul(psA[:, 0], w_qk[:, 0], xs[:], start=True, stop=True).then_inc(q_in, 1)
                    pe.matmul(psA[:, 1], w_qk[:, 1], xs[:], start=True, stop=True).then_inc(k_in, 1)
                    pe.wait_ge(v_ready, i)
                    for t in range(TC):
                        mm = pe.matmul(psA[:, 2, t * P:(t + 1) * P], xs[:, t * P:(t + 1) * P], w_v[:],
                                       start=True, stop=True)
                    mm.then_inc(v_in, 1)
                    pe.wait_ge(q_ready, i + 1)
                    pe.wait_ge(k_ready, i + 1)
                    for r in range(G):
                        pe.wait_ge(scores_read[r], i)
                        pe.nop(nofuse=True)
                        for t in range(TC):
                            for b in range(BT):
                                at = t * P + b * S
                                mm = pe.matmul(
                                    psS[b * S:(b + 1) * S, r, t * G * S:(t + 1) * G * S], qs[r * S:(r + 1) * S, at:at + S],
                                    km[r * S:(r + 1) * S, t, :, b * S:(b + 1) * S], start=True, stop=True)
                        mm.then_inc(scores_done, 1)

                def contexts(i):
                    pe.wait_ge(turned, i + 1)
                    pe.wait_ge(vm_ready, i + 1)
                    pe.wait_ge(added, i)
                    for t in range(TC):
                        pe.wait_ge(context_ready, i * TC + t)
                        for h in range(H16):
                            mm = pe.matmul(psO[0:S, h * S:(h + 1) * S], pt[:, h // G, t, h % G, :],
                                           vm[:, t, h].rearrange("p b d -> p (b d)"), start=True, stop=True)
                        mm.then_inc(context_done, 1)
                    pe.wait_ge(context_ready, i * TC + TC)
                    pe.nop(nofuse=True)
                    for t in range(TC):
                        for b in range(BT):
                            at = t * P + b * S
                            mm = pe.transpose(psA[:, 0, at:at + S], ob[:, t, b].rearrange("p h d -> p (h d)"),
                                              k.ident[0:S, 0:S])
                    mm.then_inc(context_turned, 1)
                    pe.wait_ge(ot_ready, i + 1)
                    for t in range(TC):
                        mm = pe.matmul(psO[:, t * P:(t + 1) * P], ot[:, t * P:(t + 1) * P], w_out[:],
                                       start=True, stop=True)
                    mm.then_inc(out_done, 1)

                scores(0)
                with pe.Fori(0, CHUNKS - 1) as i:
                    scores(i + 1)
                    contexts(i)
                contexts(CHUNKS - 1)

            @block.scalar
            def _(act):
                def inputs(i):
                    act.wait_ge(v_in, i)
                    act.activation(xs[:], k.XT[:, ds(i * CHUNK, CHUNK)], ACT.Copy).then_inc(xs_ready, 1)
                    act.wait_ge(q_in, i + 1)
                    act.wait_ge(scores_done, i * G)
                    act.activation(qs[:], psA[:, 0], ACT.Copy, scale=DH ** -0.5).then_inc(q_ready, 1)
                    act.wait_ge(v_in, i + 1)
                    act.wait_ge(vm_ready, i)
                    act.activation(vs[:], psA[:, 2], ACT.Copy).then_inc(v_ready, 1)

                def exponentials(i):
                    act.wait_ge(shifted, i + 1)
                    act.activation(sc[:], sc[:], ACT.Exp).then_inc(exp_done, 1)

                def outputs(i, tiles):
                    for t in tiles:
                        act.wait_ge(context_done, i * TC + t + 1)
                        act.activation(ob[:, t].rearrange("p b h d -> p h b d"),
                                       psO[0:S, :].rearrange("p (h b d) -> p h b d", h=H16, b=G),
                                       ACT.Copy).then_inc(context_ready, 1)
                    if TC - 1 in tiles:
                        act.wait_ge(context_turned, i + 1)
                        act.activation(ot[:], psA[:, 0], ACT.Copy).then_inc(ot_ready, 1)

                inputs(0)
                exponentials(0)
                with act.Fori(0, CHUNKS - 1) as i:
                    inputs(i + 1)
                    outputs(i, (0, 1))
                    exponentials(i + 1)
                    outputs(i, (2, 3))
                outputs(CHUNKS - 1, range(TC))

            @block.gpsimd
            def _(g):
                g.wait_ge(loaded, 16 * 7)
                with g.Fori(0, CHUNKS) as i:
                    g.wait_ge(v_ready, i + 1)
                    g.wait_ge(context_done, i * TC)
                    g.nop(nofuse=True)
                    for t in range(TC):
                        val = g.tensor_tensor(vm[:, t],
                                              bcast(vs[:, t * P:(t + 1) * P].rearrange("p (h d) -> p h d", d=DH), 2, G),
                                              bcast(bcast(own_batch[:], 1, H16), 3, DH), ALU.mult)
                    val.then_inc(vm_ready, 1)

            @block.vector
            def _(v):
                v.wait_ge(loaded, 16 * 7)
                def softmax(i):
                    ln = Chain(v, link, i * LINKS, LINKS)
                    v.wait_ge(k_in, i + 1)
                    v.wait_ge(scores_done, i * G)
                    v.tensor_tensor(km[:].rearrange("p t q j -> p q t j"),
                                    bcast(psA[:, 1].rearrange("p (t j) -> p t j", t=TC), 1, G),
                                    bcast(bcast(own_head[:], 2, TC), 3, P), ALU.mult).then_inc(k_ready, 1)
                    for r in range(G):
                        v.wait_ge(scores_done, i * G + r + 1)
                        v.tensor_tensor(sc[:, r].rearrange("p (t q) j -> p t (q j)", t=TC),
                                        psS[:, r].rearrange("p (t c) -> p t c", t=TC), bcast(bias[:, r], 1, TC),
                                        ALU.add).then_inc(scores_read[r], 1)
                    v.wait_ge(scores_read[G - 1], i + 1)
                    ln(v.tensor_reduce(mx[:], sc[:], AX, ALU.max))
                    v.tensor_tensor(sc[:], sc[:], bcast(mx[:], 3, S), ALU.subtract).then_inc(shifted, 1)
                    v.wait_ge(exp_done, i + 1)
                    ln(v.tensor_reduce(mx[:], sc[:], AX, ALU.add))
                    ln(v.reciprocal(mx[:], mx[:]))
                    ln(v.tensor_tensor(sc[:], sc[:], bcast(mx[:], 3, S), ALU.mult))
                    v.wait_ge(context_done, i * TC)
                    v.transpose(pt[:].rearrange("p r t q i -> p (r t q i)"),
                                sc[:].rearrange("p r w j -> p (r w j)")).then_inc(turned, 1)
                    v.wait_ge(turned, i + 1)
                    ln.done()

                def add(i):
                    v.wait_ge(out_done, i + 1)
                    v.tensor_tensor(rows[:], psO[:].rearrange("p (t d) -> p t d", t=TC), bcast(b_row[:], 1, TC),
                                    ALU.add).then_inc(summed, 1)
                    v.wait_ge(summed, i + 1)
                    at = k.X[:, ds(i * CHUNK, CHUNK)]
                    v.tensor_tensor(at, at, rows[:].rearrange("p t d -> p (t d)"), ALU.add).then_inc(added, 1)

                softmax(0)
                with v.Fori(0, CHUNKS - 1) as i:
                    softmax(i + 1)
                    add(i)
                add(CHUNKS - 1)


def project(k, name, w_name, b_name, dest):
    nc = k.nc
    ctx = Stage(k)
    with ctx:
        sb, ps = buffers(nc, ctx)
        w = sb(f"{name}_w", [P, D])
        b_row = sb(f"{name}_b_row", [P, D])
        xs = sb(f"{name}_xs", [P, 2, CHUNK])
        rows = sb(f"{name}_rows", [P, 2, TC, D])
        psP = ps(f"{name}_psP", [P, 2, CHUNK])
        loaded = k.sem(f"{name}_loaded")
        xs_ready = k.sem(f"{name}_xs_ready")
        projected = k.sem(f"{name}_projected")
        summed = k.sem(f"{name}_summed")
        added = k.sem(f"{name}_added")
        FREE = 2
        with nc.Block() as block:
            @block.sync
            def _(sp):
                sp.dma_start(w[:], k.a[w_name]).then_inc(loaded, 16)
                sp.dma_start(b_row[:], k.a[b_name].partition_broadcast(P)).then_inc(loaded, 16)

            @block.scalar
            def _(act):
                with act.Fori(0, CHUNKS // 2) as i:
                    for b in range(2):
                        c = i * 2 + b
                        act.wait_ge(projected, c + 1)
                        act.activation(xs[:, b, :], k.XT[:, ds(c * CHUNK, CHUNK)], ACT.Copy).then_inc(xs_ready, 1)

            @block.tensor
            def _(pe):
                pe.sem_inc(projected, FREE)
                pe.wait_ge(loaded, 32)
                with pe.Fori(0, CHUNKS // 2) as i:
                    for b in range(2):
                        c = i * 2 + b
                        pe.wait_ge(xs_ready, c + 1)
                        pe.wait_ge(added, c + 1)
                        for t in range(TC):
                            mm = pe.matmul(psP[:, b, t * P:(t + 1) * P], xs[:, b, t * P:(t + 1) * P], w[:],
                                           start=True, stop=True)
                        mm.then_inc(projected, 1)

            @block.vector
            def _(v):
                v.sem_inc(added, FREE)
                with v.Fori(0, CHUNKS // 2) as i:
                    for b in range(2):
                        c = i * 2 + b
                        v.wait_ge(projected, c + 1 + FREE)
                        v.wait_ge(added, c + 1)
                        v.tensor_tensor(rows[:, b], psP[:, b].rearrange("p (t d) -> p t d", t=TC),
                                        bcast(b_row[:], 1, TC), ALU.add).then_inc(summed, 1)
                        v.wait_ge(summed, c + 1)
                        at = dest[:, ds(c * CHUNK, CHUNK)]
                        v.tensor_tensor(at, at, rows[:, b].rearrange("p t d -> p (t d)"), ALU.add).then_inc(added, 1)



def batch_attention(k):
    nc = k.nc
    ctx = Stage(k)
    G = 4
    V = DH + 1
    with ctx:
        sb, ps = buffers(nc, ctx)
        w_qkv = sb("b_w_qkv", [P, 3, D])
        b_q = sb("b_b_q", [P, 1])
        b_k = sb("b_b_k", [P, 1])
        b_v = sb("b_b_v", [P, D])
        own_head = sb("b_own_head", [P, G])
        xs = sb("b_xs", [P, P])
        qs = sb("b_qs", [P, P])
        km = sb("b_km", [P, G, P])
        vs = sb("b_vs", [P, P])
        va = sb("b_va", [P, H16, V])
        mx = sb("b_mx", [P, H16])
        sc = sb("b_sc", [P, H16, P])
        pt = sb("b_pt", [P, H16, P])
        rec = sb("b_rec", [P, H16])
        ob = sb("b_ob", [P, H16, DH])
        psA = ps("b_psA", [P, CHUNK])
        psS = ps("b_psS", [P, G, CHUNK])
        psT = ps("b_psT", [P, 2, CHUNK])
        psO = ps("b_psO", [P, CHUNK])
        O = psO[:, 0:H16 * V].rearrange("p (h d) -> p h d", d=V)
        OT = psO[:, 256:256 + P]
        XTpos = k.XT[:].rearrange("p (b l) -> p l b", l=S)

        loaded = k.sem("b_loaded")
        consts_set = k.sem("b_consts_set")
        xs_ready = k.sem("b_xs_ready")
        qkv_in = k.sem("b_qkv_in")
        q_ready = k.sem("b_q_ready")
        k_ready = k.sem("b_k_ready")
        v_taken = k.sem("b_v_taken")
        v_ready = k.sem("b_v_ready")
        scores_done = k.sem("b_scores_done")
        max_done = k.sem("b_max_done")
        shifted = k.sem("b_shifted")
        exp_done = k.sem("b_exp_done")
        turned = k.sem("b_turned")
        pt_ready = k.sem("b_pt_ready")
        context_done = k.sem("b_context_done")
        rec_ready = k.sem("b_rec_ready")
        context_ready = k.sem("b_context_ready")
        context_turned = k.sem("b_context_turned")
        stored = k.sem("b_stored")

        with nc.Block() as block:
            @block.sync
            def _(sp):
                sp.dma_start(w_qkv[:], k.a["L2_ffn_w_qkv"]).then_inc(loaded, 16)
                sp.dma_start(b_q[:], k.a["L2_ffn_in_proj_b"][0:D].unsqueeze(1)).then_inc(loaded, 16)
                sp.dma_start(b_k[:], k.a["L2_ffn_in_proj_b"][D:2 * D].unsqueeze(1)).then_inc(loaded, 16)
                sp.dma_start(b_v[:], k.a["L2_ffn_in_proj_b"][2 * D:].partition_broadcast(P)).then_inc(loaded, 16)
                sp.dma_start(own_head[:], k.a["own_head"]).then_inc(loaded, 16)

            @block.tensor
            def _(pe):
                pe.wait_ge(loaded, 80)

                def project(s):
                    pe.wait_ge(xs_ready, s + 1)
                    pe.wait_ge(q_ready, s)
                    pe.wait_ge(k_ready, s)
                    pe.wait_ge(v_taken, s)
                    pe.matmul(psA[:, 0:P], w_qkv[:, 0], xs[:], start=True, stop=True)
                    pe.matmul(psA[:, P:2 * P], w_qkv[:, 1], xs[:], start=True, stop=True)
                    pe.matmul(psA[:, 2 * P:3 * P], xs[:], w_qkv[:, 2], start=True, stop=True).then_inc(qkv_in, 1)

                def scores(s):
                    pe.wait_ge(q_ready, s + 1)
                    pe.wait_ge(k_ready, s + 1)
                    pe.wait_ge(shifted, s)
                    for r in range(G):
                        mm = pe.matmul(psS[:, r], qs[r * S:(r + 1) * S, :],
                                       km[r * S:(r + 1) * S].rearrange("p q j -> p (q j)"), start=True, stop=True)
                    mm.then_inc(scores_done, 1)

                def turn_context(s):
                    pe.wait_ge(context_ready, s + 1)
                    pe.transpose(OT, ob[:].rearrange("p h d -> p (h d)"), k.ident[:]).then_inc(context_turned, 1)

                def context(s):
                    pe.wait_ge(exp_done, s + 1)
                    for r in range(G):
                        pe.wait_ge(pt_ready, s * G + r + 1)
                        for q in range(G):
                            mm = pe.transpose(psT[:, r % 2, q * P:(q + 1) * P], sc[:, r * G + q], k.ident[:])
                        mm.then_inc(turned, 1)
                    pe.wait_ge(v_ready, s + 1)
                    pe.wait_ge(stored, s)
                    for h in range(H16):
                        if h % G == 0:
                            pe.wait_ge(pt_ready, s * G + h // G + 1 + 2)
                        mm = pe.matmul(O[:, h], pt[:, h], va[:, h], start=True, stop=True)
                    mm.then_inc(context_done, 1)

                project(0)
                scores(0)
                project(1)
                scores(1)
                project(2)
                context(0)
                with pe.Fori(0, S - 3) as i:
                    scores(i + 2)
                    turn_context(i)
                    project(i + 3)
                    context(i + 1)
                scores(S - 1)
                turn_context(S - 3)
                context(S - 2)
                turn_context(S - 2)
                context(S - 1)
                turn_context(S - 1)

            @block.scalar
            def _(act):
                act.sem_inc(pt_ready, 2)
                act.wait_ge(consts_set, 2)

                def take(s):
                    act.wait_ge(qkv_in, s)
                    act.activation(xs[:], XTpos[:, ds(s, 1), :].rearrange("p l b -> p (l b)"),
                                   ACT.Copy).then_inc(xs_ready, 1)

                def queries(s):
                    act.wait_ge(qkv_in, s + 1)
                    act.wait_ge(scores_done, s)
                    act.activation(qs[:], psA[:, 0:P], ACT.Identity, scale=DH ** -0.5,
                                   bias=b_q[:]).then_inc(q_ready, 1)

                def exponentials(s):
                    act.wait_ge(shifted, s + 1)
                    act.activation(sc[:], sc[:], ACT.Exp).then_inc(exp_done, 1)

                def turn(s):
                    for r in range(G):
                        act.wait_ge(turned, s * G + r + 1)
                        if r == 0:
                            act.wait_ge(context_done, s)
                        act.activation(pt[:, r * G:(r + 1) * G].rearrange("p h t -> p (h t)"), psT[:, r % 2],
                                       ACT.Copy).then_inc(pt_ready, 1)

                def store(s):
                    act.wait_ge(context_turned, s + 1)
                    act.activation(XTpos[:, ds(s, 1), :].rearrange("p l b -> p (l b)"), OT,
                                   ACT.Copy).then_inc(stored, 1)

                take(0)
                queries(0)
                take(1)
                queries(1)
                exponentials(0)
                take(2)
                queries(2)
                turn(0)
                exponentials(1)
                with act.Fori(0, S - 3) as i:
                    take(i + 3)
                    store(i)
                    queries(i + 3)
                    turn(i + 1)
                    exponentials(i + 2)
                store(S - 3)
                turn(S - 2)
                exponentials(S - 1)
                store(S - 2)
                turn(S - 1)
                store(S - 1)

            @block.vector
            def _(v):
                v.wait_ge(loaded, 80)
                v.memset(va[:], 1.0).then_inc(consts_set, 1)
                v.tensor_scalar(b_q[:], b_q[:], DH ** -0.5, None, ALU.mult).then_inc(consts_set, 1)
                v.wait_ge(consts_set, 2)

                def keys(s):
                    v.wait_ge(q_ready, s + 1)
                    v.wait_ge(scores_done, s)
                    for q in range(G):
                        key = v.tensor_scalar(km[:, q], psA[:, P:2 * P], b_k[:, 0:1], own_head[:, q:q + 1],
                                              ALU.add, ALU.mult)
                    key.then_inc(k_ready, 1)

                def maxima(s):
                    v.wait_ge(scores_done, s + 1)
                    v.tensor_reduce(mx[:], S16, AX, ALU.max).then_inc(max_done, 1)

                def shift(s):
                    v.wait_ge(max_done, s + 1)
                    v.wait_ge(turned, s * G)
                    v.tensor_tensor(sc[:], S16, bcast(mx[:], 2, P), ALU.subtract).then_inc(shifted, 1)

                def take(s):
                    v.wait_ge(v_ready, s)
                    v.tensor_tensor(vs[:], psA[:, 2 * P:3 * P], b_v[:], ALU.add).then_inc(v_taken, 1)

                def values(s):
                    v.wait_ge(v_taken, s + 1)
                    v.wait_ge(context_done, s)
                    v.tensor_copy(va[:, :, 0:DH], vs[:].rearrange("p (h d) -> p h d", d=DH)).then_inc(v_ready, 1)

                def norm(s):
                    v.wait_ge(context_done, s + 1)
                    v.reciprocal(rec[:], O[:, :, DH]).then_inc(rec_ready, 1)
                    v.wait_ge(rec_ready, s + 1)
                    v.wait_ge(context_turned, s)
                    v.tensor_tensor(ob[:], O[:, :, 0:DH], bcast(rec[:], 2, DH), ALU.mult).then_inc(context_ready, 1)

                S16 = psS[:].rearrange("p r (q j) -> p (r q) j", q=G)
                keys(0)
                take(0)
                maxima(0)
                keys(1)
                shift(0)
                values(0)
                take(1)
                maxima(1)
                keys(2)
                shift(1)
                with v.Fori(0, S - 3) as i:
                    norm(i)
                    values(i + 1)
                    take(i + 2)
                    maxima(i + 2)
                    keys(i + 3)
                    shift(i + 2)
                norm(S - 3)
                values(S - 2)
                take(S - 1)
                maxima(S - 1)
                shift(S - 1)
                norm(S - 2)
                values(S - 1)
                norm(S - 1)


def layer2_ffn(k):
    normalise(k, "n2f", k.X, keep=k.H)
    batch_attention(k)
    project(k, "bp", "L2_ffn_out_wT", "L2_ffn_out_b", k.H)
    normalise(k, "n2g", k.H, gain="L2_ffn_ln1_g", bias="L2_ffn_ln1_b", keep=k.H, whole=True)
    mixture(k, "f2", 8, 1, k.H, "assign", "L2_ffn_wr", "L2_ffn_router_b", "L2_ffn_wu", "L2_ffn_bu", "L2_ffn_wd",
            "L2_ffn_b2")
    normalise(k, "n2h", k.H, gain="L2_ffn_ln2_g", bias="L2_ffn_ln2_b", add_to=k.X)



def layer2_xattn(k):
    nc = k.nc
    normalise(k, "n2x", k.X)
    ctx = Stage(k)
    G = 4
    GROUPS = BC // G
    NK = KEYS + S
    KT = 3
    with ctx:
        sb, ps = buffers(nc, ctx)
        w_qk = sb("x_w_qk", [P, 2, D])
        w_v = sb("x_w_v", [P, D])
        w_proj = sb("x_w_proj", [P, D])
        b_row = sb("x_b_row", [P, D])
        own_head = sb("x_own_head", [P, G])
        own16 = sb("x_own16", [P, H16])
        klast = sb("x_klast", [P, B])
        xs = sb("x_xs", [P, CHUNK])
        qs = sb("x_qs", [P, CHUNK])
        qm = sb("x_qm", [P, BC, G, S])
        kc = sb("x_kc", [P, 2, G, NK])
        kown = sb("x_kown", [P, BC, S])
        vc = sb("x_vc", [P, 2, G, 2, P])
        vt = sb("x_vt", [S + 1, 2, G, P])
        sc = sb("x_sc", [P, 2, G, NK])
        mx = sb("x_mx", [P, 2, G])
        pt = sb("x_pt", [P, 2, KT, CHUNK])
        sm = sb("x_sm", [P, 2, G])
        om = sb("x_om", [P, H16, S])
        ot = sb("x_ot", [P, CHUNK])
        rows = sb("x_rows", [P, TC, D])
        psA = ps("x_psA", [P, CHUNK])
        psS = ps("x_psS", [P, G, CHUNK])
        psT = ps("x_psT", [P, 2, CHUNK])
        psO = ps("x_psO", [P, CHUNK])

        loaded = k.sem("x_loaded")
        kc_loaded = k.sem("x_kc_loaded")
        vc_loaded = [k.sem(f"x_vc{n}_loaded") for n in range(2)]
        xs_ready = k.sem("x_xs_ready")
        in_done = k.sem("x_in_done")
        q_ready = k.sem("x_q_ready")
        qm_ready = k.sem("x_qm_ready")
        kself_ready = k.sem("x_kself_ready")
        klast_ready = k.sem("x_klast_ready")
        sum_done = k.sem("x_sum_done")
        rec_done = k.sem("x_rec_done")
        scaled = k.sem("x_scaled")
        vself_in = k.sem("x_vself_in")
        vself_ready = k.sem("x_vself_ready")
        scores_done = k.sem("x_scores_done")
        max_done = k.sem("x_max_done")
        negated = k.sem("x_negated")
        exp_done = k.sem("x_exp_done")
        turned = k.sem("x_turned")
        pt_ready = k.sem("x_pt_ready")
        pt1_ready = k.sem("x_pt1_ready")
        pt2_ready = k.sem("x_pt2_ready")
        context_done = k.sem("x_context_done")
        picked = k.sem("x_picked")
        ot_ready = k.sem("x_ot_ready")
        out_done = k.sem("x_out_done")
        summed = k.sem("x_summed")
        added = k.sem("x_added")
        LOADS = 7

        with nc.Block() as block:
            @block.sync
            def _(sp):
                for to, name in ((w_qk, "L2_xattn_w_qk"), (w_v, "L2_xattn_w_v"), (w_proj, "L2_xattn_w_projT"),
                                 (own_head, "own_head"), (own16, "own_feature")):
                    sp.dma_start(to[:], k.a[name]).then_inc(loaded, 16)
                sp.dma_start(klast[:], k.a["ctx_lastT"][0:P, :]).then_inc(loaded, 16)
                sp.dma_start(b_row[:], k.a["L2_xattn_b_proj"].partition_broadcast(P)).then_inc(loaded, 16)

                def load(n, slot, back):
                    sp.wait_ge(scores_done, back * 2)
                    sp.nop(nofuse=True)
                    sp.wait_ge(klast_ready, n)
                    sp.nop(nofuse=True)
                    first = n * G
                    sp.dma_start(kc[:, slot, :, 0:2 * P],
                                 k.a["ctxT"][ds(first, G), 0:P, 0:2 * P].rearrange("b c n -> c b n"))\
                        .then_inc(kc_loaded, 16)
                    sp.wait_ge(context_done, back)
                    sp.nop(nofuse=True)
                    for j in range(2):
                        sp.dma_start(vc[:, slot, :, j, :],
                                     k.a["ctx"][ds(first, G), j * P:(j + 1) * P, P:2 * P].rearrange("b n c -> n b c"))\
                            .then_inc(vc_loaded[slot], 16)
                    sp.dma_start(vt[S:S + 1, slot], k.a["ctx_last"][ds(first, G), P:2 * P].unsqueeze(0))\
                        .then_inc(vc_loaded[slot], 16)

                load(0, 0, 0)
                with sp.Fori(0, CHUNKS - 1) as i:
                    load(i * GROUPS + 1, 1, i * BC)
                    load(i * GROUPS + 2, 0, i * BC + G)
                    load(i * GROUPS + 3, 1, i * BC + 2 * G)
                    load(i * GROUPS + 4, 0, i * BC + 3 * G)
                last = (CHUNKS - 1) * BC
                for g in range(1, GROUPS):
                    load(last // G + g, g % 2, last + (g - 1) * G)

            @block.gpsimd
            def _(g):
                g.wait_ge(loaded, LOADS * 16)
                with g.Fori(0, CHUNKS) as i:
                    for j in range(GROUPS):
                        n = i * GROUPS + j
                        g.wait_ge(kc_loaded, (n + 1) * 16)
                        g.wait_ge(kself_ready, i + 1)
                        g.nop(nofuse=True)
                        g.tensor_copy(kc[:, j % 2, :, 2 * P:NK - 1], kown[:, j * G:(j + 1) * G])
                        g.tensor_copy(kc[:, j % 2, :, NK - 1], klast[:, ds(n * G, G)]).then_inc(klast_ready, 1)

            @block.tensor
            def _(pe):
                pe.wait_ge(loaded, LOADS * 16)

                def turn(i, c, t):
                    before = (pt1_ready, pt2_ready, pt_ready)[t]
                    pe.wait_ge(before, i * BC + c + (1 if t == 2 else 0))
                    pe.nop(nofuse=True)
                    keys = P if t < 2 else S + 1
                    for r in range(G):
                        mm = pe.transpose(psT[0:keys, (c * KT + t) % 2, r * P:(r + 1) * P],
                                          sc[:, c % 2, r, t * P:t * P + keys], k.ident[:])
                    mm.then_inc(turned, 1)

                def project(i):
                    pe.wait_ge(xs_ready, i + 1)
                    pe.wait_ge(vself_ready, i * GROUPS)
                    pe.matmul(psA[:], w_qk[:, 0], xs[:], start=True, stop=True).then_inc(in_done, 1)
                    pe.wait_ge(q_ready, i + 1)
                    pe.matmul(psA[:], w_qk[:, 1], xs[:], start=True, stop=True).then_inc(in_done, 1)

                def chunk(i, last):
                    for b in range(BC + 2):
                        if b < BC:
                            g, j = b // G, b % G
                            if j == 0:
                                pe.wait_ge(klast_ready, i * GROUPS + g + 1)
                                pe.wait_ge(vself_ready, i * GROUPS + g)
                                pe.wait_ge(kself_ready, i + 1)
                                for jj in range(G):
                                    mm = pe.matmul(psA[0:S, jj * P:(jj + 1) * P],
                                                   xs[:, (b + jj) * S:(b + jj + 1) * S], w_v[:], start=True, stop=True)
                                mm.then_inc(vself_in, 1)
                            if b == 0:
                                pe.wait_ge(qm_ready, i + 1)
                            for half in range(2):
                                pe.wait_ge(exp_done, (i * BC + b) * G + half * 2 + 2)
                                pe.nop(nofuse=True)
                                for r in range(half * 2, half * 2 + 2):
                                    mm = pe.matmul(psS[:, r, 0:NK],
                                                   qm[r * S:(r + 1) * S, b].rearrange("p q i -> p (q i)"),
                                                   kc[r * S:(r + 1) * S, g % 2, j], start=True, stop=True)
                                mm.then_inc(scores_done, 1)
                        if b == BC and not last:
                            project(i + 1)
                        if 1 <= b <= BC:
                            pe.wait_ge(scaled, i * BC + b)
                            turn(i, b - 1, 0)
                            turn(i, b - 1, 1)
                        if b >= 2:
                            c = b - 2
                            g, j = c // G, c % G
                            pe.wait_ge(pt_ready, i * BC + c + 1)
                            pe.wait_ge(pt1_ready, i * BC + c + 1)
                            pe.wait_ge(pt2_ready, i * BC + c + 1)
                            pe.wait_ge(vc_loaded[g % 2], (i * (GROUPS // 2) + g // 2 + 1) * 48)
                            pe.wait_ge(vself_ready, i * GROUPS + g + 1)
                            pe.wait_ge(picked, i * BC + c)
                            if c == 0:
                                pe.wait_ge(added, i)
                            pe.nop(nofuse=True)
                            for t in range(KT):
                                val = vc[:, g % 2, j, t] if t < 2 else vt[:, g % 2, j]
                                mm = pe.matmul(psO[:], val, pt[0:P if t < 2 else S + 1, c % 2, t],
                                               start=(t == 0), stop=(t == KT - 1))
                            mm.then_inc(context_done, 1)
                        if 1 <= b <= BC:
                            turn(i, b - 1, 2)
                    pe.wait_ge(ot_ready, (i + 1) * BC)
                    pe.wait_ge(vself_ready, (i + 1) * GROUPS)
                    for t in range(TC):
                        mm = pe.matmul(psO[:, t * P:(t + 1) * P], ot[:, t * P:(t + 1) * P], w_proj[:],
                                       start=True, stop=True)
                    mm.then_inc(out_done, 1)

                project(0)
                with pe.Fori(0, CHUNKS - 1) as i:
                    chunk(i, False)
                chunk(CHUNKS - 1, True)

            @block.scalar
            def _(act):
                act.sem_inc(exp_done, G)
                act.wait_ge(loaded, LOADS * 16)

                def inputs(i):
                    act.wait_ge(vself_in, i * GROUPS)
                    act.activation(xs[:], k.XT[:, ds(i * CHUNK, CHUNK)], ACT.Copy).then_inc(xs_ready, 1)
                    act.wait_ge(in_done, i * 2 + 1)
                    act.wait_ge(qm_ready, i)
                    act.activation(qs[:], psA[:], ACT.Copy, scale=DH ** -0.5).then_inc(q_ready, 1)
                    act.wait_ge(in_done, i * 2 + 2)
                    act.wait_ge(klast_ready, i * GROUPS)
                    act.activation(kown[:].rearrange("p b j -> p (b j)"), psA[:], ACT.Copy).then_inc(kself_ready, 1)

                def chunk(i, last):
                    def copy(c, t, done):
                        act.wait_ge(context_done, i * BC + max(c - 1, 0))
                        act.wait_ge(turned, (i * BC + c) * KT + t + 1)
                        keys = P if t < 2 else S + 1
                        act.activation(pt[0:keys, c % 2, t], psT[0:keys, (c * KT + t) % 2], ACT.Copy).then_inc(done, 1)

                    for b in range(BC):
                        g, j = b // G, b % G
                        if j == 0:
                            act.wait_ge(vself_in, i * GROUPS + g + 1)
                            act.wait_ge(context_done, i * BC + b - (G if b else 0))
                            act.activation(vt[0:S, g % 2].rearrange("p b c -> p (b c)"), psA[0:S, :],
                                           ACT.Copy).then_inc(vself_ready, 1)
                        if b >= 1:
                            copy(b - 1, 0, pt_ready)
                        for r in range(G):
                            act.wait_ge(negated, (i * BC + b) * 2 + r // 2 + 1)
                            if r == 0:
                                act.wait_ge(turned, (i * BC + max(b - 1, 0)) * KT)
                            act.activation(sc[:, b % 2, r], psS[:, r, 0:NK], ACT.Exp,
                                           bias=mx[:, b % 2, r:r + 1]).then_inc(exp_done, 1)
                        if b >= 1:
                            copy(b - 1, 2, pt2_ready)
                    if not last:
                        inputs(i + 1)
                    copy(BC - 1, 0, pt_ready)
                    copy(BC - 1, 2, pt2_ready)

                inputs(0)
                with act.Fori(0, CHUNKS - 1) as i:
                    chunk(i, False)
                chunk(CHUNKS - 1, True)

            @block.vector
            def _(v):
                v.wait_ge(loaded, LOADS * 16)

                def queries(i):
                    v.wait_ge(q_ready, i + 1)
                    v.wait_ge(scores_done, i * BC * 2)
                    v.tensor_tensor(qm[:].rearrange("p b q i -> p q b i"),
                                    bcast(qs[:].rearrange("p (b i) -> p b i", b=BC), 1, G),
                                    bcast(bcast(own_head[:], 2, BC), 3, S), ALU.mult).then_inc(qm_ready, 1)

                def chunk(i, last):
                    def maxima(b):
                        for half in range(2):
                            v.wait_ge(scores_done, (i * BC + b) * 2 + half + 1)
                            two = mx[:, b % 2, half * 2:half * 2 + 2]
                            v.tensor_reduce(two, psS[:, half * 2:half * 2 + 2, 0:NK], AX, ALU.max)\
                                .then_inc(max_done, 1)
                            v.wait_ge(max_done, (i * BC + b) * 2 + half + 1)
                            v.tensor_scalar(two, two, -1.0, None, ALU.mult).then_inc(negated, 1)

                    def copy(c):
                        v.wait_ge(turned, (i * BC + c) * KT + 2)
                        v.wait_ge(context_done, i * BC + max(c - 1, 0))
                        v.tensor_copy(pt[:, c % 2, 1], psT[:, (c * KT + 1) % 2]).then_inc(pt1_ready, 1)

                    def scale(b):
                        n = i * BC + b + 1
                        v.wait_ge(exp_done, n * G + G)
                        v.tensor_reduce(sm[:, b % 2], sc[:, b % 2], AX, ALU.add).then_inc(sum_done, 1)
                        v.wait_ge(sum_done, n)
                        v.reciprocal(sm[:, b % 2], sm[:, b % 2]).then_inc(rec_done, 1)
                        v.wait_ge(rec_done, n)
                        v.tensor_tensor(sc[:, b % 2], sc[:, b % 2], bcast(sm[:, b % 2], 2, NK), ALU.mult)\
                            .then_inc(scaled, 1)

                    def pick(c):
                        v.wait_ge(context_done, i * BC + c + 1)
                        v.wait_ge(ot_ready, i * BC + c)
                        v.tensor_tensor(om[:], psO[:].rearrange("p (h i) -> p h i", h=H16), bcast(own16[:], 2, S),
                                        ALU.mult).then_inc(picked, 1)
                        v.wait_ge(picked, i * BC + c + 1)
                        v.tensor_reduce(ot[:, c * S:(c + 1) * S], om[:].rearrange("p h i -> p i h"), AX, ALU.add)\
                            .then_inc(ot_ready, 1)

                    for b in range(BC + 2):
                        if b < BC:
                            maxima(b)
                        if b == BC and not last:
                            queries(i + 1)
                        if 1 <= b <= BC:
                            copy(b - 1)
                        if b < BC:
                            scale(b)
                        if b >= 2:
                            pick(b - 2)
                    v.wait_ge(out_done, i + 1)
                    v.tensor_tensor(rows[:], psO[:].rearrange("p (t d) -> p t d", t=TC), bcast(b_row[:], 1, TC),
                                    ALU.add).then_inc(summed, 1)
                    v.wait_ge(summed, i + 1)
                    at = k.X[:, ds(i * CHUNK, CHUNK)]
                    v.tensor_tensor(at, at, rows[:].rearrange("p t d -> p (t d)"), ALU.add).then_inc(added, 1)

                queries(0)
                with v.Fori(0, CHUNKS - 1) as i:
                    chunk(i, False)
                chunk(CHUNKS - 1, True)



def layer0_attn(k):
    nc = k.nc
    normalise(k, "n0a", k.X)
    G = 4
    V = DH + 1
    REG = 1e-6
    NL = 64
    J = S + V
    k_dram = nc.dram_tensor("l_k_dram", (TILES, P, G, G * S), F32).ap()
    r_dram = nc.dram_tensor("l_r_dram", (B, S, H16 * V), F32).ap()
    y_dram = nc.dram_tensor("l_y_dram", (B, S, H16 * V), F32).ap()
    q_dram = nc.dram_tensor("l_q_dram", (CHUNKS, P, G * CHUNK), F32).ap()
    kernel_matrices(k, q_dram, k_dram, r_dram)
    landmark_solve(k, k_dram, r_dram, y_dram, REG, NL, J)
    landmark_read(k, q_dram, y_dram)


def kernel_matrices(k, q_dram, k_dram, r_dram):
    nc = k.nc
    G = 4
    V = DH + 1
    LINKS = 3
    ctx = Stage(k)
    with ctx:
        sb, ps = buffers(nc, ctx)
        w_kq = sb("l_w_kq", [P, 4, P])
        b_kq = sb("l_b_kq", [P, 4])
        b_kq2 = sb("l_b_kq2", [P, 4])
        w_tok = sb("l_w_tok", [P, 3 * D])
        b_tok = sb("l_b_tok", [P, 3 * D])
        own_head = sb("l_own_head", [P, G])
        own_batch = sb("l_own_batch", [P, G])
        temp = sb("l_temp", [P, 1])
        ninv = sb("l_ninv", [P, 1])
        xs = sb("l_xs", [P, CHUNK])
        kk = sb("l_kk", [P, 2, CHUNK])
        lk = sb("l_lk", [P, 4, CHUNK])
        rk = sb("l_rk", [P, 2, G, CHUNK])
        tok = sb("l_tok", [P, TC, 3 * D])
        sq = sb("l_sq", [P, TC, 2 * D])
        norm = sb("l_norm", [P, TC, 2, H16])
        dist = sb("l_dist", [P, 2, G, TC * G, S])
        turn = sb("l_turn", [P, G, TC * G, S])
        vm = sb("l_vm", [P, TC, H16, G, V])
        rb = sb("l_rb", [S, 2, G, H16, V])
        psA = ps("l_psA", [P, 2, CHUNK])
        psS = ps("l_psS", [P, G, CHUNK])
        psR = ps("l_psR", [P, 2, CHUNK])

        loaded = k.sem("l_loaded")
        consts_set = k.sem("l_consts_set")
        xs_ready = k.sem("l_xs_ready")
        in_done = k.sem("l_in_done")
        in_read = k.sem("l_in_read")
        tok_in = k.sem("l_tok_in")
        tok_read = k.sem("l_tok_read")
        squared = k.sem("l_squared")
        rk_ready = k.sem("l_rk_ready")
        vm_ready = k.sem("l_vm_ready")
        scores_done = k.sem("l_scores_done")
        scores_read = [k.sem(f"l_scores{r}_read") for r in range(G)]
        dist_ready = k.sem("l_dist_ready")
        exp_done = k.sem("l_exp_done")
        turned = k.sem("l_turned")
        temp_ready = k.sem("l_temp_ready")
        right_done = [k.sem(f"l_right{n}_done") for n in range(2)]
        right_read = [k.sem(f"l_right{n}_read") for n in range(2)]
        k_stored = k.sem("l_k_stored")
        r_stored = [k.sem(f"l_r{n}_stored") for n in range(2)]
        q_stored = k.sem("l_q_stored")
        link = k.sem("l_link")

        with nc.Block() as block:
            @block.sync
            def _(sp):
                for to, name in ((w_kq, "L0_attn_w_kq"), (b_kq, "L0_attn_b_kq"), (w_tok, "L0_attn_w_tok"),
                                 (own_head, "own_head"), (own_batch, "own_batch")):
                    sp.dma_start(to[:], k.a[name]).then_inc(loaded, 16)
                sp.dma_start(b_tok[:], k.a["L0_attn_b_tok"].partition_broadcast(P)).then_inc(loaded, 16)
                sp.dma_start(temp[:], k.a["L0_attn_temperature"].partition_broadcast(P)).then_inc(loaded, 16)
                with sp.Fori(0, CHUNKS) as i:
                    sp.wait_ge(exp_done, i * 2 + 1)
                    sp.nop(nofuse=True)
                    for t in range(TC):
                        sp.dma_start(k_dram[ds(i * TC + t, 1)].rearrange("a p r c -> (a p) r c"),
                                     dist[:, 0, :, t * G:(t + 1) * G, :].rearrange("p r q j -> p r (q j)"))\
                            .then_inc(k_stored, 16)
                    sp.wait_ge(turned, i + 1)
                    sp.nop(nofuse=True)
                    sp.dma_start(q_dram[ds(i, 1)].rearrange("a p c -> (a p) c"),
                                 turn[:].rearrange("p r w j -> p (r w j)")).then_inc(q_stored, 16)
                    for t in range(TC):
                        for half in range(2):
                            sp.wait_ge(right_read[half], i * TC + t + 1)
                        sp.nop(nofuse=True)
                        sp.dma_start(r_dram[ds((i * TC + t) * BT, BT)].rearrange("b i c -> i b c"),
                                     rb[:, t % 2].rearrange("p b h d -> p b (h d)")).then_inc(r_stored[t % 2], 16)
                sp.wait_ge(q_stored, 16 * CHUNKS)
                sp.wait_ge(k_stored, 16 * TILES)
                for half in range(2):
                    sp.wait_ge(r_stored[half], 16 * TILES // 2)

            @block.tensor
            def _(pe):
                pe.wait_ge(loaded, 112)
                pe.wait_ge(consts_set, 4)

                def project(i):
                    pe.wait_ge(xs_ready, i + 1)
                    for f in range(4):
                        if f < 2:
                            pe.wait_ge(tok_read, i * TC)
                        else:
                            pe.wait_ge(in_read, i * 4 + f - 1)
                        pe.matmul(psA[:, f % 2], w_kq[:, f], xs[:], start=True, stop=True).then_inc(in_done, 1)

                def project_tokens(i):
                    for t in range(TC):
                        pe.wait_ge(in_read, (i + 1) * 4)
                        if t >= 2:
                            pe.wait_ge(tok_read, i * TC + t - 1)
                        pe.matmul(psA[:, t % 2, 0:3 * D], xs[:, t * P:(t + 1) * P], w_tok[:],
                                  start=True, stop=True).then_inc(tok_in, 1)

                def distances(i):
                    pe.wait_ge(rk_ready, i + 1)
                    for m in range(2):
                        for r in range(G):
                            low = r % 2 * 64
                            pe.wait_ge(scores_read[r], i * 2 + m)
                            pe.nop(nofuse=True)
                            for t in range(TC):
                                for b in range(BT):
                                    at = t * P + b * S
                                    mm = pe.matmul(psS[b * S:(b + 1) * S, r, t * P:(t + 1) * P],
                                                   lk[low:low + 64, m * 2 + r // 2, at:at + S],
                                                   rk[low:low + 64, r // 2, :, at:at + S], start=True, stop=True)
                            mm.then_inc(scores_done, 1)

                def right_sides(i):
                    pe.wait_ge(exp_done, i * 2 + 1)
                    pe.wait_ge(vm_ready, i + 1)
                    for t in range(TC):
                        for half in range(2):
                            pe.wait_ge(right_read[half], i * TC + t)
                            pe.nop(nofuse=True)
                            for h in range(half * 8, half * 8 + 8):
                                mm = pe.matmul(psR[0:S, half, h % 8 * G * V:(h % 8 + 1) * G * V],
                                               dist[:, 0, h // G, t * G + h % G, :],
                                               vm[:, t, h].rearrange("p b d -> p (b d)"), start=True, stop=True)
                            mm.then_inc(right_done[half], 1)

                project(0)
                project_tokens(0)
                distances(0)
                with pe.Fori(0, CHUNKS - 1) as i:
                    project(i + 1)
                    right_sides(i)
                    project_tokens(i + 1)
                    distances(i + 1)
                right_sides(CHUNKS - 1)

            @block.scalar
            def _(act):
                act.wait_ge(loaded, 112)
                act.wait_ge(consts_set, 4)

                def inputs(i):
                    act.wait_ge(tok_in, i * TC)
                    act.activation(xs[:], k.XT[:, ds(i * CHUNK, CHUNK)], ACT.Copy).then_inc(xs_ready, 1)
                    act.wait_ge(scores_done, i * 2 * G)
                    for f in range(4):
                        act.wait_ge(in_done, i * 4 + f + 1)
                        if f < 2:
                            act.wait_ge(rk_ready, i)
                            act.activation(kk[:, f], psA[:, f], ACT.Identity, bias=b_kq[:, f:f + 1])
                        for low in (0, 2 * S):
                            x = act.activation(lk[low:low + S, f], psA[low:low + S, f % 2], ACT.Identity,
                                               scale=-2.0, bias=b_kq2[low:low + S, f:f + 1])
                        x.then_inc(in_read, 1)

                def squares(i):
                    act.wait_ge(tok_read, (i + 1) * TC)
                    act.activation(sq[:], tok[:, :, 0:2 * D], ACT.Square).then_inc(squared, 1)

                def exponentials(i):
                    for m in range(2):
                        act.wait_ge(dist_ready, i * 2 + m + 1)
                        act.activation(dist[:, m], dist[:, m], ACT.Exp, scale=ninv[:]).then_inc(exp_done, 1)

                def right_sides(i):
                    for t in range(TC):
                        act.wait_ge(r_stored[t % 2], (i * (TC // 2) + t // 2) * 16)
                        for half in range(2):
                            act.wait_ge(right_done[half], i * TC + t + 1)
                            act.activation(rb[:, t % 2, :, half * 8:half * 8 + 8].rearrange("p b h d -> p h b d"),
                                           psR[0:S, half, 0:8 * G * V].rearrange("p (h b d) -> p h b d", h=8, b=G),
                                           ACT.Copy).then_inc(right_read[half], 1)

                inputs(0)
                squares(0)
                exponentials(0)
                with act.Fori(0, CHUNKS - 1) as i:
                    inputs(i + 1)
                    right_sides(i)
                    squares(i + 1)
                    exponentials(i + 1)
                right_sides(CHUNKS - 1)

            @block.gpsimd
            def _(g):
                g.wait_ge(consts_set, 4)
                g.wait_ge(loaded, 112)
                with g.Fori(0, CHUNKS) as i:
                    g.wait_ge(tok_read, (i + 1) * TC)
                    for half in range(2):
                        g.wait_ge(right_done[half], i * TC)
                    g.nop(nofuse=True)
                    for t in range(TC):
                        val = g.tensor_tensor(vm[:, t, :, :, 0:DH],
                                              bcast(tok[:, t, 2 * D:].rearrange("p (h d) -> p h d", d=DH), 2, G),
                                              bcast(bcast(own_batch[:], 1, H16), 3, DH), ALU.mult)
                    val.then_inc(vm_ready, 1)

            @block.vector
            def _(v):
                v.wait_ge(loaded, 112)
                v.tensor_scalar(b_kq2[:], b_kq[:], -2.0, None, ALU.mult).then_inc(consts_set, 1)
                v.memset(lk[:], 1.0).then_inc(consts_set, 1)
                v.tensor_copy(vm[:, :, :, :, DH].rearrange("p t h b -> p (t h) b"),
                              bcast(own_batch[:], 1, TC * H16)).then_inc(consts_set, 1)
                v.reciprocal(temp[:], temp[:]).then_inc(temp_ready, 1)
                v.wait_ge(temp_ready, 1)
                v.tensor_scalar(ninv[:], temp[:], -1.0, None, ALU.mult).then_inc(consts_set, 1)
                with v.Fori(0, CHUNKS) as i:
                    ln = Chain(v, link, i * LINKS, LINKS)
                    v.wait_ge(in_read, i * 4 + 2)
                    for low in (S, 3 * S):
                        ln(v.tensor_tensor(kk[low:low + S], kk[low:low + S], kk[low:low + S], ALU.mult))
                    v.wait_ge(scores_done, i * 2 * G)
                    for f in range(2):
                        m = v.tensor_tensor(rk[:, f], bcast(kk[:, f], 1, G), bcast(own_head[:], 2, CHUNK), ALU.mult)
                    m.then_inc(rk_ready, 1)
                    v.wait_ge(vm_ready, i)
                    v.wait_ge(squared, i)
                    for t in range(TC):
                        v.wait_ge(tok_in, i * TC + t + 1)
                        v.tensor_tensor(tok[:, t], psA[:, t % 2, 0:3 * D], b_tok[:], ALU.add).then_inc(tok_read, 1)
                    v.wait_ge(squared, i + 1)
                    ln(v.tensor_reduce(norm[:].rearrange("p t m h -> p t (m h)"),
                                       sq[:].rearrange("p t (h d) -> p t h d", d=DH), AX, ALU.add))
                    for m in range(2):
                        if m == 0:
                            v.wait_ge(right_done[0], i * TC)
                            v.wait_ge(right_done[1], i * TC)
                            v.wait_ge(k_stored, i * TC * 16)
                        for r in range(G):
                            v.wait_ge(scores_done, (i * 2 + m) * G + r + 1)
                            v.tensor_tensor(
                                dist[:, m, r].rearrange("p (t q) j -> p t q j", t=TC),
                                psS[:, r].rearrange("p (t q j) -> p t q j", t=TC, q=G),
                                bcast(norm[:, :, 1 - m, r * G:(r + 1) * G], 3, S), ALU.add)\
                                .then_inc(scores_read[r], 1)
                        v.wait_ge(scores_read[G - 1], i * 2 + m + 1)
                        v.tensor_scalar(dist[:, m], dist[:, m], 0.0, None, ALU.max).then_inc(dist_ready, 1)
                    v.wait_ge(exp_done, i * 2 + 2)
                    v.wait_ge(q_stored, i * 16)
                    v.transpose(turn[:].rearrange("p r w j -> p (r w j)"),
                                dist[:, 1].rearrange("p r w j -> p (r w j)")).then_inc(turned, 1)
                    ln.done()


def landmark_solve(k, k_dram, r_dram, y_dram, REG, NL, J):
    nc = k.nc
    V = DH + 1
    RUN = 4
    ctx = Stage(k)
    with ctx:
        sb, ps = buffers(nc, ctx)
        A = sb("s_A", [P, S, H16, J])
        rr = sb("s_rr", [P, S, H16 * V])
        tmp = sb("s_tmp", [P, S // 2, H16, J])
        idx_i = sb("s_idx_i", [P, NL], I32)
        idx = sb("s_idx", [P, NL])
        wrap = sb("s_wrap", [P, NL])
        pos = sb("s_pos", [P, S])
        hit = sb("s_hit", [P, S, NL])
        cnt = sb("s_cnt", [P, S])
        land = sb("s_land", [P, S])
        land_i = sb("s_land_i", [P, S], I32)
        any_f = sb("s_any_f", [P, S // RUN])
        any_i = sb("s_any_i", [P, S // RUN], I32)
        diag = sb("s_diag", [P, S])
        pair = sb("s_pair", [P, S, S])
        piv = sb("s_piv", [P, H16])
        ROWS = 8
        loaded = k.sem("s_loaded")
        rr_loaded = k.sem("s_rr_loaded")
        rows_loaded = [k.sem(f"s_rows{n}_loaded") for n in range(S // ROWS)]
        link = k.sem("s_link")
        solved = k.sem("s_solved")
        stored = k.sem("s_stored")
        with nc.Block() as block:
            @block.sync
            def _(sp):
                sp.dma_start(idx_i[:], k.a["L0_attn_landmark_idx"].partition_broadcast(P)).then_inc(loaded, 16)
                sp.dma_start(pos[:], k.a["pos"].partition_broadcast(P)).then_inc(loaded, 16)
                sp.dma_start(rr[:], r_dram).then_inc(rr_loaded, 16)
                for i in range(S):
                    sp.dma_start(A[:, i, :, 0:S],
                                 k_dram.rearrange("t (b i) r (q j) -> (t b) i (r q) j", b=BT, q=4)[:, i])\
                        .then_inc(rows_loaded[i // ROWS], 16)
                sp.wait_ge(solved, 1)
                sp.dma_start(y_dram, rr[:]).then_inc(stored, 16)
                sp.wait_ge(stored, 16)

            @block.vector
            def _(v):
                ln = Chain(v, link)
                v.wait_ge(loaded, 32)
                ln(v.tensor_copy(idx[:], idx_i[:]))
                ln(v.tensor_scalar(wrap[:], idx[:], 0.0, float(S), ALU.is_lt, ALU.mult))
                ln(v.tensor_tensor(idx[:], idx[:], wrap[:], ALU.add))
                ln(v.tensor_scalar(idx[:], idx[:], 0.0, float(S - 1), ALU.max, ALU.min))
                ln(v.tensor_tensor(hit[:], bcast(idx[:], 1, S), bcast(pos[:], 2, NL), ALU.is_equal))
                ln(v.tensor_reduce(cnt[:], hit[:], AX, ALU.add))
                ln(v.tensor_scalar(land[:], cnt[:], 1.0, None, ALU.min))
                ln(v.tensor_scalar(cnt[:], cnt[:], 1.0, None, ALU.max))
                ln(v.reciprocal(cnt[:], cnt[:]))
                ln(v.tensor_scalar(cnt[:], cnt[:], REG, -1.0, ALU.mult, ALU.add))
                ln(v.tensor_tensor(cnt[:], cnt[:], land[:], ALU.mult))
                ln(v.tensor_scalar(diag[:], cnt[:], 1.0, None, ALU.add))
                ln(v.tensor_tensor(pair[:], bcast(land[:], 1, S), bcast(land[:], 2, S), ALU.mult))
                for n in range(S // ROWS):
                    v.wait_ge(rows_loaded[n], 16 * ROWS)
                    part = slice(n * ROWS, (n + 1) * ROWS)
                    ln(v.tensor_tensor(A[:, part, :, 0:S], A[:, part, :, 0:S], bcast(pair[:, part], 2, H16), ALU.mult))
                v.wait_ge(rr_loaded, 16)
                ln(v.tensor_tensor(A[:, :, :, S:J],
                                   rr[:].rearrange("p i (h d) -> p i h d", d=V),
                                   bcast(bcast(land[:], 2, H16), 3, V), ALU.mult))
                ln(v.tensor_copy(land_i[:], land[:]))
                ln(v.tensor_reduce(any_f[:], land[:].rearrange("p (m n) -> p m n", n=RUN), AX, ALU.max))
                ln(v.tensor_copy(any_i[:], any_f[:]))

                def eliminate(n):
                    ln(v.tensor_scalar(piv[:], A[:, n, :, n], diag[:, n:n + 1], None, ALU.add))
                    ln(v.reciprocal(piv[:], piv[:]))
                    ln(v.tensor_tensor(A[:, n, :, n + 1:J], A[:, n, :, n + 1:J], bcast(piv[:], 2, J - n - 1),
                                       ALU.mult))
                    for lo, hi in ((n + 1, min(S, n + 1 + S // 2)), (n + 1 + S // 2, S)):
                        if lo >= hi:
                            continue
                        m = hi - lo
                        ln(v.tensor_tensor(tmp[:, 0:m, :, n + 1:J], bcast(A[:, lo:hi, :, n], 3, J - n - 1),
                                           bcast(A[:, n, :, n + 1:J], 1, m), ALU.mult))
                        ln(v.tensor_tensor(A[:, lo:hi, :, n + 1:J], A[:, lo:hi, :, n + 1:J],
                                           tmp[:, 0:m, :, n + 1:J], ALU.subtract))

                def substitute(n):
                    for lo, hi in ((0, min(n, S // 2)), (S // 2, n)):
                        if lo >= hi:
                            continue
                        m = hi - lo
                        ln(v.tensor_tensor(tmp[:, 0:m, :, S:J], bcast(A[:, lo:hi, :, n], 3, V),
                                           bcast(A[:, n, :, S:J], 1, m), ALU.mult))
                        ln(v.tensor_tensor(A[:, lo:hi, :, S:J], A[:, lo:hi, :, S:J], tmp[:, 0:m, :, S:J],
                                           ALU.subtract))

                def guarded(flag, steps):
                    before = ln.n
                    with v.If(v.value_load(flag) != 0):
                        steps()
                    with v.Else():
                        v.sem_inc(link, ln.n - before)
                        v.wait_ge(link, ln.n)

                def run(step, tokens):
                    for n in tokens:
                        guarded(land_i[0:1, n:n + 1], lambda: step(n))

                for m in range(S // RUN):
                    guarded(any_i[0:1, m:m + 1], lambda: run(eliminate, range(m * RUN, (m + 1) * RUN)))
                for m in range(S // RUN - 1, -1, -1):
                    guarded(any_i[0:1, m:m + 1],
                            lambda: run(substitute, range((m + 1) * RUN - 1, max(m * RUN, 1) - 1, -1)))
                v.tensor_copy(rr[:].rearrange("p i (h d) -> p i h d", d=V), A[:, :, :, S:J]).then_inc(solved, 1)


def landmark_read(k, q_dram, y_dram):
    nc = k.nc
    G = 4
    V = DH + 1
    LINKS = TC * 2 + 1
    ctx = Stage(k)
    with ctx:
        sb, ps = buffers(nc, ctx)
        w_out = sb("y_w_out", [P, D])
        own_batch = sb("y_own_batch", [P, G])
        b_row = sb("y_b_row", [P, D])
        pt = sb("y_pt", [P, G, TC, G, S])
        yy = sb("y_yy", [P, TC, H16, V])
        ym = sb("y_ym", [P, TC, H16, G, V])
        rec = sb("y_rec", [S, H16, G])
        ob = sb("y_ob", [S, TC, G, H16, DH])
        ot = sb("y_ot", [P, CHUNK])
        rows = sb("y_rows", [P, TC, D])
        psO = ps("y_psO", [P, 2, 2, CHUNK])
        psT = ps("y_psT", [P, CHUNK])
        psP = ps("y_psP", [P, CHUNK])
        loaded = k.sem("y_loaded")
        y_loaded = [k.sem(f"y_y{t}_loaded") for t in range(TC)]
        pt_loaded = k.sem("y_pt_loaded")
        ym_ready = k.sem("y_ym_ready")
        context_done = k.sem("y_context_done")
        context_ready = k.sem("y_context_ready")
        context_turned = k.sem("y_context_turned")
        ot_ready = k.sem("y_ot_ready")
        out_done = k.sem("y_out_done")
        added = k.sem("y_added")
        link = k.sem("y_link")
        used = [k.sem(f"y_used{t}") for t in range(TC)]
        with nc.Block() as block:
            @block.sync
            def _(sp):
                sp.dma_start(w_out[:], k.a["L0_attn_WoT"]).then_inc(loaded, 16)
                sp.dma_start(own_batch[:], k.a["own_batch"]).then_inc(loaded, 16)
                sp.dma_start(b_row[:], k.a["L0_attn_bo"].partition_broadcast(P)).then_inc(loaded, 16)

                def load(i, t):
                    sp.dma_start(yy[:, t:t + 1].rearrange("p t h d -> p t (h d)"),
                                 y_dram.rearrange("b j c -> (b j) c").rearrange("(t p) c -> p t c", p=P)
                                 [:, ds(i * TC + t, 1)]).then_inc(y_loaded[t], 16)

                for t in range(TC):
                    load(0, t)
                def load_queries(i):
                    sp.wait_ge(context_done, i * TC)
                    sp.nop(nofuse=True)
                    sp.dma_start(pt[:].rearrange("p r t q i -> p (r t q i)"),
                                 q_dram[ds(i, 1)].rearrange("a p c -> (a p) c")).then_inc(pt_loaded, 16)

                with sp.Fori(0, CHUNKS - 1) as i:
                    load_queries(i)
                    for t in range(TC):
                        sp.wait_ge(ym_ready, i * TC + t + 1)
                        sp.nop(nofuse=True)
                        load(i + 1, t)
                load_queries(CHUNKS - 1)

            @block.gpsimd
            def _(g):
                g.wait_ge(loaded, 48)
                with g.Fori(0, CHUNKS) as i:
                    for t in range(TC):
                        g.wait_ge(y_loaded[t], (i + 1) * 16)
                        g.wait_ge(used[t], i)
                        g.nop(nofuse=True)
                        g.tensor_tensor(ym[:, t], bcast(yy[:, t], 2, G), bcast(bcast(own_batch[:], 1, H16), 3, V),
                                        ALU.mult).then_inc(ym_ready, 1)

            @block.tensor
            def _(pe):
                pe.wait_ge(loaded, 48)
                with pe.Fori(0, CHUNKS) as i:
                    pe.wait_ge(pt_loaded, (i + 1) * 16)
                    for t in range(TC):
                        pe.wait_ge(ym_ready, i * TC + t + 1)
                        if t >= 2:
                            pe.wait_ge(context_ready, i * TC + t - 1)
                        for h in range(H16):
                            mm = pe.matmul(psO[0:S, t % 2, h // 8, h % 8 * G * V:(h % 8 + 1) * G * V],
                                           pt[:, h // G, t, h % G, :], ym[:, t, h].rearrange("p b d -> p (b d)"),
                                           start=True, stop=True)
                        mm.then_inc(context_done, 1)
                        pe.wait_ge(context_done, i * TC + t + 1)
                        pe.sem_inc(used[t], 1)
                    pe.wait_ge(context_ready, (i + 1) * TC)
                    pe.nop(nofuse=True)
                    for t in range(TC):
                        for b in range(BT):
                            at = t * P + b * S
                            mm = pe.transpose(psT[:, at:at + S], ob[:, t, b].rearrange("p h d -> p (h d)"),
                                              k.ident[0:S, 0:S])
                    mm.then_inc(context_turned, 1)
                    pe.wait_ge(ot_ready, i + 1)
                    pe.wait_ge(added, i)
                    for t in range(TC):
                        mm = pe.matmul(psP[:, t * P:(t + 1) * P], ot[:, t * P:(t + 1) * P], w_out[:],
                                       start=True, stop=True)
                    mm.then_inc(out_done, 1)

            @block.scalar
            def _(act):
                with act.Fori(0, CHUNKS) as i:
                    act.wait_ge(context_turned, i + 1)
                    act.activation(ot[:], psT[:], ACT.Copy).then_inc(ot_ready, 1)

            @block.vector
            def _(v):
                v.wait_ge(loaded, 48)
                with v.Fori(0, CHUNKS) as i:
                    ln = Chain(v, link, i * LINKS, LINKS)
                    for t in range(TC):
                        v.wait_ge(context_done, i * TC + t + 1)
                        view = psO[0:S, t % 2, :, 0:8 * G * V].rearrange("p f (h b d) -> p f h b d", h=8, b=G)
                        ln(v.tensor_scalar(rec[:].rearrange("p (f h) b -> p f h b", f=2), view[:, :, :, :, DH],
                                           1e-10, None, ALU.max))
                        ln(v.reciprocal(rec[:], rec[:]))
                        v.wait_ge(context_turned, i)
                        for f in range(2):
                            x = v.tensor_tensor(ob[:, t, :, f * 8:f * 8 + 8].rearrange("p b h d -> p h b d"),
                                                view[:, f, :, :, 0:DH], bcast(rec[:, f * 8:f * 8 + 8], 3, DH),
                                                ALU.mult)
                        x.then_inc(context_ready, 1)
                        v.wait_ge(context_ready, i * TC + t + 1)
                    v.wait_ge(out_done, i + 1)
                    ln(v.tensor_tensor(rows[:], psP[:].rearrange("p (t d) -> p t d", t=TC), bcast(b_row[:], 1, TC),
                                       ALU.add))
                    ln.done()
                    at = k.X[:, ds(i * CHUNK, CHUNK)]
                    v.tensor_tensor(at, at, rows[:].rearrange("p t d -> p (t d)"), ALU.add).then_inc(added, 1)


def layer0_xattn(k):
    nc = k.nc
    normalise(k, "n0x", k.X)
    ctx = Stage(k)
    w256_dram = nc.dram_tensor("c_w256_dram", (B, H16 * D), F32).ap()
    with ctx:
        sb, ps = buffers(nc, ctx)
        att = sb("c_att", [P, TOK])
        kernel_layout = Stage(k)
        with kernel_layout:
            wsb, _ = buffers(nc, kernel_layout)
            w = {"m": wsb("c_m", [P, H16, C]),
                 "u": wsb("c_u", [P, 2, H16, D]),
                 "n": wsb("c_n", [P, H16]),
                 "nv": wsb("c_nv", [H16, D])}
            context_weights(k, w, w256_dram)
            context_attention(k, w, w256_dram, att)
        normalise(k, "n0y", att, gain="L0_xattn_ln_scale", bias="L0_xattn_ln_bias", add_to=k.X, eps=1e-6)


def context_weights(k, w, w256_dram):
    nc = k.nc
    DK = 64
    nv_dram = nc.dram_tensor("d_nv_dram", (1, H16 * D), F32).ap()
    ctx = Stage(k)
    with ctx:
        sb, ps = buffers(nc, ctx)
        wq = sb("d_wq", [DK, H16, D])
        wk = sb("d_wk", [DK, H16, C])
        wv = sb("d_wv", [DK, H16, C])
        wo = sb("d_wo", [DK, H16, D])
        null = sb("d_null", [DK, 2])
        last = sb("d_last", [P, 2, B])
        nrow = sb("d_nrow", [1, H16 * D])
        w256 = sb("d_w256", [P, H16 * D])
        psW = ps("d_psW", [P, 2, CHUNK])
        loaded = k.sem("d_loaded")
        filled = k.sem("d_filled")
        taken = k.sem("d_taken")
        stored = k.sem("d_stored")
        nv_stored = k.sem("d_nv_stored")
        nv_loaded = k.sem("d_nv_loaded")
        LOADS = 7
        U_AT, N_AT, NV_AT, W_AT, END = 8, 16, 17, 21, 25

        with nc.Block() as block:
            @block.sync
            def _(sp):
                for to, name in ((wq, "L0_xattn_wqT"), (wk, "L0_xattn_wkT"), (wv, "L0_xattn_wvT"),
                                 (wo, "L0_xattn_wo"), (null, "L0_xattn_nullT")):
                    sp.dma_start(to[:], k.a[name]).then_inc(loaded, 16)
                for half in range(2):
                    sp.dma_start(last[:, half], k.a["ctx_lastT"][half * P:(half + 1) * P, :]).then_inc(loaded, 16)
                sp.wait_ge(taken, W_AT)
                sp.dma_start(nv_dram, nrow[:]).then_inc(nv_stored, 16)
                sp.wait_ge(nv_stored, 16)
                sp.dma_start(w["nv"][:], nv_dram.rearrange("o (h d) -> (o h) d", d=D)).then_inc(nv_loaded, 16)
                sp.wait_ge(taken, END)
                sp.dma_start(w256_dram, w256[:]).then_inc(stored, 16)
                sp.wait_ge(nv_loaded, 16)
                sp.wait_ge(stored, 16)

            @block.tensor
            def _(pe):
                pe.wait_ge(loaded, LOADS * 16)
                for j in range(END):
                    bank = psW[:, j % 2]
                    if j >= 2:
                        pe.wait_ge(taken, j - 1)
                    if j < U_AT:
                        for h in (2 * j, 2 * j + 1):
                            mm = pe.matmul(bank[:, h % 2 * C:(h % 2 + 1) * C], wq[:, h], wk[:, h],
                                           start=True, stop=True)
                    elif j < N_AT:
                        half, four = (j - U_AT) // 4, (j - U_AT) % 4
                        for q in range(4):
                            mm = pe.matmul(bank[:, q * D:(q + 1) * D], wv[:, four * 4 + q, half * P:(half + 1) * P],
                                           wo[:, four * 4 + q], start=True, stop=True)
                    elif j < NV_AT:
                        for h in range(H16):
                            mm = pe.matmul(bank[:, h:h + 1], wq[:, h], null[:, 0:1], start=True, stop=True)
                    elif j < W_AT:
                        four = j - NV_AT
                        mm = pe.matmul(bank[0:1], null[:, 1:2],
                                       wo[:, four * 4:four * 4 + 4].rearrange("p h d -> p (h d)"),
                                       start=True, stop=True)
                    else:
                        four = j - W_AT
                        for half in range(2):
                            mm = pe.matmul(bank, last[:, half],
                                           w["u"][:, half, four * 4:four * 4 + 4].rearrange("p h d -> p (h d)"),
                                           start=(half == 0), stop=(half == 1))
                    mm.then_inc(filled, 1)

            @block.scalar
            def _(act):
                for j in range(END):
                    bank = psW[:, j % 2]
                    act.wait_ge(filled, j + 1)
                    if j < U_AT:
                        x = act.activation(w["m"][:, 2 * j:2 * j + 2].rearrange("p h c -> p (h c)"), bank, ACT.Copy,
                                           scale=DK ** -0.5)
                    elif j < N_AT:
                        half, four = (j - U_AT) // 4, (j - U_AT) % 4
                        x = act.activation(w["u"][:, half, four * 4:four * 4 + 4].rearrange("p h d -> p (h d)"),
                                           bank, ACT.Copy)
                    elif j < NV_AT:
                        x = act.activation(w["n"][:], bank[:, 0:H16], ACT.Copy, scale=DK ** -0.5)
                    elif j < W_AT:
                        four = j - NV_AT
                        x = act.activation(nrow[:, four * CHUNK:(four + 1) * CHUNK], bank[0:1], ACT.Copy)
                    else:
                        four = j - W_AT
                        x = act.activation(w256[:, four * CHUNK:(four + 1) * CHUNK], bank, ACT.Copy)
                    x.then_inc(taken, 1)


def context_attention(k, w, w256_dram, att):
    nc = k.nc
    G = 4
    NI = B // 8
    NB = 8
    TOKS = NB * S
    NK = KEYS + 1
    GROUPS = NB // 2
    KT = 3
    FILLS = 17
    TURNS = NB * KT // 2
    q_dram = nc.dram_tensor("c_q_dram", (H16, TOKS), F32).ap()
    t_dram = nc.dram_tensor("c_t_dram", (2, BT * H16 * S), F32).ap()
    ctx = Stage(k)
    with ctx:
        sb, ps = buffers(nc, ctx)
        qt = sb("c_qt", [P, 2, NB, H16, S])
        one = sb("c_one", [1, 1])
        qn = sb("c_qn", [H16, TOKS])
        qrow = sb("c_qrow", [1, NB, H16, S])
        kc = sb("c_kc", [P, 2, 2, 2, KEYS])
        vc = sb("c_vc", [P, 2, 2, 2, C])
        sc = sb("c_sc", [P, 2, G, NK])
        mx = sb("c_mx", [P, 2, G])
        sm = sb("c_sm", [P, 2, G])
        pt = sb("c_pt", [P, 2, 2, CHUNK])
        tail = sb("c_tail", [2, BT, H16, S])
        p256 = sb("c_p256", [H16, BT, S])
        pnull = sb("c_pnull", [H16, P])
        w256 = sb("c_w256", [H16, NB, D])
        ot = sb("c_ot", [P, 2, H16, BT, S])
        psS = ps("c_psS", [P, G, CHUNK])
        psT = ps("c_psT", [P, 2, CHUNK])
        psW = ps("c_psW", [P, 2, CHUNK])

        one_set = k.sem("c_one_set")
        kc_loaded = [k.sem(f"c_kc{n}_loaded") for n in range(2)]
        vc_loaded = [k.sem(f"c_vc{n}_loaded") for n in range(2)]
        w256_loaded = k.sem("c_w256_loaded")
        wide_full = [k.sem(f"c_wide{n}_full") for n in range(2)]
        wide_read = [k.sem(f"c_wide{n}_read") for n in range(2)]
        turn_full = [k.sem(f"c_turn{n}_full") for n in range(2)]
        turn_read = [k.sem(f"c_turn{n}_read") for n in range(2)]
        null_in = k.sem("c_null_in")
        qn_ready = k.sem("c_qn_ready")
        qn_stored = k.sem("c_qn_stored")
        qrow_loaded = k.sem("c_qrow_loaded")
        scores_done = k.sem("c_scores_done")
        max_done = k.sem("c_max_done")
        negated = k.sem("c_negated")
        exp_done = k.sem("c_exp_done")
        sum_done = k.sem("c_sum_done")
        rec_done = k.sem("c_rec_done")
        scaled = k.sem("c_scaled")
        tail_ready = k.sem("c_tail_ready")
        tail_stored = k.sem("c_tail_stored")
        tails_loaded = k.sem("c_tails_loaded")

        def wide(c, half):
            return H16 + 2 * c + half + (1 if c >= BT else 0)

        def wide_out(t):
            return H16 + (t + 1) * 2 * BT + t

        with nc.Block() as block:
            @block.sync
            def _(sp):
                def load(n, slot, back):
                    if back is not None:
                        sp.wait_ge(scores_done, back * 2)
                        sp.nop(nofuse=True)
                    for j in range(2):
                        sp.dma_start(kc[:, slot, j],
                                     k.a["ctxT"][ds(n * 2 + j, 1)].rearrange("b (f p) n -> p (b f) n", p=P))\
                            .then_inc(kc_loaded[slot], 16)
                    if back is not None:
                        sp.wait_ge(scores_done, back * 2 + 5)
                        sp.nop(nofuse=True)
                    for j in range(2):
                        sp.dma_start(vc[:, slot, j],
                                     k.a["ctx"][ds(n * 2 + j, 1), 0:2 * P].rearrange("b (t p) c -> p (b t) c", p=P))\
                            .then_inc(vc_loaded[slot], 16)

                def load_last(i):
                    sp.dma_start(w256[:], w256_dram[ds(i * NB, NB)].rearrange("b (h d) -> h b d", d=D))\
                        .then_inc(w256_loaded, 16)

                load(0, 0, None)
                load(1, 1, None)
                load_last(0)
                with sp.Fori(0, NI - 1) as i:
                    for g in range(GROUPS):
                        load(i * GROUPS + 2 + g, g % 2, (i * GROUPS + 1 + g) * 2)
                    sp.wait_ge(wide_full[1], (i + 1) * FILLS)
                    sp.nop(nofuse=True)
                    load_last(i + 1)
                for g in range(2):
                    n = (NI - 1) * GROUPS + 2 + g
                    load(n, g, (n - 1) * 2)

            @block.gpsimd
            def _(g):
                g.memset(one[:], 1.0).then_inc(one_set, 1)
                with g.Fori(0, NI) as i:
                    g.wait_ge(qn_ready, i + 1)
                    g.wait_ge(qrow_loaded, i * 16)
                    g.nop(nofuse=True)
                    g.dma_start(q_dram, qn[:]).then_inc(qn_stored, 16)
                    g.wait_ge(qn_stored, (i + 1) * 16)
                    g.wait_ge(scores_done, i * NB * 2)
                    g.nop(nofuse=True)
                    g.dma_start(qrow[:], q_dram.rearrange("h (b i) -> b h i", i=S).unsqueeze(0)).then_inc(qrow_loaded, 16)
                    for t in range(2):
                        g.wait_ge(tail_ready, i * NB + (t + 1) * BT)
                        g.wait_ge(tails_loaded, (i * 2 + t) * 32)
                        g.nop(nofuse=True)
                        g.dma_start(t_dram, tail[:].rearrange("k b h i -> k (b h i)")).then_inc(tail_stored, 16)
                        g.wait_ge(tail_stored, (i * 2 + t + 1) * 16)
                        if t == 1:
                            g.wait_ge(wide_full[0], i * FILLS + wide_out(0) // 2 + 1)
                        g.nop(nofuse=True)
                        for key, to in ((0, p256[:]), (1, pnull[:].rearrange("h (b i) -> h b i", i=S))):
                            g.dma_start(to, t_dram[key:key + 1].rearrange("k (b h i) -> h (k b) i", b=BT, h=H16))\
                                .then_inc(tails_loaded, 16)

            @block.tensor
            def _(pe):
                pe.wait_ge(one_set, 1)

                def fill(i, u):
                    pe.wait_ge(wide_read[u % 2], i * FILLS + u // 2)
                    pe.nop(nofuse=True)
                    return psW[:, u % 2]

                def output(i, t):
                    u = wide_out(t)
                    bank = fill(i, u)[:, 0:D]
                    before = wide(t * BT + BT - 1, 0)
                    for n in (before, before + 1):
                        pe.wait_ge(wide_read[n % 2], i * FILLS + n // 2 + 1)
                    pe.nop(nofuse=True)
                    for half in range(2):
                        for h in range(H16):
                            pe.matmul(bank, ot[:, half, h].rearrange("p b i -> p (b i)"), w["u"][:, half, h],
                                      start=(half == 0 and h == 0), stop=False)
                    pe.wait_ge(tails_loaded, (i * 2 + t + 1) * 32)
                    pe.wait_ge(w256_loaded, (i + 1) * 16)
                    pe.nop(nofuse=True)
                    pe.matmul(bank, pnull[:], w["nv"][:], start=False, stop=False)
                    for b in range(BT):
                        mm = pe.matmul(bank[b * S:(b + 1) * S], p256[:, b], w256[:, t * BT + b],
                                       start=False, stop=True)
                    mm.then_inc(wide_full[u % 2], 1)

                def turn(i, c, t):
                    u = c * KT + t
                    keys = P if t < 2 else 2
                    pe.wait_ge(turn_read[u % 2], i * TURNS + u // 2)
                    pe.nop(nofuse=True)
                    for r in range(G):
                        mm = pe.transpose(psT[0:keys, u % 2, r * P:(r + 1) * P],
                                          sc[:, c % 2, r, t * P:t * P + keys], k.ident[:])
                    mm.then_inc(turn_full[u % 2], 1)

                with pe.Fori(0, NI) as i:
                    x = k.XT[:, ds(i * TOKS, TOKS)]
                    pe.wait_ge(exp_done, i * NB * G)
                    pe.matmul(psS[0:H16, 0, 0:TOKS], w["n"][:], x, start=True, stop=True).then_inc(null_in, 1)
                    pe.wait_ge(scores_done, i * NB * 2)
                    for u in range(H16):
                        bank = fill(i, u)
                        half, pair = u // 8, u % 8
                        for q in range(2):
                            mm = pe.matmul(bank[:, q * TOKS:(q + 1) * TOKS],
                                           w["m"][:, pair * 2 + q, half * P:(half + 1) * P], x,
                                           start=True, stop=True)
                        mm.then_inc(wide_full[u % 2], 1)
                    pe.wait_ge(qrow_loaded, (i + 1) * 16)
                    for n in range(2):
                        pe.wait_ge(wide_read[n], i * FILLS + H16 // 2)
                    pe.wait_ge(qn_ready, i + 1)
                    for b in range(NB + 2):
                        if b < NB:
                            g, j = b // 2, b % 2
                            pe.wait_ge(kc_loaded[g % 2], (i * 2 + g // 2 + 1) * 32)
                            for two in range(2):
                                pe.wait_ge(exp_done, (i * NB + b) * G - (G - two * 2 - 2 if b else 0))
                                pe.nop(nofuse=True)
                                for r in range(two * 2, two * 2 + 2):
                                    for half in range(2):
                                        pe.matmul(psS[:, r, 0:KEYS],
                                                  qt[:, half, b, r * G:(r + 1) * G].rearrange("p h i -> p (h i)"),
                                                  kc[:, g % 2, j, half], start=(half == 0), stop=(half == 1))
                                    mm = pe.matmul(psS[:, r, KEYS:NK],
                                                   qrow[:, b, r * G:(r + 1) * G].rearrange("p h i -> p (h i)"),
                                                   one[:], start=True, stop=True)
                                mm.then_inc(scores_done, 1)
                        if 1 <= b <= NB:
                            pe.wait_ge(scaled, i * NB + b)
                            turn(i, b - 1, 0)
                            turn(i, b - 1, 1)
                        if b >= 2:
                            c = b - 2
                            if c == BT:
                                output(i, 0)
                            g, j = c // 2, c % 2
                            pe.wait_ge(vc_loaded[g % 2], (i * 2 + g // 2 + 1) * 32)
                            for t in range(2):
                                u = c * KT + t
                                pe.wait_ge(turn_read[u % 2], i * TURNS + u // 2 + 1)
                            for half in range(2):
                                u = wide(c, half)
                                bank = fill(i, u)
                                for t in range(2):
                                    mm = pe.matmul(bank, vc[:, g % 2, j, t, half * P:(half + 1) * P], pt[:, c % 2, t],
                                                   start=(t == 0), stop=(t == 1))
                                mm.then_inc(wide_full[u % 2], 1)
                        if 1 <= b <= NB:
                            turn(i, b - 1, 2)
                    output(i, 1)

            @block.scalar
            def _(act):
                with act.Fori(0, NI) as i:
                    act.wait_ge(null_in, i + 1)
                    act.wait_ge(qn_stored, i * 16)
                    act.activation(qn[:], psS[0:H16, 0, 0:TOKS], ACT.Copy).then_inc(qn_ready, 1)
                    for u in range(1, H16, 2):
                        half, pair = u // 8, u % 8
                        act.wait_ge(wide_full[1], i * FILLS + u // 2 + 1)
                        act.activation(qt[:, half, :, pair * 2:pair * 2 + 2].rearrange("p b h i -> p h b i"),
                                       psW[:, 1].rearrange("p (h b i) -> p h b i", h=2, i=S),
                                       ACT.Copy).then_inc(wide_read[1], 1)

                    def read_output(t):
                        u = wide_out(t)
                        act.wait_ge(wide_full[u % 2], i * FILLS + u // 2 + 1)
                        act.activation(att[:, ds((i * 2 + t) * D, D)], psW[:, u % 2, 0:D],
                                       ACT.Copy).then_inc(wide_read[u % 2], 1)

                    for b in range(NB + 2):
                        if 1 <= b <= NB:
                            c = b - 1
                            u = c * KT
                            act.wait_ge(turn_full[u % 2], i * TURNS + u // 2 + 1)
                            act.activation(pt[:, c % 2, 0], psT[:, u % 2], ACT.Copy).then_inc(turn_read[u % 2], 1)
                        if b < NB:
                            for r in range(G):
                                act.wait_ge(negated, (i * NB + b) * 2 + r // 2 + 1)
                                if r == 0:
                                    for n in range(2):
                                        last = (b - 1) * KT - 1 if b >= 1 else -1
                                        last -= (last - n) % 2
                                        act.wait_ge(turn_full[n], i * TURNS + (last // 2 + 1 if last >= 0 else 0))
                                act.activation(sc[:, b % 2, r], psS[:, r, 0:NK], ACT.Exp,
                                               bias=mx[:, b % 2, r:r + 1]).then_inc(exp_done, 1)
                        if b >= 2:
                            c = b - 2
                            if c == BT:
                                read_output(0)
                            for half in range(2):
                                u = wide(c, half)
                                act.wait_ge(wide_full[u % 2], i * FILLS + u // 2 + 1)
                                act.activation(ot[:, half, :, c % BT],
                                               psW[:, u % 2].rearrange("p (h i) -> p h i", i=S),
                                               ACT.Copy).then_inc(wide_read[u % 2], 1)
                        if 1 <= b <= NB:
                            c = b - 1
                            u = c * KT + 2
                            act.wait_ge(turn_full[u % 2], i * TURNS + u // 2 + 1)
                            if c % BT == 0:
                                act.wait_ge(tail_stored, (i * 2 + c // BT) * 16)
                            act.activation(tail[:, c % BT].rearrange("k h i -> k (h i)"), psT[0:2, u % 2],
                                           ACT.Copy).then_inc(tail_ready, 1)
                            act.wait_ge(tail_ready, i * NB + c + 1)
                            act.sem_inc(turn_read[u % 2], 1)
                    read_output(1)

            @block.vector
            def _(v):
                with v.Fori(0, NI) as i:
                    for u in range(0, H16, 2):
                        half, pair = u // 8, u % 8
                        v.wait_ge(wide_full[0], i * FILLS + u // 2 + 1)
                        v.tensor_copy(qt[:, half, :, pair * 2:pair * 2 + 2].rearrange("p b h i -> p h b i"),
                                      psW[:, 0].rearrange("p (h b i) -> p h b i", h=2, i=S))\
                            .then_inc(wide_read[0], 1)
                    for b in range(NB + 1):
                        if b < NB:
                            for two in range(2):
                                n = (i * NB + b) * 2 + two + 1
                                v.wait_ge(scores_done, n)
                                m = mx[:, b % 2, two * 2:two * 2 + 2]
                                v.tensor_reduce(m, psS[:, two * 2:two * 2 + 2, 0:NK], AX, ALU.max)\
                                    .then_inc(max_done, 1)
                                v.wait_ge(max_done, n)
                                v.tensor_scalar(m, m, -1.0, None, ALU.mult).then_inc(negated, 1)
                        if b >= 1:
                            c = b - 1
                            u = c * KT + 1
                            v.wait_ge(turn_full[u % 2], i * TURNS + u // 2 + 1)
                            v.tensor_copy(pt[:, c % 2, 1], psT[:, u % 2]).then_inc(turn_read[u % 2], 1)
                        if b < NB:
                            n = i * NB + b + 1
                            v.wait_ge(exp_done, n * G)
                            v.tensor_reduce(sm[:, b % 2], sc[:, b % 2], AX, ALU.add).then_inc(sum_done, 1)
                            v.wait_ge(sum_done, n)
                            v.reciprocal(sm[:, b % 2], sm[:, b % 2]).then_inc(rec_done, 1)
                            v.wait_ge(rec_done, n)
                            v.tensor_tensor(sc[:, b % 2], sc[:, b % 2], bcast(sm[:, b % 2], 2, NK), ALU.mult)\
                                .then_inc(scaled, 1)



def program(nc, args, out, phases=None):
    ctx = ExitStack()
    with ctx:
        k = Core(nc, ctx, args)

        def sb(name, shape, dt=F32):
            return ctx.enter_context(nc.sbuf_tensor(name, list(shape), dt))

        k.X = sb("X", [P, TOK])
        k.XT = sb("XT", [P, TOK])
        k.ident = sb("ident", [P, P])
        x_in = ctx.enter_context(nc.semaphore("x_in"))
        x_out = ctx.enter_context(nc.semaphore("x_out"))
        with nc.Block() as block:
            @block.sync
            def _(sp):
                sp.dma_start(k.X[:].rearrange("p (t d) -> p t d", t=TILES),
                             args["x"].rearrange("(t p) d -> p t d", p=P)).then_inc(x_in, 16)
                sp.dma_start(k.ident[:], args["ident"]).then_inc(x_in, 16)
                sp.wait_ge(x_in, 32)

        for phase in PHASES:
            if phases is None or phase.__name__ in phases:
                if phase not in (layer0_xattn, layer0_attn) and not hasattr(k, "H"):
                    k.H = sb("H", [P, TOK])
                    k.DR = sb("DR", [P, TOK])
                phase(k)

        with nc.Block() as block:
            @block.sync
            def _(sp):
                sp.dma_start(out.rearrange("(t p) d -> p t d", p=P),
                             k.X[:].rearrange("p (t d) -> p t d", t=TILES)).then_inc(x_out, 16)
                sp.wait_ge(x_out, 16)


def layer0_ffn(k):
    normalise(k, "n0f", k.X)
    mixture(k, "f0", 8, 4, k.X, "gelu2", "L0_ffn_wr", None, "L0_ffn_wu", "L0_ffn_bu", "L0_ffn_wd", "L0_ffn_b_down")


def layer1_ffn(k):
    normalise(k, "n1f", k.X, gain="L1_ffn_scale", twice=True, residual=True)
    mixture(k, "f1", 16, 1, k.X, "swiglu4", "L1_ffn_wr", "L1_ffn_gate_b", "L1_ffn_wu", "L1_ffn_bu", "L1_ffn_wd",
            "L1_ffn_mlp2_b")


PHASES = [
    layer0_xattn, layer0_attn, layer0_ffn,
    layer1_xattn, layer1_attn, layer1_ffn,
    layer2_xattn, layer2_attn, layer2_ffn,
    layer3_xattn, layer3_attn, layer3_ffn]



def layout(inp):
    c = np.ascontiguousarray
    a = {"x": c(inp["x"]).reshape(TOK, D)}
    for name, v in inp.items():
        if name not in ("x", "ctx_2048") and v.ndim and v.size <= 1 << 17:
            a[name] = c(v)
    a["ident"] = np.eye(P, dtype=np.float32)
    for e in (8, 16):
        a[f"tri{e}"] = np.tril(np.ones((e, e), np.float32), -1)
        a[f"index{e}"] = np.arange(e, dtype=np.float32)
    a["L0_ffn_wr"] = c(inp["L0_ffn_w_router"].T)
    a["L0_ffn_wu"] = c(inp["L0_ffn_w_up"].reshape(8 * 4, P, D).transpose(2, 0, 1))
    a["L0_ffn_bu"] = c(inp["L0_ffn_b_up"].reshape(8 * 4, P).T)
    a["L0_ffn_wd"] = c(inp["L0_ffn_w_down"].reshape(8, D, 4, P).transpose(3, 0, 2, 1).reshape(P, 32, D))
    a["L1_ffn_wr"] = c(inp["L1_ffn_gate_w"].T)
    a["L1_ffn_wu"] = c(inp["L1_ffn_mlp1_w"][:, 0::2, :].transpose(2, 0, 1))
    a["L1_ffn_bu"] = c(inp["L1_ffn_mlp1_b"][:, 0::2].T)
    a["L1_ffn_wd"] = c(inp["L1_ffn_mlp2_w"].transpose(2, 0, 1))
    a["pos"] = np.arange(S, dtype=np.float32)
    a["part"] = np.arange(P, dtype=np.float32)[:, None]
    a["slot"] = (np.arange(P) % BT * S).astype(np.float32)[:, None]
    d = np.arange(S)[:, None] - np.arange(S)[None, :]
    a["decay"] = np.kron(np.eye(BT), np.where(d >= 0, PATCH_DECAY ** np.maximum(d, 0.0), 0.0)).astype(np.float32)
    a["ctx"] = c(inp["ctx_2048"])
    for layer in (1, 3):
        a[f"L{layer}_xattn_wT"] = c(inp[f"L{layer}_xattn_W_in"].T)
    a["L1_attn_w_in"] = c(inp["L1_attn_in_proj_w"].T.reshape(D, 4, P))
    a["L1_attn_w_conv"] = c(inp["L1_attn_conv_weight"].reshape(2, P, 4).transpose(1, 0, 2))
    a["L1_attn_b_conv"] = c(inp["L1_attn_conv_bias"].reshape(2, P).T)
    a["L1_attn_d_skip"] = c(inp["L1_attn_D"].reshape(2, P).T)
    mean = np.full((16, 2 * P), 1.0 / (2 * P), np.float32)
    dbc = np.stack([inp["L1_attn_delta_w"], inp["L1_attn_B_w"], inp["L1_attn_C_w"], mean])
    a["L1_attn_w_dbc"] = c(dbc.reshape(4, 16, 2, P).transpose(3, 2, 0, 1))
    a["L1_attn_w_out"] = c(inp["L1_attn_out_proj_w"].T.reshape(2, P, D).transpose(1, 0, 2))
    w = np.stack([inp["L2_attn_Wr"], inp["L2_attn_Wk"], inp["L2_attn_Wv"]])
    a["L2_attn_w_rkv"] = c(w.transpose(2, 0, 1))
    a["L2_attn_w_out"] = c(inp["L2_attn_Wo"].T)
    a["L2_attn_wfk"] = c(inp["L2_attn_Wfk"].T.reshape(D, 4, P))
    a["L2_attn_wfv"] = c(inp["L2_attn_Wfv"].T.reshape(4, P, D).transpose(1, 0, 2))
    a["L2_attn_wfr"] = c(inp["L2_attn_Wfr"].T)
    a["L2_ffn_w_qkv"] = c(inp["L2_ffn_in_proj_w"].T.reshape(D, 3, D))
    a["L2_ffn_out_wT"] = c(inp["L2_ffn_out_w"].T)
    a["L2_ffn_wr"] = c(inp["L2_ffn_router_w"].T)
    a["L2_ffn_wu"] = c(inp["L2_ffn_w1"].transpose(2, 0, 1))
    a["L2_ffn_bu"] = c(inp["L2_ffn_b1"].T)
    a["L2_ffn_wd"] = c(inp["L2_ffn_w2"].transpose(2, 0, 1))
    a["ctxT"] = c(inp["ctx_2048"].transpose(0, 2, 1))
    a["ctx_last"] = c(inp["ctx_2048"][:, KEYS - 1, :])
    a["ctx_lastT"] = c(inp["ctx_2048"][:, KEYS - 1, :].T)
    a["L0_xattn_wqT"] = c(inp["L0_xattn_Wq"].reshape(D, H16, 64).transpose(2, 1, 0))
    wkv = inp["L0_xattn_Wkv"].reshape(C, 2, H16, 64).transpose(1, 3, 2, 0)
    a["L0_xattn_wkT"], a["L0_xattn_wvT"] = c(wkv[0]), c(wkv[1])
    a["L0_xattn_wo"] = c(inp["L0_xattn_Wout"].reshape(H16, 64, D).transpose(1, 0, 2))
    a["L0_xattn_nullT"] = c(inp["L0_xattn_null_kv"].T)
    w = inp["L2_xattn_w_qkv"].T
    a["L2_xattn_w_qk"] = c(w[:, 0:2 * D].reshape(D, 2, D))
    a["L2_xattn_w_v"] = c(w[:, 2 * D:])
    a["L2_xattn_w_projT"] = c(inp["L2_xattn_w_proj"].T)
    a["own_feature"] = (np.arange(P)[:, None] // DH == np.arange(H16)).astype(np.float32)

    def doubled(w, bias):
        order = np.concatenate([np.tile(np.arange(r * S, r * S + S), 2) for r in range(4)])
        return w.T[:, order].reshape(D, 2, P), bias[order].reshape(2, P).T

    wk, bk = doubled(inp["L0_attn_Wk"], inp["L0_attn_bk"])
    wq, bq = doubled(inp["L0_attn_Wq"], inp["L0_attn_bq"])
    a["L0_attn_w_kq"] = c(np.concatenate([wk, wq], 1))
    a["L0_attn_b_kq"] = c(np.concatenate([bk, bq], 1))
    a["L0_attn_w_tok"] = c(np.concatenate([inp["L0_attn_Wq"].T, inp["L0_attn_Wk"].T, inp["L0_attn_Wv"].T], 1))
    a["L0_attn_b_tok"] = c(np.concatenate([inp["L0_attn_bq"], inp["L0_attn_bk"], inp["L0_attn_bv"]]))
    a["L0_attn_WoT"] = c(inp["L0_attn_Wo"].T)
    a["L0_attn_temperature"] = c(inp["L0_attn_temperature"]).reshape(1)
    qkv = inp["L3_attn_W_qkv"].T
    a["L3_attn_w_qk"] = c(qkv[:, 0:2 * D].reshape(D, 2, D))
    a["L3_attn_w_v"] = c(qkv[:, 2 * D:])
    a["L3_attn_w_outT"] = c(inp["L3_attn_W_out"].T)
    dist = np.clip(np.arange(S)[None, :] - np.arange(S)[:, None], -128, 128) + 128
    rel = inp["L3_attn_rel_emb"][dist].transpose(0, 2, 1).reshape(S, 4, 4 * S)
    a["L3_attn_bias"] = c(np.tile(rel, (BT, 1, 1)))
    part = np.arange(P)
    a["own_head"] = (part[:, None] // DH % 4 == np.arange(4)).astype(np.float32)
    a["own_batch"] = (part[:, None] // S == np.arange(4)).astype(np.float32)
    a["L3_ffn_wu"] = c(inp["L3_ffn_W1"].T.reshape(D, 4, P))
    a["L3_ffn_bu"] = c(inp["L3_ffn_b1"].reshape(4, P).T)
    a["L3_ffn_wd"] = c(inp["L3_ffn_W2"].T.reshape(4, P, D).transpose(1, 0, 2))
    return a


def build(nc, arrays, phases=None):
    args = {n: nc.dram_tensor(f"in_{n}", a.shape, mybir.dt.from_np(a.dtype), kind="ExternalInput").ap()
            for n, a in arrays.items()}
    out = nc.dram_tensor("out_x", (TOK, D), F32, kind="ExternalOutput").ap()
    program(nc, args, out, phases)


def kernel(**inputs):
    from concourse import bacc
    from concourse.bass_utils import run_bass_kernel_spmd

    arrays = layout({n: np.asarray(v) for n, v in inputs.items()})
    nc = bacc.Bacc("TRN2", target_bir_lowering=False, num_devices=1)
    build(nc, arrays)
    r = run_bass_kernel_spmd(nc, [{f"in_{n}": a for n, a in arrays.items()}], core_ids=[0])
    return r.results[0]["out_x"].reshape(B, S, D)
```
